# Optimizing a Trainium2 kernel written in Bass

```python
import numpy as np
import jax
import jax.numpy as jnp

def _softmax(x, axis=-1):
    return jax.nn.softmax(x, axis=axis)

def _gelu(x):
    return jax.nn.gelu(x, approximate=True)

def _silu(x):
    return jax.nn.silu(x)

def _sigmoid(x):
    return jax.nn.sigmoid(x)

def _layernorm(x, axis=-1, eps=1e-05):
    m = jnp.mean(x, axis=axis, keepdims=True)
    v = jnp.var(x, axis=axis, keepdims=True)
    return (x - m) / jnp.sqrt(v + eps)

def _scatter_add(tgt, idx, src, axis=0):
    return tgt.at[idx].add(src)

def _segment_sum(src, seg, n):
    return jax.ops.segment_sum(src, seg, n)
kernel_name = 'mk_seq_preln_d1_jaxref_r4_c62d4e'

def setup_inputs(seed: int=0):
    np.random.seed(seed)
    _w = jnp.asarray

    def _L0_attn_setup():
        import jax, jax.numpy as jnp
        import numpy as np
        D_MODEL = 512
        D_STATE = 64
        D_CONV = 4
        EXPAND = 2
        HEADDIM = 64
        NGROUPS = 1
        CHUNK = 64
        D_INNER = EXPAND * D_MODEL
        NHEADS = D_INNER // HEADDIM
        CONV_DIM = D_INNER + 2 * NGROUPS * D_STATE
        D_IN_PROJ = 2 * D_INNER + 2 * NGROUPS * D_STATE + NHEADS
        EPS = 1e-05

        def _chunked_ssd(x, dt, A, Bm, Cm):
            b, l, h, p = x.shape
            c = l // CHUNK
            xc = x.reshape(b, c, CHUNK, h, p)
            dtc = dt.reshape(b, c, CHUNK, h)
            Bc = Bm.reshape(b, c, CHUNK, D_STATE)
            Cc = Cm.reshape(b, c, CHUNK, D_STATE)
            Abar = (dtc * A).transpose(0, 3, 1, 2)
            Acum = jnp.cumsum(Abar, axis=-1)
            seg = Acum[..., :, None] - Acum[..., None, :]
            tri = jnp.tril(jnp.ones((CHUNK, CHUNK), bool))
            Lmat = jnp.where(tri, jnp.exp(seg), 0.0)
            xdt = xc * dtc[..., None]
            Y_diag = jnp.einsum('bcln,bcsn,bhcls,bcshp->bclhp', Cc, Bc, Lmat, xdt)
            decay_states = jnp.exp(Acum[..., -1:] - Acum)
            states = jnp.einsum('bcsn,bhcs,bcshp->bchpn', Bc, decay_states, xdt)
            Achunk = Acum[..., -1]
            Acs = jnp.cumsum(jnp.pad(Achunk, ((0, 0), (0, 0), (1, 0))), axis=-1)
            segc = Acs[..., :, None] - Acs[..., None, :]
            tric = jnp.tril(jnp.ones((c + 1, c + 1), bool))
            decay_chunk = jnp.where(tric, jnp.exp(segc), 0.0)
            states0 = jnp.pad(states, ((0, 0), (1, 0), (0, 0), (0, 0), (0, 0)))
            new_states = jnp.einsum('bhzc,bchpn->bzhpn', decay_chunk, states0)
            prev_states = new_states[:, :-1]
            state_decay = jnp.exp(Acum)
            Y_off = jnp.einsum('bcln,bchpn,bhcl->bclhp', Cc, prev_states, state_decay)
            return (Y_diag + Y_off).reshape(b, l, h, p)
        key = jax.random.key(seed)
        ks = jax.random.split(key, 7)
        B, L = (2, 512)
        u = jax.random.normal(ks[0], (B, L, D_MODEL), jnp.float32)
        W_in = jax.random.normal(ks[1], (D_IN_PROJ, D_MODEL), jnp.float32) * D_MODEL ** (-0.5)
        conv_w = jax.random.normal(ks[2], (CONV_DIM, D_CONV), jnp.float32) * D_CONV ** (-0.5)
        conv_b = jnp.zeros((CONV_DIM,), jnp.float32)
        dt = jnp.exp(jax.random.uniform(ks[3], (NHEADS,), jnp.float32) * (np.log(0.1) - np.log(0.001)) + np.log(0.001))
        dt_bias = dt + jnp.log(-jnp.expm1(-dt))
        A_log = jnp.log(jax.random.uniform(ks[4], (NHEADS,), jnp.float32, minval=1.0, maxval=16.0))
        D = jnp.ones((NHEADS,), jnp.float32)
        norm_w = jnp.ones((D_INNER,), jnp.float32)
        W_out = jax.random.normal(ks[5], (D_MODEL, D_INNER), jnp.float32) * D_INNER ** (-0.5)
        return dict(u=u, W_in=W_in, conv_w=conv_w, conv_b=conv_b, dt_bias=dt_bias, A_log=A_log, D=D, norm_w=norm_w, W_out=W_out)
    _L0_attn_in = _L0_attn_setup()

    def _L0_ffn_setup():
        import jax, jax.numpy as jnp
        import numpy as np
        _FP4_LUT = jnp.array([0.0, 0.5, 1.0, 1.5, 2.0, 3.0, 4.0, 6.0, -0.0, -0.5, -1.0, -1.5, -2.0, -3.0, -4.0, -6.0], dtype=jnp.float32)
        GROUP_SIZE = 128
        EPS = 1e-06

        def _dequant_fp4(packed_i32, scales_f16, group_size):
            out_f, in_p = packed_i32.shape
            w = packed_i32.astype(jnp.uint32)
            shifts = jnp.arange(8, dtype=jnp.uint32) * 4
            nib = w[:, :, None] >> shifts & jnp.uint32(15)
            vals = _FP4_LUT[nib.astype(jnp.int32)].reshape(out_f, in_p * 8)
            s = scales_f16.astype(jnp.float32).T
            s_full = jnp.repeat(s, group_size, axis=1)
            return vals * s_full
        key = jax.random.key(seed)
        k1, k2, k3, k4, k5 = jax.random.split(key, 5)
        B, S, H, I = (4, 512, 512, 1408)
        x = jax.random.normal(k1, (B, S, H), dtype=jnp.float32)
        gate_up_packed = jax.random.randint(k2, (2 * I, H // 8), 0, 2147483647, dtype=jnp.int32)
        gate_up_scales = jax.random.uniform(k3, (H // GROUP_SIZE, 2 * I), dtype=jnp.float32).astype(jnp.float16)
        down_packed = jax.random.randint(k4, (H, I // 8), 0, 2147483647, dtype=jnp.int32)
        down_scales = jax.random.uniform(k5, (I // GROUP_SIZE, H), dtype=jnp.float32).astype(jnp.float16)
        return {'x': x, 'gate_up_packed': gate_up_packed, 'gate_up_scales': gate_up_scales, 'down_packed': down_packed, 'down_scales': down_scales}
    _L0_ffn_in = _L0_ffn_setup()
    _d = {'L0_attn_u': _L0_attn_in['u'], 'L0_attn_W_in': _L0_attn_in['W_in'], 'L0_attn_conv_w': _L0_attn_in['conv_w'], 'L0_attn_conv_b': _L0_attn_in['conv_b'], 'L0_attn_dt_bias': _L0_attn_in['dt_bias'], 'L0_attn_A_log': _L0_attn_in['A_log'], 'L0_attn_D': _L0_attn_in['D'], 'L0_attn_norm_w': _L0_attn_in['norm_w'], 'L0_attn_W_out': _L0_attn_in['W_out'], 'L0_ffn_gate_up_packed': _L0_ffn_in['gate_up_packed'], 'L0_ffn_gate_up_scales': _L0_ffn_in['gate_up_scales'], 'L0_ffn_down_packed': _L0_ffn_in['down_packed'], 'L0_ffn_down_scales': _L0_ffn_in['down_scales']}
    _x0 = _d['L0_attn_u']
    _d['L0_attn_u'] = jax.random.normal(jax.random.fold_in(jax.random.key(seed), 1), (1, 2048, 512), dtype=_x0.dtype)
    del _x0
    return _d

def reference(L0_attn_u, L0_attn_W_in, L0_attn_conv_w, L0_attn_conv_b, L0_attn_dt_bias, L0_attn_A_log, L0_attn_D, L0_attn_norm_w, L0_attn_W_out, L0_ffn_gate_up_packed, L0_ffn_gate_up_scales, L0_ffn_down_packed, L0_ffn_down_scales):

    def _L0_attn_ref(u, W_in, conv_w, conv_b, dt_bias, A_log, D, norm_w, W_out):
        import jax, jax.numpy as jnp
        import numpy as np
        D_MODEL = 512
        D_STATE = 64
        D_CONV = 4
        EXPAND = 2
        HEADDIM = 64
        NGROUPS = 1
        CHUNK = 64
        D_INNER = EXPAND * D_MODEL
        NHEADS = D_INNER // HEADDIM
        CONV_DIM = D_INNER + 2 * NGROUPS * D_STATE
        D_IN_PROJ = 2 * D_INNER + 2 * NGROUPS * D_STATE + NHEADS
        EPS = 1e-05

        def _chunked_ssd(x, dt, A, Bm, Cm):
            b, l, h, p = x.shape
            c = l // CHUNK
            xc = x.reshape(b, c, CHUNK, h, p)
            dtc = dt.reshape(b, c, CHUNK, h)
            Bc = Bm.reshape(b, c, CHUNK, D_STATE)
            Cc = Cm.reshape(b, c, CHUNK, D_STATE)
            Abar = (dtc * A).transpose(0, 3, 1, 2)
            Acum = jnp.cumsum(Abar, axis=-1)
            seg = Acum[..., :, None] - Acum[..., None, :]
            tri = jnp.tril(jnp.ones((CHUNK, CHUNK), bool))
            Lmat = jnp.where(tri, jnp.exp(seg), 0.0)
            xdt = xc * dtc[..., None]
            Y_diag = jnp.einsum('bcln,bcsn,bhcls,bcshp->bclhp', Cc, Bc, Lmat, xdt)
            decay_states = jnp.exp(Acum[..., -1:] - Acum)
            states = jnp.einsum('bcsn,bhcs,bcshp->bchpn', Bc, decay_states, xdt)
            Achunk = Acum[..., -1]
            Acs = jnp.cumsum(jnp.pad(Achunk, ((0, 0), (0, 0), (1, 0))), axis=-1)
            segc = Acs[..., :, None] - Acs[..., None, :]
            tric = jnp.tril(jnp.ones((c + 1, c + 1), bool))
            decay_chunk = jnp.where(tric, jnp.exp(segc), 0.0)
            states0 = jnp.pad(states, ((0, 0), (1, 0), (0, 0), (0, 0), (0, 0)))
            new_states = jnp.einsum('bhzc,bchpn->bzhpn', decay_chunk, states0)
            prev_states = new_states[:, :-1]
            state_decay = jnp.exp(Acum)
            Y_off = jnp.einsum('bcln,bchpn,bhcl->bclhp', Cc, prev_states, state_decay)
            return (Y_diag + Y_off).reshape(b, l, h, p)
        b, l, _ = u.shape
        zxbcdt = u @ W_in.T
        z = zxbcdt[..., :D_INNER]
        xBC = zxbcdt[..., D_INNER:D_INNER + CONV_DIM]
        dt = jax.nn.softplus(zxbcdt[..., D_INNER + CONV_DIM:] + dt_bias)
        xp = jnp.pad(xBC, ((0, 0), (D_CONV - 1, 0), (0, 0)))
        xBC = conv_b + sum((xp[:, w:w + l, :] * conv_w[:, w] for w in range(D_CONV)))
        xBC = jax.nn.silu(xBC)
        x = xBC[..., :D_INNER].reshape(b, l, NHEADS, HEADDIM)
        Bm = xBC[..., D_INNER:D_INNER + D_STATE]
        Cm = xBC[..., D_INNER + D_STATE:]
        A = -jnp.exp(A_log)
        y = _chunked_ssd(x, dt, A, Bm, Cm)
        y = y + x * D[None, None, :, None]
        y = y.reshape(b, l, D_INNER)
        y = y * jax.nn.silu(z)
        y = y * jax.lax.rsqrt(jnp.mean(y * y, axis=-1, keepdims=True) + EPS) * norm_w
        return y @ W_out.T

    def _L0_ffn_ref(x, gate_up_packed, gate_up_scales, down_packed, down_scales):
        import jax, jax.numpy as jnp
        import numpy as np
        _FP4_LUT = jnp.array([0.0, 0.5, 1.0, 1.5, 2.0, 3.0, 4.0, 6.0, -0.0, -0.5, -1.0, -1.5, -2.0, -3.0, -4.0, -6.0], dtype=jnp.float32)
        GROUP_SIZE = 128
        EPS = 1e-06

        def _dequant_fp4(packed_i32, scales_f16, group_size):
            out_f, in_p = packed_i32.shape
            w = packed_i32.astype(jnp.uint32)
            shifts = jnp.arange(8, dtype=jnp.uint32) * 4
            nib = w[:, :, None] >> shifts & jnp.uint32(15)
            vals = _FP4_LUT[nib.astype(jnp.int32)].reshape(out_f, in_p * 8)
            s = scales_f16.astype(jnp.float32).T
            s_full = jnp.repeat(s, group_size, axis=1)
            return vals * s_full
        I = gate_up_packed.shape[0] // 2
        w_gu = _dequant_fp4(gate_up_packed, gate_up_scales, GROUP_SIZE)
        w_down = _dequant_fp4(down_packed, down_scales, GROUP_SIZE)
        gate_up = jnp.einsum('bsh,oh->bso', x, w_gu)
        gate, up = (gate_up[..., :I], gate_up[..., I:])
        h = jax.nn.silu(gate) * up
        y = jnp.einsum('bsi,hi->bsh', h, w_down)
        rms = jnp.sqrt(jnp.mean(y * y, axis=-1, keepdims=True) + EPS)
        return y / rms
    x = L0_attn_u
    x = x + _L0_attn_ref(_layernorm(x, axis=-1), L0_attn_W_in, L0_attn_conv_w, L0_attn_conv_b, L0_attn_dt_bias, L0_attn_A_log, L0_attn_D, L0_attn_norm_w, L0_attn_W_out)
    x = x + _L0_ffn_ref(_layernorm(x, axis=-1), L0_ffn_gate_up_packed, L0_ffn_gate_up_scales, L0_ffn_down_packed, L0_ffn_down_scales)
    return x

_drawn_inputs = setup_inputs


def setup_inputs(seed=0):
    import zlib

    import numpy as np

    out = dict(_drawn_inputs(seed))
    spreads = {'L0_attn_conv_b': (0.0, 0.1), 'L0_attn_D': (1.0, 0.2), 'L0_attn_norm_w': (1.0, 0.2)}
    factors = {}
    for name, (base, spread) in spreads.items():
        noise = np.random.default_rng([zlib.crc32(name.encode()), seed]).standard_normal(out[name].shape)
        drawn = base * np.exp(spread * noise) if base else spread * noise
        out[name] = jnp.asarray(drawn.astype(out[name].dtype))
    for name, factor in factors.items():
        out[name] = (out[name] * factor).astype(out[name].dtype)
    return out
```

```python
import concourse.bass as bass
from concourse import mybir
from contextlib import ExitStack

FP32 = mybir.dt.float32
FP16 = mybir.dt.float16
FP8 = mybir.dt.float8e4
I32 = mybir.dt.int32
U32 = mybir.dt.uint32
ALU = mybir.AluOpType
ACT = mybir.ActivationFunctionType

P = 128
L = 2048
D_MODEL = 512
D_INNER = 1024
D_STATE = 64
HEADDIM = 64
HEADS = D_INNER // HEADDIM
CHUNK = 64
I_FFN = 1408
KD = D_MODEL // P
JT = D_INNER // P
GT = I_FFN // P
LN_EPS = 1e-5
MIX_EPS = 1e-5
FFN_EPS = 1e-6

T = 256
NB = L // T
NT = T // P
NC = T // CHUNK
PROJ = D_INNER * 2 + P + D_STATE + P
DT_TILE = (2 * D_INNER + P + D_STATE, P)
BC_TILE = (2 * D_INNER, P)
C_TILE = (2 * D_INNER + P, D_STATE)
CONV_TILES = [BC_TILE, C_TILE] + [(D_INNER + j * P, P) for j in range(JT)]
Z_TILES = [(j * P, P) for j in range(JT)]
PROJ_TILES = [DT_TILE] + CONV_TILES + Z_TILES
NPROJ = len(PROJ_TILES)
NCONV = len(CONV_TILES)

TF = 256
NBF = L // TF
NTF = TF // P


def mixer(nc, ctx, d):
    def sb(name, shape, dt=FP32):
        return ctx.enter_context(nc.sbuf_tensor(name, shape, dt))

    def sem(name):
        return ctx.enter_context(nc.semaphore(name))

    w_in = sb("w_in", [P, KD, PROJ])
    w_out = sb("w_out", [P, JT, D_MODEL])
    norm_w = sb("norm_w", [P, JT])
    conv_w = sb("conv_w", [P, NCONV, 4])
    conv_b = sb("conv_b", [P, NCONV])
    dt_bias = sb("dt_bias", [P, 1])
    a_neg = sb("a_neg", [P, 1])
    d_skip = sb("d_skip", [P, JT])
    ident = sb("ident", [P, P])
    delta = sb("delta", [32, HEADS, CHUNK])
    keep = sb("keep", [P, T])
    ones = sb("ones", [P, 1])
    eps = sb("eps", [P, 3])

    xin = sb("xin", [P, NT, D_MODEL])
    stats = sb("stats", [P, NT, 6])
    mv = sb("mv", [P, NT, 2])
    std = sb("std", [P, NT])
    rstd = sb("rstd", [P, NT])
    xn = sb("xn", [P, NT, D_MODEL])
    xnT = sb("xnT", [P, KD, T])
    raw = sb("raw", [P, NCONV, 3 + T])
    acc = sb("acc", [P, 2, T])
    gate = sb("gate", [P, JT, T])
    xT = sb("xT", [P, JT, T])
    gc = sb("gc", [P, T])
    cT = sb("cT", [D_STATE, T])
    dts = sb("dts", [P, 6, T])
    acum = sb("acum", [P, T])
    dtT = sb("dtT", [P, NT, HEADS])
    seg_l = sb("seg_l", [P, NC, P])
    seg_r = sb("seg_r", [P, 2, HEADS, CHUNK])
    bI = sb("bI", [P, NC, D_STATE])
    decay = sb("decay", [P, HEADS, CHUNK])
    mc = sb("mc", [P, HEADS, CHUNK])
    xs = sb("xs", [P, 2, HEADS, HEADDIM])
    xsd = sb("xsd", [P, HEADS, HEADDIM])
    sq = sb("sq", [P, JT, T])
    rms = sb("rms", [P, NT, 2])
    x1 = sb("x1", [P, NT, D_MODEL])

    def bank(name):
        return ctx.enter_context(nc.psum_tensor(name, [P, 512], FP32))
    pA = [bank("pA0"), bank("pA1")]
    pE = [bank("pE0"), bank("pE1")]
    pX, pS, pY, pM = bank("pX"), bank("pS"), bank("pY"), bank("pM")

    s_const = sem("constants_loaded")
    s_win = sem("w_in_loaded")
    s_wout = sem("w_out_loaded")
    s_woutn = sem("w_out_scaled")
    s_aneg = sem("a_neg_ready")
    s_init = sem("buffers_initialised")
    s_xin = sem("x_loaded")
    s_mv = sem("ln_stats_ready")
    s_std = sem("ln_std_ready")
    s_xn = sem("xn_ready")
    s_xnTp = sem("xnT_in_psum")
    s_xnT = sem("xnT_ready")
    s_proj = sem("proj_in_psum")
    s_projfree = sem("proj_bank_free")
    s_xb = sem("dt_pre_ready")
    s_abs = sem("dt_abs_ready")
    s_exp = sem("dt_exp_ready")
    s_u = sem("dt_one_plus_ready")
    s_ln = sem("dt_ln_ready")
    s_acum = sem("acum_ready")
    s_segl = sem("seg_lhs_ready")
    s_dtT = sem("dtT_ready")
    s_conv = sem("conv_ready")
    s_silu = sem("conv_silu_ready")
    s_z = sem("gate_ready")
    s_gp = sem("G_and_B_in_psum")
    s_gc = sem("GC_ready")
    s_bI = sem("B_ready")
    s_segr = sem("seg_rhs_ready")
    s_ep = sem("seg_in_psum")
    s_e = sem("decay_ready")
    s_xp = sem("x_chunk_in_psum")
    s_xs = sem("x_dt_ready")
    s_xd = sem("x_skip_ready")
    s_mc = sem("mc_ready")
    s_xsd = sem("xs_decayed_ready")
    s_yp = sem("y_in_psum")
    s_ya = sem("y_plus_skip_ready")
    s_y = sem("y_gated_ready")
    s_sp = sem("state_in_psum")
    s_st = sem("state_ready")
    s_sq = sem("y_squares_ready")
    s_ssq = sem("square_sum_in_psum")
    s_rstd2 = sem("mix_std_ready")
    s_rr = sem("mix_rstd_ready")
    s_op = sem("out_proj_in_psum")
    s_x1 = sem("x1_ready")
    s_x1out = sem("x1_stored")
    s_dch = sem("vector_chain")
    for s in (s_xin, s_mv, s_std, s_xn, s_xnTp, s_xnT, s_proj, s_projfree, s_xb, s_abs, s_exp, s_u, s_ln, s_acum, s_segl, s_dtT, s_conv, s_silu, s_z, s_gp, s_gc, s_bI, s_segr, s_ep, s_e, s_xp, s_xs, s_xd, s_mc, s_xsd, s_yp, s_ya, s_y, s_sp, s_st, s_sq, s_ssq, s_rstd2, s_rr, s_op, s_x1, s_x1out, s_dch):
        nc.sync.sem_inc(s, 1)
    block = ctx.enter_context(nc.Block())

    u_blk = d["u"]
    x1_blk = d["x1"]

    @block.sync
    def _(sp):
        for dst, src in ((ident, "ident"), (delta, "delta"), (keep, "keep"), (conv_w, "conv_w"),
                         (conv_b, "conv_b"), (dt_bias, "dt_bias"), (a_neg, "A_log"), (d_skip, "D"), (norm_w, "norm_w")):
            sp.dma_start(dst[:], d[src]).then_inc(s_const, 16)
        sp.dma_start(seg_r[32:64, 0], d["delta"]).then_inc(s_const, 16)
        sp.dma_start(seg_r[32:64, 1], d["delta"]).then_inc(s_const, 16)
        for b in range(2):
            sp.dma_start(seg_r[64:P, b], d["mask"]).then_inc(s_const, 16)
        sp.dma_start(seg_l[64:P, :, 0:64], d["ident"][0:64, None, 0:64].to_broadcast([64, NC, 64])).then_inc(s_const, 16)
        sp.dma_start(bI[64:P, :, :], d["ident"][0:64, None, 0:64].to_broadcast([64, NC, 64])).then_inc(s_const, 16)
        for k in range(KD):
            sp.dma_start(w_in[:, k, :], d["w_in"][k * P:(k + 1) * P, :]).then_inc(s_win, 16)
        for k in range(JT):
            sp.dma_start(w_out[:, k, :], d["w_out"][k * P:(k + 1) * P, :]).then_inc(s_wout, 16)
        with sp.Fori(0, NB) as i:
            sp.wait_ge(s_x1, 1 + i * NT)
            sp.dma_start(xin[:], u_blk[bass.ds(i * T, T), :].rearrange("(t p) d -> p t d", p=P)).then_inc(s_xin, 16)
            sp.wait_ge(s_x1, 1 + i * NT + NT)
            sp.dma_start(x1_blk[bass.ds(i * T, T), :].rearrange("(t p) d -> p t d", p=P), x1[:]).then_inc(s_x1out, 16)
        sp.wait_ge(s_x1out, 1 + 16 * NB)

    NCONST = 15 * 16
    NINIT = 8
    NCHAIN = 2 + 4 + 2 * NCONV + 1

    @block.tensor
    def _(pe):
        pe.wait_ge(s_const, NCONST)
        pe.wait_ge(s_init, NINIT)
        pe.wait_ge(s_win, 16 * KD)
        pe.wait_ge(s_woutn, JT)
        with pe.Fori(0, NB) as i:
            for t in range(NT):
                pe.wait_ge(s_xn, 1 + i * NT + t + 1)
                if t == 0:
                    pe.wait_ge(s_rstd2, 1 + i)
                else:
                    pe.wait_ge(s_xnT, 1 + i * NT + t)
                for k in range(KD):
                    last = nc.tensor.transpose(pM[:, k * P:(k + 1) * P], xn[:, t, k * P:(k + 1) * P], ident[:])
                last.then_inc(s_xnTp, 1)
            pe.wait_ge(s_xnT, 1 + i * NT + NT)
            for m, (c0, wd) in enumerate(PROJ_TILES):
                if m < 2:
                    pe.wait_ge(s_projfree, 1 + i * NPROJ)
                    pe.wait_ge(s_x1, 1 + i * NT)
                else:
                    pe.wait_ge(s_projfree, 1 + i * NPROJ + m - 1)
                for k in range(KD):
                    last = nc.tensor.matmul(pA[m % 2][0:wd, 0:T], w_in[:, k, c0:c0 + wd], xnT[:, k, :],
                                            start=(k == 0), stop=(k == KD - 1))
                last.then_inc(s_proj, 1)
            pe.wait_ge(s_acum, 1 + i + 1)
            pe.wait_ge(s_silu, 1 + i * NCONV + 2)
            pe.wait_ge(s_ya, 1 + i * NC)
            for t in range(NT):
                nc.tensor.transpose(pM[:, t * P:(t + 1) * P], dts[:, 4, t * P:(t + 1) * P], ident[:])
            for c in range(NC):
                cs = slice(c * CHUNK, (c + 1) * CHUNK)
                nc.tensor.transpose(pY[0:CHUNK, T + c * CHUNK:T + (c + 1) * CHUNK], gc[0:64, cs], ident[0:64, 0:64])
            for c in range(NC):
                cs = slice(c * CHUNK, (c + 1) * CHUNK)
                last = nc.tensor.matmul(pY[0:CHUNK, cs], gc[0:64, cs], cT[:, cs], start=True, stop=True)
            last.then_inc(s_gp, 1)
            for c in range(NC):
                cs = slice(c * CHUNK, (c + 1) * CHUNK)
                pe.wait_ge(s_segl, 1 + i + 1)
                pe.wait_ge(s_segr, 1 + i * NC + c + 1)
                for e in range(2):
                    pe.wait_ge(s_e, 1 + i * 2 * NC + 2 * c)
                    last = nc.tensor.matmul(pE[e][:, :], seg_l[:, c, :],
                                            seg_r[:, c % 2].rearrange("p h l -> p (h l)")[:, e * 512:(e + 1) * 512],
                                            start=True, stop=True)
                    last.then_inc(s_ep, 1)
                if c % 2 == 0:
                    pe.wait_ge(s_silu, 1 + i * NCONV + NCONV)
                    for e in range(2):
                        pe.wait_ge(s_xs, 1 + i * 2 * NC + 2 * c + 2 * e)
                        for j in range(4):
                            last = nc.tensor.transpose(pX[:, j * P:(j + 1) * P],
                                                       xT[:, 4 * e + j, c * CHUNK:c * CHUNK + P], ident[:])
                        last.then_inc(s_xp, 1)
                pe.wait_ge(s_mc, 1 + i * NC + c + 1)
                pe.wait_ge(s_xs, 1 + i * 2 * NC + 4 * (c // 2) + 4)
                pe.wait_ge(s_st, 1 + i * 2 * NC + 2 * c)
                pe.wait_ge(s_bI, 1 + i + 1)
                if c:
                    pe.wait_ge(s_ya, 1 + i * NC + c)
                for h in range(HEADS):
                    last = nc.tensor.matmul(pY[(h % 2) * 64:(h % 2) * 64 + 64, (h // 2) * CHUNK:(h // 2 + 1) * CHUNK],
                                            xs[:, c % 2, h, :], mc[:, h, :], start=True, stop=True)
                last.then_inc(s_yp, 1)
                pe.wait_ge(s_xsd, 1 + i * NC + c + 1)
                for e in range(2):
                    pe.wait_ge(s_st, 1 + i * 2 * NC + 2 * c + e)
                    nc.tensor.matmul(pS[64:P, :], bI[:, c, :],
                                     xsd[:].rearrange("p h q -> p (h q)")[:, e * 512:(e + 1) * 512],
                                     start=True, stop=True).then_inc(s_sp, 1)
            pe.wait_ge(s_sq, 1 + i * NC + NC)
            pe.wait_ge(s_gc, 1 + i + 1)
            for t in range(NT):
                for j in range(JT):
                    last = nc.tensor.matmul(pM[:, t:t + 1], sq[:, j, t * P:(t + 1) * P], ones[:],
                                            start=(j == 0), stop=(j == JT - 1))
            last.then_inc(s_ssq, 1)
            pe.wait_ge(s_projfree, 1 + i * NPROJ + NPROJ)
            for t in range(NT):
                for j in range(JT):
                    last = nc.tensor.matmul(pA[t][:, :], xT[:, j, t * P:(t + 1) * P], w_out[:, j, :],
                                            start=(j == 0), stop=(j == JT - 1))
                last.then_inc(s_op, 1)


    @block.scalar
    def _(act):
        act.wait_ge(s_const, NCONST)
        act.activation(a_neg[:], a_neg[:], ACT.Exp).then_inc(s_aneg, 1)
        with act.Fori(0, NB) as i:
            act.wait_ge(s_mv, 1 + i + 1)
            act.wait_ge(s_x1, 1 + i * NT)
            act.activation(std[:], mv[:, :, 1], ACT.Sqrt, bias=eps[:, 0:1]).then_inc(s_std, 1)
            for t in range(NT):
                act.wait_ge(s_xnTp, 1 + i * NT + t + 1)
                act.activation(xnT[:, :, t * P:(t + 1) * P], pM[:, :].rearrange("p (k n) -> p k n", k=KD),
                               ACT.Copy).then_inc(s_xnT, 1)
            act.wait_ge(s_proj, 1 + i * NPROJ + 1)
            act.activation(dts[:, 0, :], pA[0][:, 0:T], ACT.Identity, bias=dt_bias[:]).then_inc(s_projfree, 1)
            act.wait_ge(s_projfree, 1 + i * NPROJ + 1)
            act.activation(dts[:, 1, :], dts[:, 0, :], ACT.Abs).then_inc(s_abs, 1)
            act.wait_ge(s_abs, 1 + i + 1)
            act.activation(dts[:, 2, :], dts[:, 1, :], ACT.Exp, scale=-1.0).then_inc(s_exp, 1)
            act.wait_ge(s_u, 1 + i + 1)
            act.activation(dts[:, 5, :], dts[:, 3, :], ACT.Ln).then_inc(s_ln, 1)

            def silu(m):
                wd = CONV_TILES[m][1]
                dst = gc[:, :] if m == 0 else cT[:, :] if m == 1 else xT[:, m - 2, :]
                act.wait_ge(s_conv, 1 + i * NCONV + m + 1)
                act.activation(dst, acc[0:wd, m % 2, :], ACT.Silu).then_inc(s_silu, 1)

            for m in range(NCONV):
                wd = CONV_TILES[m][1]
                src = pA[(m + 1) % 2][0:wd, 0:T]
                act.wait_ge(s_proj, 1 + i * NPROJ + m + 2)
                if m >= 2:
                    act.wait_ge(s_silu, 1 + i * NCONV + m - 1)
                act.activation(acc[0:wd, m % 2, :], src, ACT.Identity, bias=conv_b[0:wd, m:m + 1],
                               scale=conv_w[0:wd, m, 3:4])
                act.activation(raw[0:wd, m, 3:3 + T], src, ACT.Copy).then_inc(s_projfree, 1)
                if m >= 1:
                    silu(m - 1)
            silu(NCONV - 1)
            for j in range(JT):
                m = 1 + NCONV + j
                act.wait_ge(s_proj, 1 + i * NPROJ + m + 1)
                act.activation(gate[:, j, :], pA[m % 2][:, 0:T], ACT.Silu).then_inc(s_projfree, 1)
            for c in range(NC):
                cs = slice(c * CHUNK, (c + 1) * CHUNK)
                act.wait_ge(s_xsd, 1 + i * NC + c)
                for e in range(2):
                    act.wait_ge(s_ep, 1 + i * 2 * NC + 2 * c + e + 1)
                    act.activation(decay[:, 8 * e:8 * e + 8, :].rearrange("p h l -> p (h l)"), pE[e][:, :],
                                   ACT.Exp).then_inc(s_e, 1)
                for e in range(2):
                    act.wait_ge(s_sp, 1 + i * 2 * NC + 2 * c + e + 1)
                    act.activation(xs[64:P, (c + 1) % 2, 8 * e:8 * e + 8, :].rearrange("p h q -> p (h q)"), pS[64:P, :],
                                   ACT.Copy).then_inc(s_st, 1)
                act.wait_ge(s_y, 1 + i * NC + c + 1)
                act.wait_ge(s_ssq, 1 + i)
                act.activation(sq[:, :, cs], xT[:, :, cs], ACT.Square).then_inc(s_sq, 1)
            act.wait_ge(s_ssq, 1 + i + 1)
            act.activation(rms[:, :, 0], pM[:, 0:NT], ACT.Sqrt, scale=1.0 / D_INNER, bias=eps[:, 1:2]).then_inc(s_rstd2, 1)

    @block.vector
    def _(dve):
        chain = [0]

        def link(ins, i):
            chain[0] += 1
            ins.then_inc(s_dch, 1)
            dve.wait_ge(s_dch, 1 + i * NCHAIN + chain[0])

        dve.memset(eps[:, 0:1], LN_EPS).then_inc(s_init, 1)
        dve.memset(eps[:, 1:2], MIX_EPS).then_inc(s_init, 1)
        dve.memset(raw[:], 0.0).then_inc(s_init, 1)
        dve.memset(seg_l[0:32], 1.0).then_inc(s_init, 1)
        dve.memset(seg_l[32:64], 0.0).then_inc(s_init, 1)
        dve.memset(seg_l[64:P, :, 64:P], 0.0).then_inc(s_init, 1)
        dve.memset(xs[64:P, 0], 0.0).then_inc(s_init, 1)
        dve.memset(ones[:], 1.0).then_inc(s_init, 1)
        dve.wait_ge(s_const, NCONST)
        dve.wait_ge(s_aneg, 1)
        dve.wait_ge(s_init, NINIT)
        with dve.Fori(0, NB) as i:
            dve.wait_ge(s_xin, 1 + i * 16 + 16)
            for t in range(NT):
                ins = dve.bn_stats(stats[:, t, :], xin[:, t, :])
            link(ins, i)
            dve.tensor_copy(raw[:, :, 0:3], raw[:, :, T:T + 3])
            for t in range(NT):
                last = dve.bn_aggr(mv[:, t, :], stats[:, t, :])
            last.then_inc(s_mv, 1)
            dve.wait_ge(s_std, 1 + i + 1)
            link(dve.reciprocal(rstd[:], std[:]), i)
            for t in range(NT):
                dve.tensor_scalar(xn[:, t, :], xin[:, t, :], mv[:, t, 0:1], rstd[:, t:t + 1],
                                  ALU.subtract, ALU.mult).then_inc(s_xn, 1)
            dve.wait_ge(s_exp, 1 + i + 1)
            dve.tensor_scalar(dts[:, 3, :], dts[:, 2, :], 1.0, None, ALU.add).then_inc(s_u, 1)
            dve.wait_ge(s_u, 1 + i + 1)
            link(dve.scalar_tensor_tensor(dts[:, 1, :], dts[:, 3, :], -1.0, dts[:, 2, :], ALU.add, ALU.subtract), i)
            dve.wait_ge(s_ln, 1 + i + 1)
            link(dve.tensor_tensor(dts[:, 5, :], dts[:, 5, :], dts[:, 1, :], ALU.subtract), i)
            link(dve.scalar_tensor_tensor(dts[:, 4, :], dts[:, 0, :], 0.0, dts[:, 5, :], ALU.max, ALU.add), i)
            link(dve.tensor_scalar(dts[:, 2, :], dts[:, 4, :], a_neg[:], -1.0, ALU.mult, ALU.mult), i)
            dve.tensor_tensor_scan(acum[:], keep[:], dts[:, 2, :], 0.0, ALU.mult, ALU.add).then_inc(s_acum, 1)
            dve.wait_ge(s_acum, 1 + i + 1)
            dve.tensor_scalar(seg_l[32:64, :, 0:CHUNK], acum[32:64, :].rearrange("p (c s) -> p c s", c=NC), -1.0, None,
                              ALU.mult).then_inc(s_segl, 1)
            for m in range(NCONV):
                wd = CONV_TILES[m][1]
                dve.wait_ge(s_projfree, 1 + i * NPROJ + m + 2)
                for k in range(3):
                    ins = dve.scalar_tensor_tensor(acc[0:wd, m % 2, :], raw[0:wd, m, k:k + T], conv_w[0:wd, m, k:k + 1],
                                                   acc[0:wd, m % 2, :], ALU.mult, ALU.add)
                    if k < 2:
                        link(ins, i)
                ins.then_inc(s_conv, 1)
            dve.wait_ge(s_gp, 1 + i + 1)
            dve.tensor_copy(dtT[:], pM[:, 0:NT * P].rearrange("p (t r) -> p t r", t=NT)[:, :, 0:HEADS]).then_inc(s_dtT, 1)
            dve.tensor_copy(gc[0:64, :], pY[0:64, 0:T]).then_inc(s_gc, 1)
            dve.tensor_copy(bI[0:CHUNK, :, :], pY[0:CHUNK, T:2 * T].rearrange("p (c n) -> p c n", c=NC)).then_inc(s_bI, 1)
            dve.wait_ge(s_gc, 1 + i + 1)
            for c in range(NC):
                cs = slice(c * CHUNK, (c + 1) * CHUNK)
                if c % 2 == 0:
                    dve.wait_ge(s_yp, 1 + i * NC + c)
                    dve.wait_ge(s_dtT, 1 + i + 1)
                    for e in range(2):
                        dve.wait_ge(s_xp, 1 + i * NC + c + e + 1)
                        for b in range(2):
                            rows = slice(b * 64, b * 64 + 64)
                            dve.tensor_tensor(xs[0:64, b, 8 * e:8 * e + 8, :],
                                              pX[rows, :].rearrange("p (h q) -> p h q", h=8),
                                              dtT[rows, c // 2, 8 * e:8 * e + 8, None].to_broadcast([64, 8, HEADDIM]),
                                              ALU.mult).then_inc(s_xs, 1)
                dve.wait_ge(s_e, 1 + i * 2 * NC + 2 * c + 2)
                dve.wait_ge(s_yp, 1 + i * NC + c)
                dve.tensor_tensor(mc[:], decay[:], gc[:, None, cs].to_broadcast([P, HEADS, CHUNK]),
                                  ALU.mult).then_inc(s_mc, 1)
                dve.wait_ge(s_st, 1 + i * 2 * NC + 2 * c)
                dve.wait_ge(s_xs, 1 + i * 2 * NC + 4 * (c // 2) + 4)
                dve.wait_ge(s_sp, 1 + i * 2 * NC + 2 * c)
                dve.tensor_tensor(xsd[:], xs[:, c % 2], decay[:, :, CHUNK - 1:CHUNK].to_broadcast([P, HEADS, HEADDIM]),
                                  ALU.mult).then_inc(s_xsd, 1)
                dve.wait_ge(s_yp, 1 + i * NC + c + 1)
                dve.wait_ge(s_xd, 1 + i * NC + c + 1)
                dve.tensor_tensor(xT[:, :, cs], pY[:, :].rearrange("p (j l) -> p j l", j=JT), xT[:, :, cs],
                                  ALU.add).then_inc(s_ya, 1)
                dve.wait_ge(s_ya, 1 + i * NC + c + 1)
                dve.wait_ge(s_projfree, 1 + i * NPROJ + NPROJ)
                dve.tensor_tensor(xT[:, :, cs], xT[:, :, cs], gate[:, :, cs], ALU.mult).then_inc(s_y, 1)
            dve.wait_ge(s_rstd2, 1 + i + 1)
            link(dve.reciprocal(rms[:, :, 1], rms[:, :, 0]), i)
            dve.wait_ge(s_x1out, 1 + i * 16)
            for t in range(NT):
                dve.wait_ge(s_op, 1 + i * NT + t + 1)
                dve.scalar_tensor_tensor(x1[:, t, :], pA[t][:, :], rms[:, t, 1:2], xin[:, t, :], ALU.mult,
                                         ALU.add).then_inc(s_x1, 1)
        assert chain[0] == NCHAIN

    @block.gpsimd
    def _(pool):
        pool.wait_ge(s_const, NCONST)
        for j in range(JT):
            pool.wait_ge(s_wout, 16 * JT)
            if j:
                pool.wait_ge(s_woutn, j)
            pool.tensor_scalar(w_out[:, j, :], w_out[:, j, :], norm_w[:, j:j + 1], 1.0, ALU.mult, ALU.mult).then_inc(s_woutn, 1)
        pool.wait_ge(s_woutn, JT)
        with pool.Fori(0, NB) as i:
            for c in range(NC):
                cs = slice(c * CHUNK, (c + 1) * CHUNK)
                pool.wait_ge(s_acum, 1 + i + 1)
                pool.wait_ge(s_ep, 1 + i * 2 * NC + 2 * max(c - 1, 0))
                pool.wait_ge(s_xd, 1 + i * NC + c)
                pool.tensor_tensor(seg_r[0:32, c % 2], delta[:],
                                   acum[0:32, None, cs].to_broadcast([32, HEADS, CHUNK]), ALU.mult).then_inc(s_segr, 1)
                pool.wait_ge(s_xp, 1 + i * NC + 2 * (c // 2) + 2)
                pool.wait_ge(s_segr, 1 + i * NC + c + 1)
                pool.tensor_tensor(xT[:, :, cs], xT[:, :, cs], d_skip[:, :, None].to_broadcast([P, JT, CHUNK]),
                                   ALU.mult).then_inc(s_xd, 1)


def unpack(nc, ctx, d, w_gu, w_dn):
    def sb(name, shape, dt):
        return ctx.enter_context(nc.sbuf_tensor(name, shape, dt))

    def sem(name):
        return ctx.enter_context(nc.semaphore(name))

    O = 2 * I_FFN
    NP_ = 4
    W = O // NP_
    word = sb("word", [P, O], I32)
    scale = sb("scale", [P, O], FP16)
    lo = sb("lo", [P, 2, 1536], I32)
    sign = sb("sign", [P, 1536], I32)
    dword = sb("dword", [P, GT, D_MODEL], I32)
    dscale = sb("dscale", [P, GT, D_MODEL], FP16)
    shift = sb("shift", [P, 1], I32)
    s_gup = sem("gate_up_loaded")
    s_dn = sem("down_loaded")
    s_ch = sem("unpack_chain")
    s_done = sem("unpack_done")
    block = ctx.enter_context(nc.Block())

    @block.sync
    def _(sp):
        sp.dma_start(word[0:64, :], d["gu_packed"]).then_inc(s_gup, 16)
        sp.dma_start(word[64:P, :], d["gu_packed"]).then_inc(s_gup, 16)
        sp.dma_start(scale[:], d["gu_scale"]).then_inc(s_gup, 16)
        for n in range(8):
            sp.dma_start(dword[16 * n:16 * n + 16], d["dn_packed"].rearrange("g w o -> w g o")).then_inc(s_dn, 16)
        sp.dma_start(dscale[:], d["dn_scale"][None, :, :].to_broadcast([P, GT, D_MODEL])).then_inc(s_dn, 16)
        sp.dma_start(shift[:], d["shift"]).then_inc(s_dn, 16)

    @block.vector
    def _(dve):
        chain = [0]

        def link(ins):
            chain[0] += 1
            ins.then_inc(s_ch, 1)
            dve.wait_ge(s_ch, chain[0])

        dve.wait_ge(s_gup, 48)
        for q in range(NP_):
            cols = slice(q * W, (q + 1) * W)
            dve.tensor_scalar(lo[0:64, 0, 0:W], word[0:64, cols], 2, 0x1C1C1C1C, ALU.logical_shift_left, ALU.bitwise_and)
            dve.tensor_scalar(lo[64:P, 0, 0:W], word[64:P, cols], 2, 0x1C1C1C1C, ALU.logical_shift_right, ALU.bitwise_and)
            dve.tensor_scalar(sign[0:64, 0:W], word[0:64, cols], 4, M80, ALU.logical_shift_left, ALU.bitwise_and)
            link(dve.tensor_scalar(sign[64:P, 0:W], word[64:P, cols], M80, 0, ALU.bitwise_and, ALU.logical_shift_left))
            link(dve.tensor_tensor(lo[:, 0, 0:W], lo[:, 0, 0:W], sign[:, 0:W], ALU.bitwise_or))
            val = lo[:, 0, 0:W].bitcast(FP8).rearrange("p (o b) -> p o b", b=4)
            for b in range(KD):
                last = dve.scalar_tensor_tensor(w_gu[:, b, cols], val[:, :, b], 64.0, scale[:, cols], ALU.mult, ALU.mult)
            link(last)
        dve.wait_ge(s_dn, 160)
        for g in range(GT):
            link(dve.tensor_tensor(lo[:, 0, 0:D_MODEL], dword[:, g, :], shift[:].to_broadcast([P, D_MODEL]), ALU.logical_shift_right))
            dve.tensor_scalar(sign[:, 0:D_MODEL], lo[:, 0, 0:D_MODEL], 8, 4, ALU.bitwise_and, ALU.logical_shift_left)
            link(dve.tensor_scalar(lo[:, 1, 0:D_MODEL], lo[:, 0, 0:D_MODEL], 7, 2, ALU.bitwise_and, ALU.logical_shift_left))
            link(dve.tensor_tensor(lo[:, 0, 0:D_MODEL], lo[:, 1, 0:D_MODEL], sign[:, 0:D_MODEL], ALU.bitwise_or))
            val = lo[:, 0, 0:D_MODEL].bitcast(FP8).rearrange("p (o b) -> p o b", b=4)
            link(dve.scalar_tensor_tensor(w_dn[:, g, :], val[:, :, 0], 64.0, dscale[:, g, :], ALU.mult, ALU.mult))


M80 = -2139062144


def ffn(nc, ctx, d, w_gu, w_dn):
    def sb(name, shape, dt=FP32):
        return ctx.enter_context(nc.sbuf_tensor(name, shape, dt))

    def sem(name):
        return ctx.enter_context(nc.semaphore(name))

    def bank(name):
        return ctx.enter_context(nc.psum_tensor(name, [P, 512], FP32))

    ident = sb("f_ident", [P, P])
    eps = sb("f_eps", [P, 2])
    x1 = sb("f_x1", [P, NTF, D_MODEL])
    stats = sb("f_stats", [P, NTF, 6])
    mv = sb("f_mv", [P, NTF, 2])
    std = sb("f_std", [P, NTF])
    rstd = sb("f_rstd", [P, NTF])
    xn = sb("f_xn", [P, NTF, D_MODEL])
    xnT = sb("f_xnT", [P, KD, TF])
    sg = sb("f_sg", [P, 2, TF])
    hT = sb("f_hT", [P, GT, TF])
    junk = sb("f_junk", [P, D_MODEL])
    ssq = sb("f_ssq", [P, NTF, 3])
    o = sb("f_o", [P, NTF, D_MODEL])
    pT = [bank("f_pT0"), bank("f_pT1")]
    pG = [bank("f_pG0"), bank("f_pG1")]
    pU = [bank("f_pU0"), bank("f_pU1")]
    pD = [bank("f_pD0"), bank("f_pD1")]
    s_id = sem("f_ident_loaded")
    s_eps = sem("f_eps_ready")
    s_x = sem("f_x_loaded")
    s_st = sem("f_stats_ready")
    s_mv = sem("f_mv_ready")
    s_std = sem("f_std_ready")
    s_rstd = sem("f_rstd_ready")
    s_xn = sem("f_xn_ready")
    s_tp = sem("f_xnT_in_psum")
    s_t = sem("f_xnT_ready")
    s_g = sem("f_gate_in_psum")
    s_u = sem("f_up_in_psum")
    s_sg = sem("f_silu_ready")
    s_h = sem("f_h_ready")
    s_d = sem("f_down_in_psum")
    s_q = sem("f_ssq_ready")
    s_r = sem("f_rms_ready")
    s_rr = sem("f_rrms_ready")
    s_o = sem("f_out_ready")
    s_out = sem("f_out_stored")
    for s in (s_x, s_st, s_mv, s_std, s_rstd, s_xn, s_tp, s_t, s_g, s_u, s_sg, s_h, s_d, s_q, s_r, s_rr, s_o, s_out):
        nc.sync.sem_inc(s, 1)
    block = ctx.enter_context(nc.Block())

    @block.sync
    def _(sp):
        sp.dma_start(ident[:], d["ident"]).then_inc(s_id, 16)
        with sp.Fori(0, NBF) as i:
            sp.wait_ge(s_o, 1 + i * NTF)
            sp.dma_start(x1[:], d["x1"][bass.ds(i * TF, TF), :].rearrange("(t p) d -> p t d", p=P)).then_inc(s_x, 16)
            sp.wait_ge(s_o, 1 + i * NTF + NTF)
            sp.dma_start(d["out"][bass.ds(i * TF, TF), :].rearrange("(t p) d -> p t d", p=P), o[:]).then_inc(s_out, 16)
        sp.wait_ge(s_out, 1 + 16 * NBF)

    @block.tensor
    def _(pe):
        pe.wait_ge(s_id, 16)
        with pe.Fori(0, NBF) as i:
            for t in range(NTF):
                pe.wait_ge(s_xn, 1 + i * NTF + t + 1)
                pe.wait_ge(s_t, 1 + i * NTF)
                for k in range(KD):
                    last = nc.tensor.transpose(pT[t][:, k * P:(k + 1) * P], xn[:, t, k * P:(k + 1) * P], ident[:])
                last.then_inc(s_tp, 1)
            pe.wait_ge(s_t, 1 + i * NTF + NTF)
            for g in range(GT):
                pe.wait_ge(s_sg, 1 + i * GT + max(g - 1, 0))
                for k in range(KD):
                    last = nc.tensor.matmul(pG[g % 2][:, 0:TF], w_gu[:, k, g * P:(g + 1) * P], xnT[:, k, :],
                                            start=(k == 0), stop=(k == KD - 1))
                last.then_inc(s_g, 1)
                pe.wait_ge(s_h, 1 + i * GT + max(g - 1, 0))
                for k in range(KD):
                    last = nc.tensor.matmul(pU[g % 2][:, 0:TF], w_gu[:, k, I_FFN + g * P:I_FFN + (g + 1) * P],
                                            xnT[:, k, :], start=(k == 0), stop=(k == KD - 1))
                last.then_inc(s_u, 1)
            pe.wait_ge(s_h, 1 + i * GT + GT)
            pe.wait_ge(s_o, 1 + i * NTF)
            for t in range(NTF):
                for g in range(GT):
                    last = nc.tensor.matmul(pD[t][:, :], hT[:, g, t * P:(t + 1) * P], w_dn[:, g, :],
                                            start=(g == 0), stop=(g == GT - 1))
                last.then_inc(s_d, 1)

    @block.scalar
    def _(act):
        act.wait_ge(s_eps, 2)
        with act.Fori(0, NBF) as i:
            act.wait_ge(s_mv, 1 + i + 1)
            act.activation(std[:], mv[:, :, 1], ACT.Sqrt, bias=eps[:, 0:1]).then_inc(s_std, 1)
            for t in range(NTF):
                act.wait_ge(s_tp, 1 + i * NTF + t + 1)
                act.activation(xnT[:, :, t * P:(t + 1) * P], pT[t][:, :].rearrange("p (k n) -> p k n", k=KD),
                               ACT.Copy).then_inc(s_t, 1)
            for g in range(GT):
                act.wait_ge(s_g, 1 + i * GT + g + 1)
                act.wait_ge(s_h, 1 + i * GT + max(g - 1, 0))
                act.activation(sg[:, g % 2, :], pG[g % 2][:, 0:TF], ACT.Silu).then_inc(s_sg, 1)
            for t in range(NTF):
                act.wait_ge(s_d, 1 + i * NTF + t + 1)
                act.wait_ge(s_q, 1 + i * NTF + t)
                act.activation(junk[:], pD[t][:, :], ACT.Square, accum_out=ssq[:, t, 0:1]).then_inc(s_q, 1)
            act.wait_ge(s_q, 1 + i * NTF + NTF)
            for t in range(NTF):
                act.activation(ssq[:, t, 1:2], ssq[:, t, 0:1], ACT.Sqrt, scale=1.0 / D_MODEL,
                               bias=eps[:, 1:2]).then_inc(s_r, 1)

    @block.vector
    def _(dve):
        dve.memset(eps[:, 0:1], LN_EPS).then_inc(s_eps, 1)
        dve.memset(eps[:, 1:2], FFN_EPS).then_inc(s_eps, 1)
        with dve.Fori(0, NBF) as i:
            dve.wait_ge(s_x, 1 + i * 16 + 16)
            for t in range(NTF):
                last = dve.bn_stats(stats[:, t, :], x1[:, t, :])
            last.then_inc(s_st, 1)
            dve.wait_ge(s_st, 1 + i + 1)
            dve.tensor_copy(std[:], stats[:, :, 0])
            for t in range(NTF):
                last = dve.bn_aggr(mv[:, t, :], stats[:, t, :])
            last.then_inc(s_mv, 1)
            dve.wait_ge(s_std, 1 + i + 1)
            dve.reciprocal(rstd[:], std[:]).then_inc(s_rstd, 1)
            dve.wait_ge(s_rstd, 1 + i + 1)
            for t in range(NTF):
                dve.tensor_scalar(xn[:, t, :].rearrange("p (b n w) -> p b n w", b=4, n=2),
                                  x1[:, t, :].rearrange("p (w b n) -> p b n w", b=4, n=2),
                                  mv[:, t, 0:1], rstd[:, t:t + 1], ALU.subtract, ALU.mult).then_inc(s_xn, 1)
            for g in range(GT):
                dve.wait_ge(s_u, 1 + i * GT + g + 1)
                dve.wait_ge(s_sg, 1 + i * GT + g + 1)
                if g == 0:
                    dve.wait_ge(s_d, 1 + i * NTF)
                dve.tensor_tensor(hT[:, g, :], pU[g % 2][:, 0:TF], sg[:, g % 2, :], ALU.mult).then_inc(s_h, 1)
            for t in range(NTF):
                dve.wait_ge(s_r, 1 + i * NTF + t + 1)
                dve.reciprocal(ssq[:, t, 2:3], ssq[:, t, 1:2]).then_inc(s_rr, 1)
                dve.wait_ge(s_rr, 1 + i * NTF + t + 1)
                dve.wait_ge(s_out, 1 + i * 16)
                dve.scalar_tensor_tensor(o[:, t, :], pD[t][:, :], ssq[:, t, 2:3], x1[:, t, :], ALU.mult,
                                         ALU.add).then_inc(s_o, 1)


def build(nc, d):
    with ExitStack() as ctx:
        mixer(nc, ctx, d)
    with ExitStack() as weights:
        w_gu = weights.enter_context(nc.sbuf_tensor("w_gu", [P, KD, 2 * I_FFN], FP32))
        w_dn = weights.enter_context(nc.sbuf_tensor("w_dn", [P, GT, D_MODEL], FP32))
        with ExitStack() as ctx:
            unpack(nc, ctx, d, w_gu, w_dn)
        with ExitStack() as ctx:
            ffn(nc, ctx, d, w_gu, w_dn)


def kernel(L0_attn_u, L0_attn_W_in, L0_attn_conv_w, L0_attn_conv_b, L0_attn_dt_bias, L0_attn_A_log, L0_attn_D,
           L0_attn_norm_w, L0_attn_W_out, L0_ffn_gate_up_packed, L0_ffn_gate_up_scales, L0_ffn_down_packed,
           L0_ffn_down_scales):
    import numpy as np
    import concourse.bacc as bacc
    from concourse.bass_utils import run_bass_kernel_spmd as run

    arr = np.asarray
    w_in = arr(L0_attn_W_in).T
    bc0, dt0 = 2 * D_INNER, 2 * D_INNER + 2 * D_STATE
    w_in = np.concatenate([w_in[:, :dt0], w_in[:, bc0 + D_STATE:dt0]] + [w_in[:, dt0:]] * 8, axis=1)

    def conv_rows(a):
        x, bc, c = a[:D_INNER], a[D_INNER:], a[D_INNER + D_STATE:]
        return np.concatenate([bc, c, c, x], axis=0)

    conv_w = conv_rows(arr(L0_attn_conv_w)).reshape(NCONV, P, 4).transpose(1, 0, 2)
    conv_b = conv_rows(arr(L0_attn_conv_b)).reshape(NCONV, P).T
    heads = lambda a: np.concatenate([arr(a)] * 8).reshape(P, 1)
    d_skip = np.repeat(arr(L0_attn_D), HEADDIM).reshape(JT, P).T
    norm_w = arr(L0_attn_norm_w).reshape(JT, P).T

    def ffn_cols(a):
        return a.reshape(a.shape[0], 2 * GT, 16, 8).transpose(0, 1, 3, 2).reshape(a.shape[0], 2 * I_FFN)

    gu_packed = ffn_cols(arr(L0_ffn_gate_up_packed).T)
    gu_scale = ffn_cols(arr(L0_ffn_gate_up_scales))
    gu_scale = np.concatenate([np.repeat(gu_scale, 16, axis=0)] * 2, axis=0)
    dn_packed = arr(L0_ffn_down_packed).T.reshape(GT, 16, D_MODEL)

    delta = np.zeros((32, HEADS, CHUNK), np.float32)
    for h in range(HEADS):
        delta[h, h] = 1.0
    keep = np.ones((P, T), np.float32)
    keep[:, ::CHUNK] = 0.0
    inputs = {
        "u": arr(L0_attn_u).reshape(L, D_MODEL), "w_in": w_in, "w_out": arr(L0_attn_W_out).T, "conv_w": conv_w,
        "conv_b": conv_b, "dt_bias": heads(L0_attn_dt_bias), "A_log": heads(L0_attn_A_log), "D": d_skip,
        "norm_w": norm_w, "gu_packed": gu_packed, "gu_scale": gu_scale, "dn_packed": dn_packed,
        "dn_scale": arr(L0_ffn_down_scales), "ident": np.eye(P, dtype=np.float32),
        "mask": np.repeat(-1e30 * np.tril(np.ones((CHUNK, CHUNK), np.float32), -1)[:, None, :], HEADS, axis=1).astype(np.float32), "delta": delta, "keep": keep,
        "shift": (4 * (np.arange(P) // 16)).astype(np.int32).reshape(P, 1),
    }
    inputs = {k: np.ascontiguousarray(v) for k, v in inputs.items()}
    nc = bacc.Bacc("TRN2", target_bir_lowering=False, num_devices=1)
    d = {k: nc.dram_tensor(f"in_{k}", v.shape, mybir.dt.from_np(v.dtype), kind="ExternalInput").ap()
         for k, v in inputs.items()}
    d["x1"] = nc.dram_tensor("x1_scratch", [L, D_MODEL], FP32, kind="Internal").ap()
    d["out"] = nc.dram_tensor("out_0", [L, D_MODEL], FP32, kind="ExternalOutput").ap()
    build(nc, d)
    r = run(nc, [{f"in_{k}": v for k, v in inputs.items()}], core_ids=[0])
    return r.results[0]["out_0"].reshape(1, L, D_MODEL)
```

```python
import concourse.bass as bass
from concourse import mybir
from contextlib import ExitStack

FP32 = mybir.dt.float32
BF16 = mybir.dt.bfloat16
FP32R = mybir.dt.float32r
FP16 = mybir.dt.float16
FP8 = mybir.dt.float8e4
I32 = mybir.dt.int32
U32 = mybir.dt.uint32
ALU = mybir.AluOpType
ACT = mybir.ActivationFunctionType

P = 128
L = 2048
D_MODEL = 512
D_INNER = 1024
D_STATE = 64
HEADDIM = 64
HEADS = D_INNER // HEADDIM
CHUNK = 64
I_FFN = 1408
KD = D_MODEL // P
JT = D_INNER // P
GT = I_FFN // P
LN_EPS = 1e-5
MIX_EPS = 1e-5
FFN_EPS = 1e-6

T = 256
NB = L // T
NT = T // P
NC = T // CHUNK
NCONV = JT + 2
DTB = 1
NPROJ = NCONV + JT
PROJ = NPROJ * P
IN_CHUNK = [[0, 1, 2], [3, 4, 10], [5, 6, 11], [7, 8, 12]]
IN_TAIL = [9, 13, 14, 15, 16, 17]
LATE = [2, 4, 6, 8]
SEQ = [k for tiles in IN_CHUNK for k in tiles] + IN_TAIL
POS = {k: i for i, k in enumerate(SEQ)}
X_SCALE = 2048.0
Y_SCALE = 1024.0
EXPONENT = 0x7F800000
RSQRT_MAGIC = 1597463007.0
HALF = 64
NLINK = 13
NCHAIN = NLINK + 2 * NCONV + 8
AHEAD = NCHAIN + NLINK


def weights(nc, ctx, outer, d):
    def keep(name, shape, dt=FP32):
        return outer.enter_context(nc.sbuf_tensor(name, shape, dt))

    def sb(name, shape, dt=FP32):
        return ctx.enter_context(nc.sbuf_tensor(name, shape, dt))

    def sem(name):
        return ctx.enter_context(nc.semaphore(name))

    w = {
        "in_h": keep("w_in_h", [P, KD, PROJ], FP16), "in_l": keep("w_in_l", [P, KD, PROJ], FP16),
        "out_h": keep("w_out_h", [P, JT, D_MODEL], FP16), "out_l": keep("w_out_l", [P, JT, D_MODEL], FP16),
        "unscale": keep("unscale", [P, 4]),
        "conv_w": keep("conv_w", [P, NCONV, 4]), "conv_b": keep("conv_b", [P, NCONV]),
        "a_exp": keep("a_exp", [P, 1]),
    }
    fin = sb("w_in_f", [P, KD, PROJ])
    fout = sb("w_out_f", [P, JT, D_MODEL])
    norm_w = sb("norm_w", [P, JT])
    junk = sb("w_junk", [P, PROJ], BF16)
    l1 = sb("w_l1", [P, KD + JT])
    lmax = sb("w_lmax", [P, 2])
    lall = sb("w_lall", [P, 2])
    pow2 = sb("w_pow2", [P, 2], I32)
    rp = sb("w_rp", [P, 2])
    sc = sb("w_scale", [P, 2])
    s_c = sem("w_small_loaded")
    s_i = [sem(f"w_in_loaded{k}") for k in range(KD)]
    s_o = sem("w_out_loaded")
    s_on = sem("w_out_weighted")
    s_l1 = sem("w_l1_ready")
    s_lm = sem("w_max_ready")
    s_all = sem("w_max_of_all")
    s_ch = sem("w_scale_steps")
    s_sc = sem("w_scales_ready")
    s_hi = sem("w_hi_split")
    s_lo = sem("w_lo_split")
    block = ctx.enter_context(nc.Block())

    @block.sync
    def _(sp):
        for k in range(KD):
            sp.dma_start(fin[:, k, :], d["w_in"][k * P:(k + 1) * P, :]).then_inc(s_i[k], 16)
        for dst, src in ((w["conv_w"], "conv_w"), (w["conv_b"], "conv_b"), (w["a_exp"], "A_log"), (norm_w, "norm_w")):
            sp.dma_start(dst[:], d[src]).then_inc(s_c, 16)
        sp.dma_start(fout[:], d["w_out"].rearrange("(j p) o -> p j o", p=P)).then_inc(s_o, 16)

    @block.scalar
    def _(act):
        act.wait_ge(s_c, 64)
        act.activation(w["a_exp"][:], w["a_exp"][:], ACT.Exp)
        for k in range(KD):
            act.wait_ge(s_i[k], 16)
            if k:
                act.wait_ge(s_l1, k)
            act.activation(junk[:], fin[:, k, :], ACT.Abs, accum_out=l1[:, k:k + 1]).then_inc(s_l1, 1)
        for j in range(JT):
            act.wait_ge(s_on, j + 1)
            act.wait_ge(s_l1, KD + j)
            act.activation(junk[:, 0:D_MODEL], fout[:, j, :], ACT.Abs, accum_out=l1[:, KD + j:KD + j + 1]).then_inc(s_l1, 1)
        act.wait_ge(s_sc, 1)
        for n in range(NPROJ // 2):
            c = slice(2 * n * P, 2 * (n + 1) * P)
            act.activation(w["in_h"][:, :, c], fin[:, :, c], ACT.Copy, scale=sc[:, 0:1]).then_inc(s_hi, 1)
        for j in range(JT):
            act.activation(w["out_h"][:, j, :], fout[:, j, :], ACT.Copy, scale=sc[:, 1:2]).then_inc(s_hi, 1)

    @block.gpsimd
    def _(pool):
        pool.wait_ge(s_lm, 2)
        pool.partition_all_reduce(lall[:], lmax[:], P, bass.bass_isa.ReduceOp.max).then_inc(s_all, 1)

    @block.vector
    def _(dve):
        n = [0]

        def link(ins):
            n[0] += 1
            ins.then_inc(s_ch, 1)
            dve.wait_ge(s_ch, n[0])

        dve.wait_ge(s_c, 64)
        dve.wait_ge(s_o, 16)
        for j in range(JT):
            dve.tensor_scalar(fout[:, j, :], fout[:, j, :], norm_w[:, j:j + 1], None, ALU.mult).then_inc(s_on, 1)
        dve.wait_ge(s_l1, KD + JT)
        dve.reduce_max(lmax[:, 0:1], l1[:, 0:KD], mybir.AxisListType.X).then_inc(s_lm, 1)
        dve.reduce_max(lmax[:, 1:2], l1[:, KD:], mybir.AxisListType.X).then_inc(s_lm, 1)
        dve.wait_ge(s_all, 1)
        link(dve.tensor_scalar(rp[:], lall[:], 2.0 ** -80, None, ALU.max))
        link(dve.tensor_scalar(pow2[:], rp[:].bitcast(I32), EXPONENT, 0, ALU.bitwise_and, ALU.logical_shift_left))
        link(dve.reciprocal(rp[:], pow2[:].bitcast(FP32)))
        dve.tensor_scalar(sc[:], rp[:], 2.0 ** 14, None, ALU.mult).then_inc(s_sc, 1)
        p2 = pow2[:].bitcast(FP32)
        dve.tensor_scalar(w["unscale"][:, 0:1], p2[:, 0:1], 2.0 ** -14 / X_SCALE, None, ALU.mult)
        dve.tensor_scalar(w["unscale"][:, 3:4], p2[:, 1:2], 2.0 ** -14 / Y_SCALE, None, ALU.mult)
        link(dve.tensor_scalar(w["unscale"][:, 1:2], p2[:, 0:1], 2.0 ** -15 / X_SCALE, None, ALU.mult))
        dve.tensor_scalar(w["conv_w"][:], w["conv_w"][:], w["unscale"][:, 1:2], None, ALU.mult)
        dve.tensor_scalar(w["conv_b"][:], w["conv_b"][:], 0.5, None, ALU.mult)
        dve.wait_ge(s_sc, 1)
        for n_ in range(NPROJ // 2):
            c = slice(2 * n_ * P, 2 * (n_ + 1) * P)
            dve.wait_ge(s_hi, n_ + 1)
            dve.scalar_tensor_tensor(w["in_l"][:, :, c], fin[:, :, c], sc[:, 0:1], w["in_h"][:, :, c], ALU.mult,
                                     ALU.subtract).then_inc(s_lo, 1)
        for j in range(JT):
            dve.wait_ge(s_hi, NPROJ // 2 + j + 1)
            dve.scalar_tensor_tensor(w["out_l"][:, j, :], fout[:, j, :], sc[:, 1:2], w["out_h"][:, j, :], ALU.mult,
                                     ALU.subtract).then_inc(s_lo, 1)
        dve.wait_ge(s_lo, NPROJ // 2 + JT)
    return w


def mixer(nc, ctx, d, w):
    def sb(name, shape, dt=FP32):
        return ctx.enter_context(nc.sbuf_tensor(name, shape, dt))

    def sem(name):
        return ctx.enter_context(nc.semaphore(name))

    def bank(name):
        return ctx.enter_context(nc.psum_tensor(name, [P, 512], FP32))

    conv_w, conv_b, unscale = w["conv_w"], w["conv_b"], w["unscale"]
    dt_bias = sb("dt_bias", [HALF, 1])
    d_skip = sb("d_skip", [P, JT])
    ident = sb("ident", [P, P])
    delta = sb("delta", [32, HEADS, CHUNK])
    keep = sb("keep", [HALF, T])
    part = sb("part", [HALF, 2])
    ones = sb("ones", [P, P])
    seg_r = sb("seg_r", [P, 2, HEADS, CHUNK], FP32R)
    seg_l = sb("seg_l", [P, 2, NC, P], FP32R)

    xin = sb("xin", [P, NT, D_MODEL])
    xres = sb("xres", [P, NT, D_MODEL])
    xn = sb("xn", [P, NT, D_MODEL])
    x1 = sb("x1", [P, NT, D_MODEL])
    xt_h = sb("m_xt_h", [P, KD, T], FP16)
    xt_l = sb("m_xt_l", [P, KD, T], FP16)
    stats = sb("stats", [P, NT, 6])
    mv = sb("mv", [P, NT, 2])
    var = sb("var", [P, 2 * NT])
    rs = sb("rs", [P, 2 * NT])
    nw = sb("newton", [P, 2, 2 * NT])
    waited = sb("waited", [P, 1])
    raw = sb("raw", [P, NCONV, 3 + T])
    acc = sb("acc", [P, 3, T])
    th = sb("th", [P, 2, T])
    tz = sb("tz", [P, 4, T])
    gate = sb("gate", [P, 2, JT, T])
    xT = sb("xT", [P, 2, JT, T])
    gc = sb("gc", [P, 2, T])
    bT = sb("bT", [P, T])
    dts = sb("dts", [HALF, 6, T])
    acum = sb("acum", [HALF, T])
    acum_h = sb("acum_h", [HALF, T], FP32R)
    acum_p = sb("acum_p", [HALF, 2, T])
    dtT = sb("dtT", [P, 2, NT, HEADS])
    bI = sb("bI", [P, 2, NC, D_STATE])
    decay = sb("decay", [P, 2, HEADS, CHUNK])
    mc = sb("mc", [P, HEADS, CHUNK])
    xs = sb("xs", [P, NC, HEADS, HEADDIM])
    xsd = sb("xsd", [P, HEADS, HEADDIM])
    diag = sb("diag", [P, NT, P])
    ybuf = sb("ybuf", [P, NT, JT, P])
    y_h = [ybuf[:, t].rearrange("p j n -> p (j n)").bitcast(FP16)[:, 0:JT * P].rearrange("p (j n) -> p j n", j=JT)
           for t in range(NT)]
    y_l = [ybuf[:, t].rearrange("p j n -> p (j n)").bitcast(FP16)[:, JT * P:].rearrange("p (j n) -> p j n", j=JT)
           for t in range(NT)]

    pA = [bank("pA0"), bank("pA1")]
    pE = [bank("pE0"), bank("pE1")]
    pX, pS, pY, pM = bank("pX"), bank("pS"), bank("pY"), bank("pM")

    s_const = sem("constants_loaded")
    s_init = sem("buffers_initialised")
    s_xin = sem("x_loaded")
    s_xres = sem("residual_loaded")
    s_st = sem("ln_stats_ready")
    s_mv = sem("ln_mean_var_ready")
    s_rs = sem("rsqrt_ready")
    s_xn = sem("xn_ready")
    s_tp = sem("xt_in_psum")
    s_th = sem("xt_hi_ready")
    s_tl = sem("xt_lo_ready")
    s_proj = sem("proj_in_psum")
    s_free = sem("proj_bank_free")
    s_conv = sem("conv_ready")
    s_tanh = sem("conv_tanh_ready")
    s_silu = sem("conv_silu_ready")
    s_zt = sem("z_tanh_ready")
    s_z = sem("gate_ready")
    s_abs = sem("dt_abs_ready")
    s_exp = sem("dt_exp_ready")
    s_u = sem("dt_one_plus_ready")
    s_ln = sem("dt_ln_ready")
    s_acum = sem("acum_parts_ready")
    s_segl = sem("seg_lhs_ready")
    s_gp = sem("dt_B_G_in_psum")
    s_gc = sem("dt_B_G_ready")
    s_segr = sem("seg_rhs_ready")
    s_ep = sem("seg_in_psum")
    s_e = sem("decay_ready")
    s_xp = sem("x_chunks_in_psum")
    s_xs = sem("x_dt_ready")
    s_xd = sem("x_skip_ready")
    s_mc = sem("mc_ready")
    s_xsd = sem("xs_decayed_ready")
    s_yp = sem("y_in_psum")
    s_ya = sem("y_plus_skip_ready")
    s_y = sem("y_gated_ready")
    s_sq = sem("y_squares_ready")
    s_sum = sem("squares_added")
    s_sp = sem("state_in_psum")
    s_state = sem("state_ready")
    s_ssq = sem("square_sum_in_psum")
    s_ms = sem("mean_square_ready")
    s_diag = sem("rsqrt_diag_ready")
    s_rb = sem("rsqrt_rows_in_psum")
    s_yn = sem("y_normalised")
    s_yh = sem("y_hi_ready")
    s_yl = sem("y_lo_ready")
    s_op = sem("out_proj_in_psum")
    s_x1 = sem("x1_ready")
    s_x1out = sem("x1_stored")
    s_ch = sem("vector_chain")
    for s in (s_xin, s_xres, s_st, s_mv, s_rs, s_xn, s_tp, s_th, s_tl, s_proj, s_free, s_conv, s_tanh, s_silu, s_zt,
              s_z, s_abs, s_exp, s_u, s_ln, s_acum, s_segl, s_gp, s_gc, s_segr, s_ep, s_e, s_xp, s_xs, s_xd, s_mc,
              s_xsd, s_yp, s_ya, s_y, s_sq, s_sum, s_sp, s_state, s_ssq, s_ms, s_diag, s_rb, s_yn, s_yh, s_yl, s_op, s_x1,
              s_x1out, s_ch):
        nc.sync.sem_inc(s, 1)
    block = ctx.enter_context(nc.Block())
    NCONST = 16 * 8
    NINIT = 6

    def steps(eng, step):
        with eng.Fori(0, (NB - 2) // 2) as r:
            step(2 * r, 0, True, True)
            step(2 * r + 1, 1, True, True)
        step(NB - 2, 0, True, False)
        step(NB - 1, 1, False, False)

    @block.sync
    def _(sp):
        def load_x(b):
            sp.dma_start(xin[:], d["u"][bass.ds(b * T, T), :].rearrange("(t p) d -> p t d", p=P)).then_inc(s_xin, 16)

        load_x(0)
        for dst, src in ((ident, "ident"), (delta, "delta"), (keep, "keep"), (part, "part"), (dt_bias, "dt_bias"),
                         (d_skip, "D")):
            sp.dma_start(dst[:], d[src]).then_inc(s_const, 16)
        sp.dma_start(decay[HALF:P, 0], d["mask"]).then_inc(s_const, 16)
        sp.dma_start(decay[32:HALF, 0], d["delta"]).then_inc(s_const, 16)
        sp.wait_ge(s_xn, 1 + NT)
        load_x(1)

        def step(s, par, proj, norm):
            sp.wait_ge(s_x1, 1 + s * NT)
            sp.dma_start(xres[:], d["u"][bass.ds(s * T, T), :].rearrange("(t p) d -> p t d", p=P)).then_inc(s_xres, 16)
            if norm:
                sp.wait_ge(s_xn, 1 + (s + 2) * NT)
                load_x(s + 2)
            sp.wait_ge(s_x1, 1 + (s + 1) * NT)
            sp.dma_start(d["x1"][bass.ds(s * T, T), :].rearrange("(t p) d -> p t d", p=P), x1[:]).then_inc(s_x1out, 16)
        steps(sp, step)
        sp.wait_ge(s_x1out, 1 + 16 * NB)

    @block.tensor
    def _(pe):
        def product(out, a_h, a_l, b_h, b_l, start, stop):
            nc.tensor.matmul(out, a_h, b_h, start=start, stop=False)
            nc.tensor.matmul(out, a_h, b_l, start=False, stop=False)
            return nc.tensor.matmul(out, a_l, b_h, start=False, stop=stop)

        def transposes(b):
            pe.wait_ge(s_gc, 1 + 3 * b)
            for t in range(NT):
                pe.wait_ge(s_xn, 1 + b * NT + t + 1)
                pe.wait_ge(s_tl, 1 + b * NT + t)
                for k in range(KD):
                    last = nc.tensor.transpose(pM[:, k * P:(k + 1) * P], xn[:, t, k * P:(k + 1) * P], ident[:])
                last.then_inc(s_tp, 1)

        def tile(b, k):
            pos = POS[k]
            if pos == 0:
                pe.wait_ge(s_tl, 1 + b * NT + NT)
            pe.wait_ge(s_free, 1 + b * NPROJ + max(pos - 1, 0))
            for kd in range(KD):
                c = slice(k * P, (k + 1) * P)
                last = product(pA[pos % 2][:, 0:T], w["in_h"][:, kd, c], w["in_l"][:, kd, c], xt_h[:, kd, :],
                               xt_l[:, kd, :], kd == 0, kd == KD - 1)
            last.then_inc(s_proj, 1)

        def dt_b_g(b, par):
            for t in range(NT):
                nc.tensor.transpose(pM[:, t * HALF:(t + 1) * HALF], dts[:, 4, t * P:(t + 1) * P], ident[0:HALF, 0:HALF])
            for c in range(NC):
                cs = slice(c * CHUNK, (c + 1) * CHUNK)
                nc.tensor.transpose(pY[0:CHUNK, T + c * CHUNK:T + (c + 1) * CHUNK], gc[0:HALF, par, cs],
                                    ident[0:HALF, 0:HALF])
            for c in range(NC):
                cs = slice(c * CHUNK, (c + 1) * CHUNK)
                last = nc.tensor.matmul(pY[0:CHUNK, cs], bT[HALF:P, cs], gc[HALF:P, par, cs], start=True, stop=True)
            last.then_inc(s_gp, 1)

        def wait_dt_b_g(b):
            pe.wait_ge(s_acum, 1 + b + 1)
            pe.wait_ge(s_silu, 1 + b * NCONV + 2)
            pe.wait_ge(s_ya, 1 + b * NC)
            pe.wait_ge(s_ms, 1 + b)

        def exponents(s, par, c):
            pe.wait_ge(s_segr, 1 + s * NC + c + 1)
            pe.wait_ge(s_segl, 1 + s + 1)
            pe.wait_ge(s_e, 1 + s * 2 * NC + 2 * c)
            for e in range(2):
                nc.tensor.matmul(pE[e][:, :], seg_l[:, par, c, :],
                                 seg_r[:, c % 2].rearrange("p h l -> p (h l)")[:, e * 512:(e + 1) * 512],
                                 start=True, stop=True).then_inc(s_ep, 1)

        def x_pair(s, par, pair, e):
            pe.wait_ge(s_silu, 1 + (s + 1) * NCONV)
            pe.wait_ge(s_xs, 1 + s * 2 * NC + 4 * pair + 2 * e)
            for j in range(4):
                last = nc.tensor.transpose(pX[:, j * P:(j + 1) * P], xT[:, par, 4 * e + j, pair * P:(pair + 1) * P],
                                           ident[:])
            last.then_inc(s_xp, 1)

        def scan_y(s, c):
            pe.wait_ge(s_mc, 1 + s * NC + c + 1)
            pe.wait_ge(s_xs, 1 + s * 2 * NC + 4 * (c // 2) + 4)
            pe.wait_ge(s_state, 1 + s * 2 * NC + 2 * c)
            pe.wait_ge(s_ya, 1 + s * NC + c)
            pe.wait_ge(s_gc, 1 + s * 3 + 3)
            for h in range(HEADS):
                last = nc.tensor.matmul(pY[(h % 2) * HALF:(h % 2) * HALF + HALF, (h // 2) * CHUNK:(h // 2 + 1) * CHUNK],
                                        xs[:, c, h, :], mc[:, h, :], start=True, stop=True)
            last.then_inc(s_yp, 1)

        def next_state(s, par, c, e):
            pe.wait_ge(s_xsd, 1 + s * NC + c + 1)
            pe.wait_ge(s_state, 1 + s * 2 * NC + 2 * c + e)
            nc.tensor.matmul(pS[HALF:P, :], bI[:, par, c, :],
                             xsd[:].rearrange("p h q -> p (h q)")[:, e * 512:(e + 1) * 512],
                             start=True, stop=True).then_inc(s_sp, 1)

        def square_sums(s, proj):
            pe.wait_ge(s_sum, 1 + 3 * NC * (s + 1))
            pe.wait_ge(s_tl, 1 + (s + (2 if proj else 1)) * NT)
            for t in range(NT):
                last = nc.tensor.matmul(pM[:, 256 + t:257 + t], ybuf[:, t, 0, :], ones[:, 0:1], start=True, stop=True)
            last.then_inc(s_ssq, 1)

        def rsqrt_rows(s, proj):
            if proj:
                pe.wait_ge(s_gc, 1 + (s + 2) * 3)
            pe.wait_ge(s_ms, 1 + s + 1)
            pe.wait_ge(s_diag, 1 + s * NT + NT)
            last = nc.tensor.matmul(pM[:, 0:T], ones[:], diag[:].rearrange("p t n -> p (t n)"), start=True, stop=True)
            last.then_inc(s_rb, 1)

        def out_proj(s, t):
            pe.wait_ge(s_yl, 1 + s * NT + t + 1)
            for j in range(JT):
                last = product(pA[t][:, :], y_h[t][:, j, :], y_l[t][:, j, :], w["out_h"][:, j, :], w["out_l"][:, j, :],
                               j == 0, j == JT - 1)
            last.then_inc(s_op, 1)

        def step(s, par, proj, norm):
            for c in range(NC):
                tiles = IN_CHUNK[c] if proj else []
                if c < 2:
                    x_pair(s, par, 1, c)
                scan_y(s, c)
                if c < NC - 1:
                    exponents(s, par, c + 1)
                for k in tiles[0:1]:
                    if k == 0:
                        pe.wait_ge(s_x1, 1 + s * NT)
                    tile(s + 1, k)
                next_state(s, par, c, 0)
                for k in tiles[1:2]:
                    tile(s + 1, k)
                next_state(s, par, c, 1)
                for k in tiles[2:]:
                    tile(s + 1, k)
            if proj:
                tile(s + 1, IN_TAIL[0])
                tile(s + 1, IN_TAIL[1])
            square_sums(s, proj)
            if proj:
                tile(s + 1, IN_TAIL[2])
                wait_dt_b_g(s + 1)
                tile(s + 1, IN_TAIL[3])
                dt_b_g(s + 1, 1 - par)
            rsqrt_rows(s, proj)
            if proj:
                tile(s + 1, IN_TAIL[4])
                tile(s + 1, IN_TAIL[5])
                exponents(s + 1, 1 - par, 0)
                x_pair(s + 1, 1 - par, 0, 0)
                pe.wait_ge(s_free, 1 + (s + 2) * NPROJ)
            else:
                pe.wait_ge(s_x1, 1 + s * NT)
            out_proj(s, 0)
            if proj:
                x_pair(s + 1, 1 - par, 0, 1)
            out_proj(s, 1)
            if norm:
                transposes(s + 2)

        pe.wait_ge(s_const, NCONST)
        pe.wait_ge(s_init, NINIT)
        transposes(0)
        for k in SEQ[:-1]:
            tile(0, k)
        wait_dt_b_g(0)
        tile(0, SEQ[-1])
        dt_b_g(0, 0)
        exponents(0, 0, 0)
        x_pair(0, 0, 0, 0)
        x_pair(0, 0, 0, 1)
        transposes(1)
        steps(pe, step)

    @block.scalar
    def _(act):
        def xt_hi(b):
            for t in range(NT):
                act.wait_ge(s_tp, 1 + b * NT + t + 1)
                act.activation(xt_h[:, :, t * P:(t + 1) * P], pM[:, :].rearrange("p (k n) -> p k n", k=KD),
                               ACT.Copy).then_inc(s_th, 1)

        def conv_in(b, m):
            lo = HALF if m == DTB else 0
            full = pA[POS[m] % 2]
            src = full[lo:P, 0:T]
            act.wait_ge(s_proj, 1 + b * NPROJ + POS[m] + 1)
            act.wait_ge(s_silu, 1 + b * NCONV + max(m - 2, 0))
            act.activation(acc[lo:P, m % 3, :], src, ACT.Identity, bias=conv_b[lo:P, m:m + 1], scale=conv_w[lo:P, m, 3:4])
            if m == DTB:
                act.activation(dts[:, 0, :], full[0:HALF, 0:T], ACT.Identity, bias=dt_bias[:],
                               scale=unscale[0:HALF, 0:1])
            act.activation(raw[lo:P, m, 3:3 + T], src, ACT.Copy).then_inc(s_free, 1)

        def conv_tanh(b, m):
            lo = HALF if m == DTB else 0
            act.wait_ge(s_conv, 1 + b * NCONV + m + 1)
            act.wait_ge(s_silu, 1 + b * NCONV + max(m - 1, 0))
            act.activation(th[lo:P, m % 2, :], acc[lo:P, m % 3, :], ACT.Tanh).then_inc(s_tanh, 1)

        def softplus_exp(b):
            act.wait_ge(s_free, 1 + b * NPROJ + POS[DTB] + 1)
            act.activation(dts[:, 1, :], dts[:, 0, :], ACT.Abs).then_inc(s_abs, 1)
            act.wait_ge(s_abs, 1 + b + 1)
            act.activation(dts[:, 2, :], dts[:, 1, :], ACT.Exp, scale=-1.0).then_inc(s_exp, 1)

        def softplus_log(b):
            act.wait_ge(s_u, 1 + b + 1)
            act.activation(dts[:, 5, :], dts[:, 3, :], ACT.Ln).then_inc(s_ln, 1)

        def gate_in(b, par, j):
            pos = POS[NCONV + j]
            act.wait_ge(s_proj, 1 + b * NPROJ + pos + 1)
            act.activation(gate[:, par, j, :], pA[pos % 2][:, 0:T], ACT.Copy, scale=unscale[:, 1:2])
            act.wait_ge(s_z, 1 + b * JT + max(j - 3, 0))
            act.activation(tz[:, j % 4, :], pA[pos % 2][:, 0:T], ACT.Tanh, scale=unscale[:, 1:2]).then_inc(s_free, 1)

        def decays(s, c):
            act.wait_ge(s_xsd, 1 + s * NC + max(c - 1, 0))
            for e in range(2):
                act.wait_ge(s_ep, 1 + s * 2 * NC + 2 * c + e + 1)
                act.activation(decay[:, c % 2, 8 * e:8 * e + 8, :].rearrange("p h l -> p (h l)"), pE[e][:, :],
                               ACT.Exp).then_inc(s_e, 1)

        def state(s, c, e):
            act.wait_ge(s_sp, 1 + s * 2 * NC + 2 * c + e + 1)
            act.activation(xs[HALF:P, (c + 1) % NC, 8 * e:8 * e + 8, :].rearrange("p h q -> p (h q)"), pS[HALF:P, :],
                           ACT.Copy).then_inc(s_state, 1)

        def squares(s, par, c):
            act.wait_ge(s_y, 1 + s * NC + c + 1)
            act.wait_ge(s_op, 1 + s * NT)
            act.activation(ybuf[:, c // 2, :, (c % 2) * CHUNK:(c % 2 + 1) * CHUNK],
                           xT[:, par, :, c * CHUNK:(c + 1) * CHUNK], ACT.Square).then_inc(s_sq, 1)

        def step(s, par, proj, norm):
            for c in range(NC):
                tiles = IN_CHUNK[c] if proj else []
                conv_tiles = [k for k in tiles if k < NCONV]
                if c < NC - 1:
                    decays(s, c + 1)
                for m in conv_tiles[0:1]:
                    conv_in(s + 1, m)
                state(s, c, 0)
                if proj and c > 0:
                    conv_tanh(s + 1, LATE[c - 1])
                for m in conv_tiles[1:2]:
                    conv_in(s + 1, m)
                state(s, c, 1)
                if c > 0:
                    squares(s, par, c - 1)
                for m in conv_tiles[0:1]:
                    conv_tanh(s + 1, m)
                if proj and c == 0:
                    conv_tanh(s + 1, conv_tiles[1])
                    softplus_exp(s + 1)
                if proj and c == 1:
                    softplus_log(s + 1)
                for m in conv_tiles[2:]:
                    conv_in(s + 1, m)
                for k in tiles[len(conv_tiles):]:
                    gate_in(s + 1, 1 - par, k - NCONV)
            if proj:
                conv_tanh(s + 1, LATE[-1])
            squares(s, par, NC - 1)
            if proj:
                conv_in(s + 1, IN_TAIL[0])
                conv_tanh(s + 1, IN_TAIL[0])
                for k in IN_TAIL[1:-1]:
                    gate_in(s + 1, 1 - par, k - NCONV)
            for t in range(NT):
                act.wait_ge(s_yn, 1 + s * NT + t + 1)
                act.activation(y_h[t], xT[:, par, :, t * P:(t + 1) * P], ACT.Copy).then_inc(s_yh, 1)
                if proj and t == 0:
                    gate_in(s + 1, 1 - par, JT - 1)
            if proj:
                decays(s + 1, 0)
            if norm:
                xt_hi(s + 2)

        act.wait_ge(s_const, NCONST)
        act.wait_ge(s_init, NINIT)
        xt_hi(0)
        for i, k in enumerate(SEQ):
            if k < NCONV:
                conv_in(0, k)
            else:
                gate_in(0, 0, k - NCONV)
            if i and SEQ[i - 1] < NCONV:
                conv_tanh(0, SEQ[i - 1])
            if i == 2:
                softplus_exp(0)
            if i == 4:
                softplus_log(0)
        decays(0, 0)
        xt_hi(1)
        steps(act, step)

    @block.gpsimd
    def _(pool):
        def seg_rhs(s, par, c):
            cs = slice(c * CHUNK, (c + 1) * CHUNK)
            pool.wait_ge(s_acum, 1 + s + 1)
            pool.wait_ge(s_ep, 1 + s * 2 * NC + 2 * max(c - 1, 0))
            pool.tensor_tensor(seg_r[0:32, c % 2], delta[:],
                               acum_p[0:32, par, None, cs].to_broadcast([32, HEADS, CHUNK]),
                               ALU.mult).then_inc(s_segr, 1)
            pool.wait_ge(s_segr, 1 + s * NC + c + 1)

        def skip(s, par, c):
            cs = slice(c * CHUNK, (c + 1) * CHUNK)
            pool.wait_ge(s_xp, 1 + s * NC + 2 * (c // 2) + 2)
            pool.tensor_tensor(xT[:, par, :, cs], xT[:, par, :, cs], d_skip[:, :, None].to_broadcast([P, JT, CHUNK]),
                               ALU.mult).then_inc(s_xd, 1)
            pool.wait_ge(s_xd, 1 + s * NC + c + 1)

        def gated(s, par, c):
            cs = slice(c * CHUNK, (c + 1) * CHUNK)
            pool.wait_ge(s_ya, 1 + s * NC + c + 1)
            pool.wait_ge(s_z, 1 + (s + 1) * JT)
            pool.tensor_tensor(xT[:, par, :, cs], xT[:, par, :, cs], gate[:, par, :, cs], ALU.mult).then_inc(s_y, 1)
            pool.wait_ge(s_y, 1 + s * NC + c + 1)

        def normalise(b):
            pool.wait_ge(s_tp, 1 + b * NT)
            pool.wait_ge(s_rs, 1 + b + 1)
            pool.tensor_tensor(waited[:], mv[:, 0, 0:1], mv[:, 1, 0:1], ALU.add)
            for t in range(NT):
                pool.tensor_scalar(xn[:, t, :], xin[:, t, :], mv[:, t, 0:1], rs[:, NT + t:NT + t + 1],
                                   ALU.subtract, ALU.mult).then_inc(s_xn, 1)

        def sum_squares(s, c):
            pool.wait_ge(s_sq, 1 + s * NC + c + 1)
            q = ybuf[:, c // 2, :, (c % 2) * CHUNK:(c % 2 + 1) * CHUNK]
            for i, m in enumerate((4, 2, 1)):
                pool.tensor_tensor(q[:, 0:m], q[:, 0:m], q[:, m:2 * m], ALU.add).then_inc(s_sum, 1)
                pool.wait_ge(s_sum, 1 + 3 * (s * NC + c) + i + 1)

        def step(s, par, proj, norm):
            for c in range(NC):
                if c == 0:
                    skip(s, par, 0)
                if c + 2 < NC:
                    seg_rhs(s, par, c + 2)
                if c > 0:
                    sum_squares(s, c - 1)
                gated(s, par, c)
                if c + 1 < NC:
                    skip(s, par, c + 1)
            sum_squares(s, NC - 1)
            if proj:
                seg_rhs(s + 1, 1 - par, 0)
                seg_rhs(s + 1, 1 - par, 1)
            if norm:
                normalise(s + 2)

        pool.wait_ge(s_const, NCONST)
        pool.wait_ge(s_init, NINIT)
        normalise(0)
        seg_rhs(0, 0, 0)
        seg_rhs(0, 0, 1)
        normalise(1)
        steps(pool, step)

    @block.vector
    def _(dve):
        links = [0, 0]

        def link(ins):
            links[1] += 1
            ins.then_inc(s_ch, 1)
            dve.wait_ge(s_ch, 1 + links[0] + links[1])

        def ln_stats(b):
            dve.wait_ge(s_xin, 1 + b * 16 + 16)
            for t in range(NT):
                last = dve.bn_stats(stats[:, t, :], xin[:, t, :])
            last.then_inc(s_st, 1)
            dve.wait_ge(s_st, 1 + b + 1)
            dve.wait_ge(s_xn, 1 + b * NT)
            dve.tensor_copy(nw[:, 0, 0:1], stats[:, 0, 0:1])
            for t in range(NT):
                last = dve.bn_aggr(mv[:, t, :], stats[:, t, :])
            last.then_inc(s_mv, 1)
            dve.wait_ge(s_mv, 1 + 2 * b + 1)
            dve.tensor_scalar(var[:, NT:2 * NT], mv[:, :, 1], X_SCALE ** -2, LN_EPS * X_SCALE ** -2, ALU.mult,
                              ALU.add).then_inc(s_mv, 1)
            dve.wait_ge(s_mv, 1 + 2 * b + 2)

        def rsqrt(n):
            a, b = nw[:, 0], nw[:, 1]
            link(dve.tensor_scalar(a.bitcast(I32), var[:].bitcast(I32), 1, 0, ALU.logical_shift_right,
                                   ALU.logical_shift_left))
            link(dve.tensor_scalar(rs[:].bitcast(I32), a.bitcast(I32), -1.0, RSQRT_MAGIC, ALU.mult, ALU.add))
            for i in range(4):
                link(dve.tensor_tensor(a, rs[:], rs[:], ALU.mult))
                link(dve.scalar_tensor_tensor(b, a, -0.5, var[:], ALU.mult, ALU.mult))
                ins = dve.scalar_tensor_tensor(rs[:], b, 1.5, rs[:], ALU.add, ALU.mult)
                if i < 3:
                    link(ins)
            ins.then_inc(s_rs, 1)
            dve.wait_ge(s_rs, 1 + n + 1)

        def xt_lo(b):
            for t in range(NT):
                dve.wait_ge(s_th, 1 + b * NT + t + 1)
                dve.tensor_tensor(xt_l[:, :, t * P:(t + 1) * P], pM[:, :].rearrange("p (k n) -> p k n", k=KD),
                                  xt_h[:, :, t * P:(t + 1) * P], ALU.subtract).then_inc(s_tl, 1)

        def convs(b, tiles):
            written = {}
            for k in range(3):
                for m in tiles:
                    lo = HALF if m == DTB else 0
                    if k == 0:
                        dve.wait_ge(s_free, 1 + b * NPROJ + POS[m] + 1)
                    else:
                        dve.wait_ge(s_ch, 1 + links[0] + written[m])
                    ins = dve.scalar_tensor_tensor(acc[lo:P, m % 3, :], raw[lo:P, m, k:k + T], conv_w[lo:P, m, k:k + 1],
                                                   acc[lo:P, m % 3, :], ALU.mult, ALU.add)
                    if k < 2:
                        links[1] += 1
                        written[m] = links[1]
                        ins.then_inc(s_ch, 1)
                    else:
                        ins.then_inc(s_conv, 1)

        def silu(b, par, m):
            lo = HALF if m == DTB else 0
            dst = gc[:, par, :] if m == 0 else bT[HALF:P, :] if m == DTB else xT[:, par, m - 2, :]
            dve.wait_ge(s_tanh, 1 + b * NCONV + m + 1)
            dve.tensor_copy(raw[lo:P, m, 0:3], raw[lo:P, m, T:T + 3])
            dve.scalar_tensor_tensor(dst, th[lo:P, m % 2, :], 1.0, acc[lo:P, m % 3, :], ALU.add,
                                     ALU.mult).then_inc(s_silu, 1)

        def gates(b, par, j):
            dve.wait_ge(s_free, 1 + b * NPROJ + POS[NCONV + j] + 1)
            dve.scalar_tensor_tensor(gate[:, par, j, :], tz[:, j % 4, :], 1.0, gate[:, par, j, :], ALU.add,
                                     ALU.mult).then_inc(s_z, 1)

        def one_plus(b):
            dve.wait_ge(s_exp, 1 + b + 1)
            dve.tensor_scalar(dts[:, 3, :], dts[:, 2, :], 1.0, None, ALU.add).then_inc(s_u, 1)

        def dt_parts(b, par):
            dve.wait_ge(s_u, 1 + b + 1)
            link(dve.scalar_tensor_tensor(dts[:, 1, :], dts[:, 3, :], -1.0, dts[:, 2, :], ALU.add, ALU.subtract))
            dve.wait_ge(s_ln, 1 + b + 1)
            link(dve.tensor_tensor(dts[:, 5, :], dts[:, 5, :], dts[:, 1, :], ALU.subtract))
            link(dve.scalar_tensor_tensor(dts[:, 4, :], dts[:, 0, :], 0.0, dts[:, 5, :], ALU.max, ALU.add))
            link(dve.tensor_scalar(dts[:, 2, :], dts[:, 4, :], w["a_exp"][0:HALF], -1.0, ALU.mult, ALU.mult))
            link(dve.tensor_tensor_scan(acum[:], keep[:], dts[:, 2, :], 0.0, ALU.mult, ALU.add))
            link(dve.tensor_copy(acum_h[:], acum[:]))
            high = acum_h[:].bitcast(FP32)
            link(dve.tensor_tensor(dts[:, 1, :], acum[:], high, ALU.subtract))
            link(dve.tensor_scalar(dts[:, 3, :], dts[:, 1, :], part[:, 1:2], None, ALU.mult))
            dve.scalar_tensor_tensor(acum_p[:, par, :], high, part[:, 0:1], dts[:, 3, :], ALU.mult,
                                     ALU.add).then_inc(s_acum, 1)
            dve.wait_ge(s_acum, 1 + b + 1)
            dve.tensor_scalar(seg_l[32:HALF, par, :, 0:CHUNK],
                              acum_p[32:HALF, par, :].rearrange("p (c s) -> p c s", c=NC), -1.0, None,
                              ALU.mult).then_inc(s_segl, 1)

        def dt_b_g(b, par):
            dve.wait_ge(s_gp, 1 + b + 1)
            dve.tensor_copy(dtT[:, par], pM[:, 0:NT * HALF].rearrange("p (t r) -> p t r", t=NT)[:, :, 0:HEADS]
                            ).then_inc(s_gc, 1)
            dve.tensor_copy(gc[0:HALF, par, :], pY[0:HALF, 0:T]).then_inc(s_gc, 1)
            dve.tensor_copy(bI[0:CHUNK, par, :, :], pY[0:CHUNK, T:2 * T].rearrange("p (c n) -> p c n", c=NC)
                            ).then_inc(s_gc, 1)

        def x_dt(s, par, pair, e):
            dve.wait_ge(s_xp, 1 + s * NC + 2 * pair + e + 1)
            dve.wait_ge(s_yp, 1 + s * NC)
            dve.wait_ge(s_gc, 1 + s * 3 + 3)
            for b in range(2):
                rows = slice(b * HALF, b * HALF + HALF)
                dve.tensor_tensor(xs[0:HALF, 2 * pair + b, 8 * e:8 * e + 8, :],
                                  pX[rows, :].rearrange("p (h q) -> p h q", h=8),
                                  dtT[rows, par, pair, 8 * e:8 * e + 8, None].to_broadcast([HALF, 8, HEADDIM]),
                                  ALU.mult).then_inc(s_xs, 1)

        def mix(s, par, c):
            dve.wait_ge(s_e, 1 + s * 2 * NC + 2 * c + 2)
            dve.wait_ge(s_yp, 1 + s * NC + c)
            dve.wait_ge(s_gc, 1 + s * 3 + 3)
            dve.tensor_tensor(mc[:], decay[:, c % 2],
                              gc[:, par, None, c * CHUNK:(c + 1) * CHUNK].to_broadcast([P, HEADS, CHUNK]),
                              ALU.mult).then_inc(s_mc, 1)

        def decayed(s, c):
            dve.wait_ge(s_state, 1 + s * 2 * NC + 2 * c)
            dve.wait_ge(s_xs, 1 + s * 2 * NC + 4 * (c // 2) + 4)
            dve.wait_ge(s_sp, 1 + s * 2 * NC + 2 * c)
            dve.tensor_tensor(xsd[:], xs[:, c], decay[:, c % 2, :, CHUNK - 1:CHUNK].to_broadcast([P, HEADS, HEADDIM]),
                              ALU.mult).then_inc(s_xsd, 1)

        def add_skip(s, par, c):
            cs = slice(c * CHUNK, (c + 1) * CHUNK)
            dve.wait_ge(s_yp, 1 + s * NC + c + 1)
            dve.wait_ge(s_xd, 1 + s * NC + c + 1)
            dve.tensor_tensor(xT[:, par, :, cs], pY[:, :].rearrange("p (j l) -> p j l", j=JT), xT[:, par, :, cs],
                              ALU.add).then_inc(s_ya, 1)

        def x1_tile(s, t):
            dve.wait_ge(s_op, 1 + s * NT + t + 1)
            dve.scalar_tensor_tensor(x1[:, t, :], pA[t][:, :], unscale[:, 3:4], xres[:, t, :], ALU.mult,
                                     ALU.add).then_inc(s_x1, 1)

        def step(s, par, proj, norm):
            links[0], links[1] = AHEAD + s * NCHAIN, 0
            for c in range(NC):
                tiles = IN_CHUNK[c] if proj else []
                conv_tiles = [k for k in tiles if k < NCONV and k != LATE[c]]
                decayed(s, c)
                if c == 0:
                    x_dt(s, par, 1, 0)
                elif proj:
                    convs(s + 1, LATE[c - 1:c])
                add_skip(s, par, c)
                if c < NC - 1:
                    mix(s, par, c + 1)
                if c > 0 and proj:
                    silu(s + 1, 1 - par, LATE[c - 1])
                if c == 1:
                    x_dt(s, par, 1, 1)
                convs(s + 1, conv_tiles)
                for m in conv_tiles:
                    silu(s + 1, 1 - par, m)
                if proj and c == 0:
                    one_plus(s + 1)
                if proj and c == 1:
                    dt_parts(s + 1, 1 - par)
                if proj and c > 0:
                    gates(s + 1, 1 - par, c - 1)
            if proj:
                convs(s + 1, LATE[-1:])
                silu(s + 1, 1 - par, LATE[-1])
                convs(s + 1, IN_TAIL[0:1])
                silu(s + 1, 1 - par, IN_TAIL[0])
            if norm:
                ln_stats(s + 2)
            if proj:
                gates(s + 1, 1 - par, 3)
            dve.wait_ge(s_ssq, 1 + s + 1)
            dve.tensor_scalar(var[:, 0:NT], pM[:, 256:256 + NT], 1.0 / D_INNER, MIX_EPS, ALU.mult,
                              ALU.add).then_inc(s_ms, 1)
            dve.wait_ge(s_ms, 1 + s + 1)
            rsqrt(s + 2)
            for t in range(NT):
                dve.tensor_scalar(diag[:, t, :], ident[:], rs[:, t:t + 1], Y_SCALE, ALU.mult, ALU.mult
                                  ).then_inc(s_diag, 1)
            if proj:
                dt_b_g(s + 1, 1 - par)
                gates(s + 1, 1 - par, 4)
            dve.wait_ge(s_rb, 1 + s + 1)
            for t in range(NT):
                ts = slice(t * P, (t + 1) * P)
                dve.tensor_tensor(xT[:, par, :, ts], xT[:, par, :, ts], pM[:, None, ts].to_broadcast([P, JT, P]),
                                  ALU.mult).then_inc(s_yn, 1)
            if proj:
                gates(s + 1, 1 - par, 5)
            for t in range(NT):
                dve.wait_ge(s_yh, 1 + s * NT + t + 1)
                dve.tensor_tensor(y_l[t], xT[:, par, :, t * P:(t + 1) * P], y_h[t], ALU.subtract).then_inc(s_yl, 1)
                if proj:
                    gates(s + 1, 1 - par, 6 + t)
            if proj:
                x_dt(s + 1, 1 - par, 0, 0)
                mix(s + 1, 1 - par, 0)
            dve.wait_ge(s_x1out, 1 + s * 16)
            dve.wait_ge(s_xres, 1 + s * 16 + 16)
            x1_tile(s, 0)
            if proj:
                x_dt(s + 1, 1 - par, 0, 1)
            x1_tile(s, 1)
            if norm:
                xt_lo(s + 2)

        dve.memset(raw[:], 0.0).then_inc(s_init, 1)
        dve.memset(xs[HALF:P, 0], 0.0).then_inc(s_init, 1)
        dve.memset(ones[:], 1.0).then_inc(s_init, 1)
        dve.memset(var[:], 1.0).then_inc(s_init, 1)
        dve.memset(decay[:, 1], 0.0).then_inc(s_init, 1)
        dve.wait_ge(s_init, 5)
        dve.wait_ge(s_const, NCONST)
        for b in range(2):
            dve.tensor_copy(seg_r[HALF:P, b], decay[HALF:P, 0])
            dve.tensor_copy(seg_r[32:HALF, b], decay[32:HALF, 0])
            dve.tensor_copy(seg_l[0:32, b], ones[0:32, None, :].to_broadcast([32, NC, P]))
            dve.tensor_copy(seg_l[32:HALF, b, :, HALF:P], decay[32:HALF, 1, 0:NC, :])
            dve.tensor_copy(seg_l[HALF:P, b, :, HALF:P], decay[HALF:P, 1, 0:NC, :])
            dve.tensor_copy(seg_l[HALF:P, b, :, 0:HALF], ident[HALF:P, None, HALF:P].to_broadcast([HALF, NC, HALF]))
            last = dve.tensor_copy(bI[HALF:P, b], ident[HALF:P, None, HALF:P].to_broadcast([HALF, NC, HALF]))
        last.then_inc(s_init, 1)
        ln_stats(0)
        rsqrt(0)
        xt_lo(0)
        ln_stats(1)
        for i, k in enumerate(SEQ + [None]):
            if i < NPROJ and k < NCONV:
                convs(0, [k])
            if i and SEQ[i - 1] < NCONV:
                silu(0, 0, SEQ[i - 1])
            elif i:
                gates(0, 0, SEQ[i - 1] - NCONV)
            if i == 0:
                rsqrt(1)
            if i == 2:
                one_plus(0)
            if i == 5:
                dt_parts(0, 0)
        dt_b_g(0, 0)
        x_dt(0, 0, 0, 0)
        mix(0, 0, 0)
        x_dt(0, 0, 0, 1)
        xt_lo(1)
        steps(dve, step)


TF = 512
NBF = L // TF
NTF = TF // P
WORDS_LANES = 128
GL = 8
GR = GT - GL
NIB = 0x1C1C1C1C
SGN = -2139062144


def ffn(nc, ctx, d):
    def sb(name, shape, dt=FP32):
        return ctx.enter_context(nc.sbuf_tensor(name, shape, dt))

    def sem(name):
        return ctx.enter_context(nc.semaphore(name))

    def bank(name):
        return ctx.enter_context(nc.psum_tensor(name, [P, 512], FP32))

    GC = 2 * P
    wg_h = sb("wg_h", [P, KD, GT * GC], BF16)
    wg_l = sb("wg_l", [P, KD, GT * GC], BF16)
    wd_h = sb("wd_h", [P, GT, D_MODEL], BF16)
    wd_l = sb("wd_l", [P, GT, D_MODEL], BF16)
    word = sb("word", [P, GT * GC], I32)
    scale = sb("scale", [P, GT * GC], FP16)
    dword = sb("dword", [P, 2 + GR, D_MODEL], I32)
    dscale = sb("dscale", [P, 2 + GR, D_MODEL], FP16)
    shift = sb("shift", [P, 1], I32)
    bits = sb("bits", [P, 3, D_MODEL], I32)
    wf = sb("wf", [P, 2, 4 * GC])
    wfd = wf[:].rearrange("p a b -> p (a b)")
    scales_flat = sb("scales_flat", [P, P_SC], FP16)
    sjunk = sb("sjunk", [P, P_SC], FP16)
    smax = sb("smax", [P, 2])
    pow2 = sb("pow2", [P, 1], I32)
    rp2 = sb("rp2", [P, 1])
    hs = sb("hs", [P, 1])
    hsx = sb("hsx", [P, 1])
    ident = sb("f_ident", [P, P])
    eps = sb("f_eps", [P, 2])
    xl = sb("f_xl", [P, NTF, D_MODEL])
    xr = sb("f_xr", [P, NTF, D_MODEL])
    stats = sb("f_stats", [P, NTF, 6])
    mv = sb("f_mv", [P, NTF, 2])
    std = sb("f_std", [P, NTF])
    rstd = sb("f_rstd", [P, NTF])
    xn = sb("f_xn", [P, NTF, D_MODEL])
    xt_h = sb("xt_h", [P, KD, TF], FP16)
    xt_l = sb("xt_l", [P, KD, TF], FP16)
    sg = sb("f_sg", [P, 2, TF])
    hf = sb("f_h", [P, 2, TF])
    h_h = sb("h_h", [P, GT, TF], FP16)
    h_l = sb("h_l", [P, GT, TF], FP16)
    junk = sb("f_junk", [P, D_MODEL])
    ssq = sb("f_ssq", [P, 3, NTF])
    o = sb("f_o", [P, NTF, D_MODEL])
    pT = bank("f_pT")
    pG = [bank("f_pG0"), bank("f_pG1")]
    pU = [bank("f_pU0"), bank("f_pU1")]
    pD = [bank("f_pD0"), bank("f_pD1"), pG[0], pU[0]]

    s_id = sem("f_consts_loaded")
    s_wd = sem("gate_up_words_loaded")
    s_wd2 = sem("gate_up_rest_loaded")
    s_dnw = sem("down_words_loaded")
    s_eps = sem("f_eps_ready")
    s_smax = sem("f_scale_max")
    s_bit = sem("bits_ready")
    s_wf = sem("w_float_ready")
    s_wh = sem("w_hi_ready")
    s_wl = sem("w_lo_ready")
    s_x = sem("f_x_loaded")
    s_xr = sem("f_residual_loaded")
    s_st = sem("f_stats_ready")
    s_mv = sem("f_mv_ready")
    s_std = sem("f_std_ready")
    s_rstd = sem("f_rstd_ready")
    s_xn = sem("f_xn_ready")
    s_tp = sem("f_xt_in_psum")
    s_th = sem("f_xt_hi_ready")
    s_tl = sem("f_xt_lo_ready")
    s_g = sem("f_gate_in_psum")
    s_u = sem("f_up_in_psum")
    s_sg = sem("f_silu_ready")
    s_h = sem("f_h_ready")
    s_hh = sem("f_h_hi_ready")
    s_hl = sem("f_h_lo_ready")
    s_d = sem("f_down_in_psum")
    s_q = sem("f_ssq_ready")
    s_r = sem("f_rms_ready")
    s_rr = sem("f_rrms_ready")
    s_o = sem("f_out_ready")
    s_out = sem("f_out_stored")
    for s in (s_x, s_xr, s_st, s_mv, s_std, s_rstd, s_xn, s_tp, s_th, s_tl, s_g, s_u, s_sg, s_h, s_hh, s_hl, s_d,
              s_q, s_r, s_rr, s_o, s_out):
        nc.sync.sem_inc(s, 1)
    block = ctx.enter_context(nc.Block())

    def blocks(eng, step):
        step(0, True, True)
        with eng.Fori(1, NBF - 1) as i:
            step(i, False, True)
        step(NBF - 1, False, False)

    @block.sync
    def _(sp):
        def load_x(i):
            sp.dma_start(xl[:], d["x1"][bass.ds(i * TF, TF), :].rearrange("(t p) d -> p t d", p=P)).then_inc(s_x, 16)

        load_x(0)
        sp.dma_start(ident[:], d["ident"]).then_inc(s_id, 16)
        sp.dma_start(scales_flat[:], d["gu_scale_flat"]).then_inc(s_id, 16)
        first = 2 * GC
        for half in range(2):
            sp.dma_start(word[64 * half:64 * half + 64, 0:first], d["gu_packed"][:, 0:first]).then_inc(s_wd, 16)
        sp.dma_start(scale[:, 0:first], d["gu_scale"][:, 0:first]).then_inc(s_wd, 16)
        for half in range(2):
            sp.dma_start(word[64 * half:64 * half + 64, first:], d["gu_packed"][:, first:]).then_inc(s_wd2, 16)
        sp.dma_start(scale[:, first:], d["gu_scale"][:, first:]).then_inc(s_wd2, 16)
        for half in range(2):
            sp.dma_start(dword[64 * half:64 * half + 64, 0:2, :],
                         d["dn_packed"][0:WORDS_LANES].rearrange("(q w) o -> w q o", q=2)).then_inc(s_dnw, 16)
        for n in range(8):
            sp.dma_start(dword[16 * n:16 * n + 16, 2:, :],
                         d["dn_packed"][WORDS_LANES:].rearrange("(g w) o -> w g o", g=GR)).then_inc(s_dnw, 16)
        sp.dma_start(dscale[:], d["dn_scale"]).then_inc(s_dnw, 16)
        sp.dma_start(shift[:], d["shift"]).then_inc(s_dnw, 16)

        def step(i, first, more):
            sp.wait_ge(s_o, 1 + i * NTF)
            sp.dma_start(xr[:], d["x1"][bass.ds(i * TF, TF), :].rearrange("(t p) d -> p t d", p=P)).then_inc(s_xr, 16)
            if more:
                sp.wait_ge(s_xn, 1 + (i + 1) * NTF)
                load_x(i + 1)
            sp.wait_ge(s_o, 1 + (i + 1) * NTF)
            sp.dma_start(d["out"][bass.ds(i * TF, TF), :].rearrange("(t p) d -> p t d", p=P), o[:]).then_inc(s_out, 16)
        blocks(sp, step)
        sp.wait_ge(s_out, 1 + 16 * NBF)

    @block.tensor
    def _(pe):
        def transposes(i, t):
            pe.wait_ge(s_xn, 1 + i * NTF + t + 1)
            pe.wait_ge(s_tl, 1 + i * NTF + t)
            for k in range(KD):
                last = nc.tensor.transpose(pT[:, k * P:(k + 1) * P],
                                           xn[:, t, k * P:(k + 1) * P], ident[:])
            last.then_inc(s_tp, 1)

        def product(out, parts, start, stop):
            for n, (a, b) in enumerate(parts):
                last = nc.tensor.matmul(out, a, b, start=start and n == 0, stop=stop and n == len(parts) - 1)
            return last

        def step(i, first, more):
            pe.wait_ge(s_tl, 1 + i * NTF + NTF)
            for g in range(GT):
                if first:
                    pe.wait_ge(s_wl, g + 1)
                for gu, (ps, done, free) in enumerate(((pG, s_g, s_sg), (pU, s_u, s_h))):
                    pe.wait_ge(free, 1 + i * GT + max(g - 1, 0))
                    if g == 1:
                        pe.wait_ge(s_o, 1 + i * NTF)
                    c = slice(g * GC + gu * P, g * GC + gu * P + P)
                    for k in range(KD):
                        last = product(ps[(g + 1) % 2][:, :], ((wg_h[:, k, c], xt_h[:, k, :]),
                                                                (wg_h[:, k, c], xt_l[:, k, :]),
                                                                (wg_l[:, k, c], xt_h[:, k, :])), k == 0, k == KD - 1)
                    last.then_inc(done, 1)
            for t in range(NTF):
                if more:
                    transposes(i + 1, t)
                ts = slice(t * P, (t + 1) * P)
                pe.wait_ge(s_o, 1 + i * NTF)
                if t >= 2:
                    pe.wait_ge(s_h, 1 + i * GT + GT - 1)
                for g in range(GT):
                    if first and t == 0:
                        pe.wait_ge(s_wl, GT + (g // 4 if g < GL else 2 + g - GL) + 1)
                    if t == 0 and g in (0, GT - 2, GT - 1):
                        pe.wait_ge(s_hl, 1 + i * GT + (GT - 2 if g == 0 else g + 1))
                    last = product(pD[t][:, :], ((h_h[:, g, ts], wd_h[:, g, :]), (h_l[:, g, ts], wd_h[:, g, :]),
                                                 (h_h[:, g, ts], wd_l[:, g, :])), g == 0, g == GT - 1)
                last.then_inc(s_d, 1)

        pe.wait_ge(s_id, 32)
        for t in range(NTF):
            transposes(0, t)
        blocks(pe, step)

    @block.scalar
    def _(act):
        def ln_std(i):
            act.wait_ge(s_mv, 1 + i + 1)
            act.activation(std[:], mv[:, :, 1], ACT.Sqrt, scale=X_SCALE ** -2, bias=eps[:, 0:1]).then_inc(s_std, 1)

        def xt_hi(i, t):
            act.wait_ge(s_tp, 1 + i * NTF + t + 1)
            act.activation(xt_h[:, :, t * P:(t + 1) * P], pT[:, :].rearrange("p (k n) -> p k n", k=KD),
                           ACT.Copy).then_inc(s_th, 1)

        def w_hi(n):
            act.wait_ge(s_wf, n + 1)
            if n < GT:
                act.activation(wg_h[:, :, n * GC:(n + 1) * GC], wf[:, n % 2, :].rearrange("p (k c) -> p k c", k=KD),
                               ACT.Copy).then_inc(s_wh, 1)
            elif n < GT + 2:
                q = n - GT
                act.activation(wd_h[:, 4 * q:4 * q + 4, :].rearrange("p g c -> p (g c)"), wfd[:, :],
                               ACT.Copy).then_inc(s_wh, 1)
            else:
                g = n - GT - 2 + GL
                act.activation(wd_h[:, g, :], wf[:, n % 2, 0:D_MODEL], ACT.Copy).then_inc(s_wh, 1)

        def step(i, first, more):
            for g in range(GT):
                if first:
                    for n in UNPACK_AT[g]:
                        w_hi(n)
                act.wait_ge(s_g, 1 + i * GT + g + 1)
                act.wait_ge(s_h, 1 + i * GT + max(g - 1, 0))
                act.activation(sg[:, g % 2, :], pG[(g + 1) % 2][:, :], ACT.Silu, scale=1.0 / X_SCALE).then_inc(s_sg, 1)
                if g >= 1:
                    h_hi(i, g - 1)
                if g == LN_AT and more:
                    ln_std(i + 1)
            h_hi(i, GT - 1)
            for t in range(NTF):
                if more:
                    xt_hi(i + 1, t)
                act.wait_ge(s_d, 1 + i * NTF + t + 1)
                act.wait_ge(s_q, 1 + i * NTF + t)
                act.activation(junk[:], pD[t][:, :], ACT.Square, accum_out=ssq[:, 0, t:t + 1]).then_inc(s_q, 1)
            act.wait_ge(s_q, 1 + i * NTF + NTF)
            act.activation(ssq[:, 1, :], ssq[:, 0, :], ACT.Sqrt, scale=1.0 / D_MODEL, bias=eps[:, 1:2]).then_inc(s_r, 1)

        def h_hi(i, g):
            act.wait_ge(s_h, 1 + i * GT + g + 1)
            if g == 0:
                act.wait_ge(s_d, 1 + i * NTF)
            act.activation(h_h[:, g, :], hf[:, g % 2, :], ACT.Copy).then_inc(s_hh, 1)

        act.wait_ge(s_eps, 3)
        ln_std(0)
        for t in range(NTF):
            xt_hi(0, t)
        blocks(act, step)

    @block.gpsimd
    def _(pool):
        pool.wait_ge(s_smax, 1)
        pool.partition_all_reduce(smax[:, 1:2], smax[:, 0:1], P, bass.bass_isa.ReduceOp.max).then_inc(s_smax, 1)
        pool.wait_ge(s_smax, 2)
        for g in range(GT):
            for n in UNPACK_AT[g]:
                if n:
                    pool.wait_ge(s_wl, n)
                pool.wait_ge(s_wh, n + 1)
                if n < GT:
                    c = slice(n * GC, (n + 1) * GC)
                    pool.tensor_tensor(wg_l[:, :, c], wf[:, n % 2, :].rearrange("p (k c) -> p k c", k=KD),
                                       wg_h[:, :, c], ALU.subtract).then_inc(s_wl, 1)
                elif n < GT + 2:
                    q = n - GT
                    pool.tensor_tensor(wd_l[:, 4 * q:4 * q + 4, :].rearrange("p g c -> p (g c)"), wfd[:, :],
                                       wd_h[:, 4 * q:4 * q + 4, :].rearrange("p g c -> p (g c)"),
                                       ALU.subtract).then_inc(s_wl, 1)
                else:
                    gg = n - GT - 2 + GL
                    pool.tensor_tensor(wd_l[:, gg, :], wf[:, n % 2, 0:D_MODEL], wd_h[:, gg, :],
                                       ALU.subtract).then_inc(s_wl, 1)

    @block.vector
    def _(dve):
        bit = [0]

        def link(ins):
            bit[0] += 1
            ins.then_inc(s_bit, 1)
            dve.wait_ge(s_bit, bit[0])

        def lanes(src, dst, tmp):
            dve.tensor_scalar(dst[0:64], src[0:64], 2, NIB, ALU.logical_shift_left, ALU.bitwise_and)
            dve.tensor_scalar(dst[64:P], src[64:P], 2, NIB, ALU.logical_shift_right, ALU.bitwise_and)
            dve.tensor_scalar(tmp[0:64], src[0:64], 4, SGN, ALU.logical_shift_left, ALU.bitwise_and)
            link(dve.tensor_scalar(tmp[64:P], src[64:P], SGN, 0, ALU.bitwise_and, ALU.logical_shift_left))
            link(dve.tensor_tensor(dst, dst, tmp, ALU.bitwise_or))

        def unpack(n):
            if n < GT:
                if n == 2:
                    dve.wait_ge(s_wd2, 48)
                c = slice(n * GC, (n + 1) * GC)
                lanes(word[:, c], bits[:, 0, 0:GC], bits[:, 1, 0:GC])
                val = bits[:, 0, 0:GC].bitcast(FP8).rearrange("p (o b) -> p o b", b=4)
                if n >= 2:
                    dve.wait_ge(s_wl, n - 1)
                for b in range(KD):
                    last = dve.scalar_tensor_tensor(wf[:, n % 2, b * GC:(b + 1) * GC], val[:, :, b], 64.0, scale[:, c],
                                                    ALU.mult, ALU.mult)
            elif n < GT + 2:
                q = n - GT
                if q == 0:
                    dve.wait_ge(s_dnw, 16 * 12)
                lanes(dword[:, q, :], bits[:, 0, :], bits[:, 1, :])
                val = bits[:, 0, :].bitcast(FP8).rearrange("p (o b) -> p o b", b=4)
                dve.wait_ge(s_wl, n)
                for b in range(4):
                    last = dve.scalar_tensor_tensor(wfd[:, b * D_MODEL:(b + 1) * D_MODEL], val[:, :, b], 64.0,
                                                    dscale[:, q, :], ALU.mult, ALU.mult)
            else:
                q = n - GT
                dve.wait_ge(s_wl, n if n == GT + 2 else n - 1)
                link(dve.tensor_tensor(bits[:, 2, :], dword[:, q, :], shift[:].to_broadcast([P, D_MODEL]),
                                       ALU.logical_shift_right))
                dve.tensor_scalar(bits[:, 1, :], bits[:, 2, :], 8, 4, ALU.bitwise_and, ALU.logical_shift_left)
                link(dve.tensor_scalar(bits[:, 0, :], bits[:, 2, :], 7, 2, ALU.bitwise_and, ALU.logical_shift_left))
                link(dve.tensor_tensor(bits[:, 0, :], bits[:, 0, :], bits[:, 1, :], ALU.bitwise_or))
                val = bits[:, 0, :].bitcast(FP8).rearrange("p (o b) -> p o b", b=4)
                last = dve.scalar_tensor_tensor(wf[:, n % 2, 0:D_MODEL], val[:, :, 0], 64.0, dscale[:, q, :],
                                                ALU.mult, ALU.mult)
            last.then_inc(s_wf, 1)
            dve.wait_ge(s_wf, n + 1)

        def layernorm(i):
            dve.wait_ge(s_x, 1 + i * 16 + 16)
            for t in range(NTF):
                last = dve.bn_stats(stats[:, t, :], xl[:, t, :])
            last.then_inc(s_st, 1)
            dve.wait_ge(s_st, 1 + i + 1)
            dve.tensor_copy(rstd[:, 0:1], stats[:, 0, 0:1])
            for t in range(NTF):
                last = dve.bn_aggr(mv[:, t, :], stats[:, t, :])
            last.then_inc(s_mv, 1)

        def normalise(i):
            dve.wait_ge(s_std, 1 + i + 1)
            dve.reciprocal(rstd[:], std[:]).then_inc(s_rstd, 1)
            dve.wait_ge(s_rstd, 1 + i + 1)
            for t in range(NTF):
                dve.wait_ge(s_tp, 1 + i * NTF)
                dve.tensor_scalar(xn[:, t, :].rearrange("p (b n w) -> p b n w", b=4, n=2),
                                  xl[:, t, :].rearrange("p (w b n) -> p b n w", b=4, n=2),
                                  mv[:, t, 0:1], rstd[:, t:t + 1], ALU.subtract, ALU.mult).then_inc(s_xn, 1)

        def xt_lo(i, t):
            dve.wait_ge(s_th, 1 + i * NTF + t + 1)
            dve.tensor_tensor(xt_l[:, :, t * P:(t + 1) * P], pT[:, :].rearrange("p (k n) -> p k n", k=KD),
                              xt_h[:, :, t * P:(t + 1) * P], ALU.subtract).then_inc(s_tl, 1)

        def h_lo(i, g):
            dve.wait_ge(s_hh, 1 + i * GT + g + 1)
            dve.tensor_tensor(h_l[:, g, :], hf[:, g % 2, :], h_h[:, g, :], ALU.subtract).then_inc(s_hl, 1)

        def step(i, first, more):
            for g in range(GT):
                if first:
                    for n in UNPACK_AT[g]:
                        unpack(n)
                dve.wait_ge(s_u, 1 + i * GT + g + 1)
                dve.wait_ge(s_sg, 1 + i * GT + g + 1)
                if g >= 2:
                    dve.wait_ge(s_hl, 1 + i * GT + g - 1)
                dve.scalar_tensor_tensor(hf[:, g % 2, :], pU[(g + 1) % 2][:, :], hsx[:], sg[:, g % 2, :], ALU.mult,
                                         ALU.mult).then_inc(s_h, 1)
                if g >= 1:
                    h_lo(i, g - 1)
                if g == LN_AT - 1 and more:
                    layernorm(i + 1)
                if g == LN_AT + 1 and more:
                    normalise(i + 1)
            h_lo(i, GT - 1)
            if more:
                for t in range(NTF):
                    xt_lo(i + 1, t)
            dve.wait_ge(s_r, 1 + i + 1)
            dve.reciprocal(ssq[:, 2, :], ssq[:, 1, :]).then_inc(s_rr, 1)
            dve.wait_ge(s_rr, 1 + i + 1)
            dve.wait_ge(s_out, 1 + i * 16)
            dve.wait_ge(s_xr, 1 + i * 16 + 16)
            for t in range(NTF):
                dve.scalar_tensor_tensor(o[:, t, :], pD[t][:, :], ssq[:, 2, t:t + 1], xr[:, t, :], ALU.mult,
                                         ALU.add).then_inc(s_o, 1)

        dve.wait_ge(s_id, 32)
        link(dve.scalar_tensor_tensor(sjunk[:], scales_flat[:], -1.0, scales_flat[:], ALU.mult, ALU.max))
        dve.reduce_max(smax[:, 0:1], sjunk[:], mybir.AxisListType.X).then_inc(s_smax, 1)
        dve.memset(eps[:, 0:1], LN_EPS / X_SCALE ** 2).then_inc(s_eps, 1)
        layernorm(0)
        dve.wait_ge(s_smax, 2)
        link(dve.tensor_scalar(smax[:, 0:1], smax[:, 1:2], 2.0 ** -24, None, ALU.max))
        link(dve.tensor_scalar(pow2[:], smax[:, 0:1].bitcast(I32), EXPONENT, 0, ALU.bitwise_and, ALU.logical_shift_left))
        link(dve.reciprocal(rp2[:], pow2[:].bitcast(FP32)))
        link(dve.tensor_scalar(hs[:], rp2[:], rp2[:], 2.0 ** -11, ALU.mult, ALU.mult))
        dve.tensor_scalar(hsx[:], hs[:], 1.0 / X_SCALE, None, ALU.mult).then_inc(s_eps, 1)
        dve.tensor_scalar(eps[:, 1:2], hs[:], hs[:], FFN_EPS, ALU.mult, ALU.mult).then_inc(s_eps, 1)
        normalise(0)
        dve.wait_ge(s_wd, 48)
        for t in range(NTF):
            xt_lo(0, t)
        dve.wait_ge(s_eps, 3)
        blocks(dve, step)


LN_AT = 7
P_SC = KD * 2 * I_FFN // P
UNPACK_AT = [[0, 1], [2, 3], [4], [5, 6], [7], [8], [9, 10], [GT], [GT + 1], [GT + 2], [GT + 3, GT + 4]]


def build(nc, d):
    with ExitStack() as outer:
        with ExitStack() as ctx:
            w = weights(nc, ctx, outer, d)
        with ExitStack() as ctx:
            mixer(nc, ctx, d, w)
    with ExitStack() as ctx:
        ffn(nc, ctx, d)


def kernel(L0_attn_u, L0_attn_W_in, L0_attn_conv_w, L0_attn_conv_b, L0_attn_dt_bias, L0_attn_A_log, L0_attn_D,
           L0_attn_norm_w, L0_attn_W_out, L0_ffn_gate_up_packed, L0_ffn_gate_up_scales, L0_ffn_down_packed,
           L0_ffn_down_scales):
    import numpy as np
    import concourse.bacc as bacc
    from concourse.bass_utils import run_bass_kernel_spmd as run

    arr = np.asarray
    w_in = arr(L0_attn_W_in).T
    z, x, bm, cm, dt = np.split(w_in, np.cumsum([D_INNER, D_INNER, D_STATE, D_STATE]), axis=1)
    w_in = np.concatenate([bm, cm] + [dt] * 4 + [bm, x, z], axis=1)

    def conv_rows(a):
        x, bm, cm = np.split(a, np.cumsum([D_INNER, D_STATE]), axis=0)
        return np.concatenate([bm, cm, bm, bm, x], axis=0)

    conv_w = conv_rows(arr(L0_attn_conv_w)).reshape(NCONV, P, 4).transpose(1, 0, 2)
    conv_b = conv_rows(arr(L0_attn_conv_b)).reshape(NCONV, P).T
    heads = lambda a, copies: np.concatenate([arr(a)] * copies).reshape(-1, 1)
    d_skip = np.repeat(arr(L0_attn_D), HEADDIM).reshape(JT, P).T
    norm_w = arr(L0_attn_norm_w).reshape(JT, P).T

    row = np.arange(P)
    order = np.concatenate([8 * (64 * (g // 4) + row % 64) + 2 * (g % 4) + row // 64 if g < GL else
                            P * g + 8 * (row % 16) + row // 16 for g in range(GT)])

    def ffn_cols(a):
        a = a.reshape(a.shape[0], 2, I_FFN)[:, :, order].reshape(a.shape[0], 2, GT, P)
        return a.transpose(0, 2, 1, 3).reshape(a.shape[0], 2 * I_FFN)

    gu_packed = ffn_cols(arr(L0_ffn_gate_up_packed).T)
    gu_scale = ffn_cols(arr(L0_ffn_gate_up_scales))
    gu_scale = np.concatenate([np.repeat(gu_scale, 16, axis=0)] * 2, axis=0)
    dn_packed = arr(L0_ffn_down_packed).T
    dn = arr(L0_ffn_down_scales)
    dn_scale = np.stack([np.concatenate([np.repeat(dn[4 * q:4 * q + 4], 16, axis=0)] * 2) for q in range(2)] +
                        [np.repeat(dn[g:g + 1], P, axis=0) for g in range(GL, GT)], axis=1)

    delta = np.zeros((32, HEADS, CHUNK), np.float32)
    delta[np.arange(32), np.arange(32) % HEADS] = 1.0
    keep = np.ones((HALF, T), np.float32)
    keep[:, ::CHUNK] = 0.0
    part = np.zeros((HALF, 2), np.float32)
    part[np.arange(HALF), np.arange(HALF) // HEADS % 2] = 1.0
    mask = np.full((CHUNK, CHUNK), -1e30, np.float32)
    mask = np.repeat(np.tril(mask, -1)[:, None, :], HEADS, axis=1)
    inputs = {
        "u": arr(L0_attn_u).reshape(L, D_MODEL), "w_in": w_in, "w_out": arr(L0_attn_W_out).T, "conv_w": conv_w,
        "conv_b": conv_b, "dt_bias": heads(L0_attn_dt_bias, 4), "A_log": heads(L0_attn_A_log, 8), "D": d_skip,
        "norm_w": norm_w, "gu_packed": gu_packed, "gu_scale": gu_scale, "dn_packed": dn_packed,
        "dn_scale": dn_scale, "gu_scale_flat": arr(L0_ffn_gate_up_scales).reshape(P, P_SC), "ident": np.eye(P, dtype=np.float32),
        "mask": mask, "delta": delta, "keep": keep, "part": part,
        "shift": (4 * (np.arange(P) // 16)).astype(np.int32).reshape(P, 1),
    }
    inputs = {k: np.ascontiguousarray(v) for k, v in inputs.items()}
    nc = bacc.Bacc("TRN2", target_bir_lowering=False, num_devices=1)
    d = {k: nc.dram_tensor(f"in_{k}", v.shape, mybir.dt.from_np(v.dtype), kind="ExternalInput").ap()
         for k, v in inputs.items()}
    d["x1"] = nc.dram_tensor("x1_scratch", [L, D_MODEL], FP32, kind="Internal").ap()
    d["out"] = nc.dram_tensor("out_0", [L, D_MODEL], FP32, kind="ExternalOutput").ap()
    build(nc, d)
    r = run(nc, [{f"in_{k}": v for k, v in inputs.items()}], core_ids=[0])
    return r.results[0]["out_0"].reshape(1, L, D_MODEL)
```

```python
import concourse.bass as bass
from concourse import mybir
from contextlib import ExitStack

FP32 = mybir.dt.float32
BF16 = mybir.dt.bfloat16
FP32R = mybir.dt.float32r
FP16 = mybir.dt.float16
FP8 = mybir.dt.float8e4
I32 = mybir.dt.int32
U32 = mybir.dt.uint32
ALU = mybir.AluOpType
ACT = mybir.ActivationFunctionType

P = 128
L = 2048
D_MODEL = 512
D_INNER = 1024
D_STATE = 64
HEADDIM = 64
HEADS = D_INNER // HEADDIM
CHUNK = 64
I_FFN = 1408
KD = D_MODEL // P
JT = D_INNER // P
GT = I_FFN // P
LN_EPS = 1e-5
MIX_EPS = 1e-5
FFN_EPS = 1e-6

T = 256
NB = L // T
NT = T // P
NC = T // CHUNK
NCONV = JT + 2
DTB = 1
NPROJ = NCONV + JT
PROJ = NPROJ * P
IN_CHUNK = [[0, 1, 2], [3, 4, 10], [5, 6, 11], [7, 8, 12]]
IN_TAIL = [9, 13, 14, 15, 16, 17]
LATE = [2, 4, 6, 8]
SEQ = [k for tiles in IN_CHUNK for k in tiles] + IN_TAIL
POS = {k: i for i, k in enumerate(SEQ)}
X_SCALE = 2048.0
Y_SCALE = 1024.0
EXPONENT = 0x7F800000
RSQRT_MAGIC = 1597463007.0
HALF = 64

TF = 512
NBF = L // TF
NTF = TF // P
GC = 2 * P

P_SC = KD * 2 * I_FFN // P
NLINK = 13
NCHAIN = NLINK + 2 * NCONV + 8
AHEAD = NCHAIN + NLINK


def weights(nc, ctx, outer, d):
    def keep(name, shape, dt=FP32):
        return outer.enter_context(nc.sbuf_tensor(name, shape, dt))

    def sb(name, shape, dt=FP32):
        return ctx.enter_context(nc.sbuf_tensor(name, shape, dt))

    def sem(name):
        return ctx.enter_context(nc.semaphore(name))

    w = {
        "in_h": keep("w_in_h", [P, KD, PROJ], FP16), "in_l": keep("w_in_l", [P, KD, PROJ], FP16),
        "out_h": keep("w_out_h", [P, JT, D_MODEL], FP16), "out_l": keep("w_out_l", [P, JT, D_MODEL], FP16),
        "unscale": keep("unscale", [P, 4]),
        "conv_w": keep("conv_w", [P, NCONV, 4]), "conv_b": keep("conv_b", [P, NCONV]),
        "a_exp": keep("a_exp", [P, 1]),
        "dt_bias": keep("dt_bias", [HALF, 1]), "d_skip": keep("d_skip", [P, JT]), "ident": keep("ident", [P, P]),
        "delta": keep("delta", [32, HEADS, CHUNK]), "keep": keep("keep", [HALF, T]),
        "part": keep("part", [HALF, 2]),
        "ones": keep("ones", [P, P]), "seg_r": keep("seg_r", [P, 2, HEADS, CHUNK], FP32R),
        "seg_l": keep("seg_l", [P, 2, NC, P], FP32R), "bI": keep("bI", [P, 2, NC, D_STATE]),
        "xin": keep("xin", [P, NT, D_MODEL]), "raw": keep("raw", [P, NCONV, 3 + T]),
        "var": keep("var", [P, 2 * NT]),
        "decay": keep("decay", [P, 2, HEADS, CHUNK]), "xs": keep("xs", [P, NC, HEADS, HEADDIM]),
    }
    ident, ones, seg_r, seg_l, decay = (w[k] for k in ("ident", "ones", "seg_r", "seg_l", "decay"))
    fin = sb("w_in_f", [P, KD, PROJ])
    fout = sb("w_out_f", [P, JT, D_MODEL])
    norm_w = sb("norm_w", [P, JT])
    junk = sb("w_junk", [P, PROJ], BF16)
    l1 = sb("w_l1", [P, KD + JT])
    lmax = sb("w_lmax", [P, 2])
    lall = sb("w_lall", [P, 2])
    pow2 = sb("w_pow2", [P, 2], I32)
    rp = sb("w_rp", [P, 2])
    sc = sb("w_scale", [P, 2])
    s_const = sem("exponent_constants_loaded")
    s_init = sem("buffers_cleared")
    s_rest = sem("mixer_start_loaded")
    s_c = sem("w_small_loaded")
    s_i = [sem(f"w_in_loaded{k}") for k in range(KD)]
    s_o = sem("w_out_loaded")
    s_on = sem("w_out_weighted")
    s_l1 = sem("w_l1_ready")
    s_lm = sem("w_max_ready")
    s_all = sem("w_max_of_all")
    s_ch = sem("w_scale_steps")
    s_sc = sem("w_scales_ready")
    s_hi = sem("w_hi_split")
    s_lo = sem("w_lo_split")
    block = ctx.enter_context(nc.Block())

    @block.sync
    def _(sp):
        for dst, src in ((decay[HALF:P, 0], "mask"), (decay[32:HALF, 0], "delta"), (ident[:], "ident")):
            sp.dma_start(dst, d[src]).then_inc(s_const, 16)
        for k in range(KD):
            sp.dma_start(fin[:, k, :], d["w_in"][k * P:(k + 1) * P, :]).then_inc(s_i[k], 16)
        for dst, src in ((w["conv_w"], "conv_w"), (w["conv_b"], "conv_b"), (w["a_exp"], "A_log"), (norm_w, "norm_w")):
            sp.dma_start(dst[:], d[src]).then_inc(s_c, 16)
        sp.dma_start(fout[:], d["w_out"].rearrange("(j p) o -> p j o", p=P)).then_inc(s_o, 16)
        sp.dma_start(w["xin"][:], d["u"][0:T, :].rearrange("(t p) d -> p t d", p=P)).then_inc(s_rest, 16)
        for name, src in (("delta", "delta"), ("keep", "keep"), ("part", "part"), ("dt_bias", "dt_bias"),
                          ("d_skip", "D")):
            sp.dma_start(w[name][:], d[src]).then_inc(s_rest, 16)
        sp.wait_ge(s_rest, 16 * 6)

    @block.scalar
    def _(act):
        act.wait_ge(s_c, 64)
        act.activation(w["a_exp"][:], w["a_exp"][:], ACT.Exp)
        for k in range(KD):
            act.wait_ge(s_i[k], 16)
            if k:
                act.wait_ge(s_l1, k)
            act.activation(junk[:], fin[:, k, :], ACT.Abs, accum_out=l1[:, k:k + 1]).then_inc(s_l1, 1)
        for j in range(JT):
            act.wait_ge(s_on, j + 1)
            act.wait_ge(s_l1, KD + j)
            act.activation(junk[:, 0:D_MODEL], fout[:, j, :], ACT.Abs, accum_out=l1[:, KD + j:KD + j + 1]).then_inc(s_l1, 1)
        act.wait_ge(s_sc, 1)
        for n in range(NPROJ // 2):
            c = slice(2 * n * P, 2 * (n + 1) * P)
            act.activation(w["in_h"][:, :, c], fin[:, :, c], ACT.Copy, scale=sc[:, 0:1]).then_inc(s_hi, 1)
        for j in range(JT):
            act.activation(w["out_h"][:, j, :], fout[:, j, :], ACT.Copy, scale=sc[:, 1:2]).then_inc(s_hi, 1)

    @block.gpsimd
    def _(pool):
        pool.wait_ge(s_lm, 2)
        pool.partition_all_reduce(lall[:], lmax[:], P, bass.bass_isa.ReduceOp.max).then_inc(s_all, 1)

    @block.vector
    def _(dve):
        n = [0]

        def link(ins):
            n[0] += 1
            ins.then_inc(s_ch, 1)
            dve.wait_ge(s_ch, n[0])

        dve.memset(w["raw"][:], 0.0).then_inc(s_init, 1)
        dve.memset(w["xs"][HALF:P, 0], 0.0).then_inc(s_init, 1)
        dve.memset(ones[:], 1.0).then_inc(s_init, 1)
        dve.memset(w["var"][:], 1.0).then_inc(s_init, 1)
        dve.memset(decay[:, 1], 0.0).then_inc(s_init, 1)
        dve.wait_ge(s_init, 5)
        dve.wait_ge(s_const, 16 * 3)
        for b in range(2):
            dve.tensor_copy(seg_r[HALF:P, b], decay[HALF:P, 0])
            dve.tensor_copy(seg_r[32:HALF, b], decay[32:HALF, 0])
            dve.tensor_copy(seg_l[0:32, b], ones[0:32, None, :].to_broadcast([32, NC, P]))
            dve.tensor_copy(seg_l[32:HALF, b, :, HALF:P], decay[32:HALF, 1, 0:NC, :])
            dve.tensor_copy(seg_l[HALF:P, b, :, HALF:P], decay[HALF:P, 1, 0:NC, :])
            dve.tensor_copy(seg_l[HALF:P, b, :, 0:HALF], ident[HALF:P, None, HALF:P].to_broadcast([HALF, NC, HALF]))
            dve.tensor_copy(w["bI"][HALF:P, b], ident[HALF:P, None, HALF:P].to_broadcast([HALF, NC, HALF]))
        dve.wait_ge(s_c, 16 * 4)
        dve.wait_ge(s_o, 16)
        for j in range(JT):
            dve.tensor_scalar(fout[:, j, :], fout[:, j, :], norm_w[:, j:j + 1], None, ALU.mult).then_inc(s_on, 1)
        dve.wait_ge(s_l1, KD + JT)
        dve.reduce_max(lmax[:, 0:1], l1[:, 0:KD], mybir.AxisListType.X).then_inc(s_lm, 1)
        dve.reduce_max(lmax[:, 1:2], l1[:, KD:], mybir.AxisListType.X).then_inc(s_lm, 1)
        dve.wait_ge(s_all, 1)
        link(dve.tensor_scalar(rp[:], lall[:], 2.0 ** -80, None, ALU.max))
        link(dve.tensor_scalar(pow2[:], rp[:].bitcast(I32), EXPONENT, 0, ALU.bitwise_and, ALU.logical_shift_left))
        link(dve.reciprocal(rp[:], pow2[:].bitcast(FP32)))
        dve.tensor_scalar(sc[:], rp[:], 2.0 ** 14, None, ALU.mult).then_inc(s_sc, 1)
        p2 = pow2[:].bitcast(FP32)
        dve.tensor_scalar(w["unscale"][:, 0:1], p2[:, 0:1], 2.0 ** -14 / X_SCALE, None, ALU.mult)
        dve.tensor_scalar(w["unscale"][:, 3:4], p2[:, 1:2], 2.0 ** -14 / Y_SCALE, None, ALU.mult)
        link(dve.tensor_scalar(w["unscale"][:, 1:2], p2[:, 0:1], 2.0 ** -15 / X_SCALE, None, ALU.mult))
        dve.tensor_scalar(w["conv_w"][:], w["conv_w"][:], w["unscale"][:, 1:2], None, ALU.mult)
        dve.tensor_scalar(w["conv_b"][:], w["conv_b"][:], 0.5, None, ALU.mult)
        dve.wait_ge(s_sc, 1)
        for n_ in range(NPROJ // 2):
            c = slice(2 * n_ * P, 2 * (n_ + 1) * P)
            dve.wait_ge(s_hi, n_ + 1)
            dve.scalar_tensor_tensor(w["in_l"][:, :, c], fin[:, :, c], sc[:, 0:1], w["in_h"][:, :, c], ALU.mult,
                                     ALU.subtract).then_inc(s_lo, 1)
        for j in range(JT):
            dve.wait_ge(s_hi, NPROJ // 2 + j + 1)
            dve.scalar_tensor_tensor(w["out_l"][:, j, :], fout[:, j, :], sc[:, 1:2], w["out_h"][:, j, :], ALU.mult,
                                     ALU.subtract).then_inc(s_lo, 1)
        dve.wait_ge(s_lo, NPROJ // 2 + JT)
    return w


def mixer(nc, ctx, d, w, early):
    def sb(name, shape, dt=FP32):
        return ctx.enter_context(nc.sbuf_tensor(name, shape, dt))

    def sem(name):
        return ctx.enter_context(nc.semaphore(name))

    def bank(name):
        return ctx.enter_context(nc.psum_tensor(name, [P, 512], FP32))

    conv_w, conv_b, unscale = w["conv_w"], w["conv_b"], w["unscale"]
    dt_bias, d_skip, ident, delta, keep, part, ones, seg_r, seg_l, bI, xin, raw, var, decay, xs = (
        w[k] for k in ("dt_bias", "d_skip", "ident", "delta", "keep", "part", "ones", "seg_r", "seg_l", "bI", "xin",
                       "raw", "var", "decay", "xs"))

    x1 = sb("x1", [P, NT, D_MODEL])
    xn = sb("xn", [P, NT, D_MODEL])
    xt_h = sb("m_xt_h", [P, KD, T], FP16)
    xt_l = sb("m_xt_l", [P, KD, T], FP16)
    stats = sb("stats", [P, NT, 6])
    mv = sb("mv", [P, NT, 2])
    rs = sb("rs", [P, 2 * NT])
    nw = sb("newton", [P, 2, 2 * NT])
    waited = sb("waited", [P, 1])
    acc = sb("acc", [P, 3, T])
    th = sb("th", [P, 2, T])
    tz = sb("tz", [P, 4, T])
    gate = sb("gate", [P, 2, JT, T])
    xT = sb("xT", [P, 2, JT, T])
    gc = sb("gc", [P, 2, T])
    bT = sb("bT", [P, T])
    dts = sb("dts", [HALF, 6, T])
    acum = sb("acum", [HALF, T])
    acum_h = sb("acum_h", [HALF, T], FP32R)
    acum_p = sb("acum_p", [HALF, 2, T])
    dtT = sb("dtT", [P, 2, NT, HEADS])
    mc = sb("mc", [P, HEADS, CHUNK])
    xsd = sb("xsd", [P, HEADS, HEADDIM])
    diag = sb("diag", [P, NT, P])
    ybuf = sb("ybuf", [P, NT, JT, P])
    y_h = [ybuf[:, t].rearrange("p j n -> p (j n)").bitcast(FP16)[:, 0:JT * P].rearrange("p (j n) -> p j n", j=JT)
           for t in range(NT)]
    y_l = [ybuf[:, t].rearrange("p j n -> p (j n)").bitcast(FP16)[:, JT * P:].rearrange("p (j n) -> p j n", j=JT)
           for t in range(NT)]

    pA = [bank("pA0"), bank("pA1")]
    pE = [bank("pE0"), bank("pE1")]
    pX, pS, pY, pM = bank("pX"), bank("pS"), bank("pY"), bank("pM")

    s_early = sem("ffn_start_loaded")
    s_xin = sem("x_loaded")
    s_xres = sem("residual_loaded")
    s_st = sem("ln_stats_ready")
    s_mv = sem("ln_mean_var_ready")
    s_rs = sem("rsqrt_ready")
    s_xn = sem("xn_ready")
    s_tp = sem("xt_in_psum")
    s_th = sem("xt_hi_ready")
    s_tl = sem("xt_lo_ready")
    s_proj = sem("proj_in_psum")
    s_free = sem("proj_bank_free")
    s_conv = sem("conv_ready")
    s_tanh = sem("conv_tanh_ready")
    s_silu = sem("conv_silu_ready")
    s_zt = sem("z_tanh_ready")
    s_z = sem("gate_ready")
    s_abs = sem("dt_abs_ready")
    s_exp = sem("dt_exp_ready")
    s_u = sem("dt_one_plus_ready")
    s_ln = sem("dt_ln_ready")
    s_acum = sem("acum_parts_ready")
    s_segl = sem("seg_lhs_ready")
    s_gp = sem("dt_B_G_in_psum")
    s_gc = sem("dt_B_G_ready")
    s_segr = sem("seg_rhs_ready")
    s_ep = sem("seg_in_psum")
    s_e = sem("decay_ready")
    s_xp = sem("x_chunks_in_psum")
    s_xs = sem("x_dt_ready")
    s_xd = sem("x_skip_ready")
    s_mc = sem("mc_ready")
    s_xsd = sem("xs_decayed_ready")
    s_yp = sem("y_in_psum")
    s_ya = sem("y_plus_skip_ready")
    s_y = sem("y_gated_ready")
    s_sq = sem("y_squares_ready")
    s_sum = sem("squares_added")
    s_sp = sem("state_in_psum")
    s_state = sem("state_ready")
    s_ssq = sem("square_sum_in_psum")
    s_ms = sem("mean_square_ready")
    s_diag = sem("rsqrt_diag_ready")
    s_rb = sem("rsqrt_rows_in_psum")
    s_yn = sem("y_normalised")
    s_yh = sem("y_hi_ready")
    s_yl = [sem("y0_lo_ready"), sem("y1_lo_ready")]
    s_op = sem("out_proj_in_psum")
    s_x1 = [sem("x1_ready0"), sem("x1_ready1")]
    s_x1out = sem("x1_stored")
    s_ch = sem("vector_chain")
    for s in (s_xin, s_xres, s_st, s_mv, s_rs, s_xn, s_tp, s_th, s_tl, s_proj, s_free, s_conv, s_tanh, s_silu, s_zt,
              s_z, s_abs, s_exp, s_u, s_ln, s_acum, s_segl, s_gp, s_gc, s_segr, s_ep, s_e, s_xp, s_xs, s_xd, s_mc,
              s_xsd, s_yp, s_ya, s_y, s_sq, s_sum, s_sp, s_state, s_ssq, s_ms, s_diag, s_rb, s_yn, s_yh, *s_yl, s_op, *s_x1,
              s_x1out, s_ch):
        nc.sync.sem_inc(s, 1)
    block = ctx.enter_context(nc.Block())

    def steps(eng, step):
        with eng.Fori(0, (NB - 2) // 2) as r:
            step(2 * r, 0, True, True)
            step(2 * r + 1, 1, True, True)
        step(NB - 2, 0, True, False)
        step(NB - 1, 1, False, False)

    @block.sync
    def _(sp):
        def load_x(b):
            sp.dma_start(xin[:], d["u"][bass.ds(b * T, T), :].rearrange("(t p) d -> p t d", p=P)).then_inc(s_xin, 16)

        sp.wait_ge(s_xn, 1 + NT)
        load_x(1)

        def load_early():
            sp.wait_ge(s_x1out, 1 + 16 * (TF // T))
            for dst, src in ((early["ident"][:], d["ident"]), (early["scales_flat"][:], d["gu_scale_flat"]),
                             (early["word"][0:HALF], d["gu_packed"][:, 0:2 * GC]),
                             (early["word"][HALF:P], d["gu_packed"][:, 0:2 * GC]),
                             (early["scale"][:], d["gu_scale"][:, 0:2 * GC]),
                             (early["x"][:], d["x1"][0:TF, :].rearrange("(t p) d -> p t d", p=P))):
                sp.dma_start(dst, src).then_inc(s_early, 16)

        def step(s, par, proj, norm):
            sp.wait_ge(s_x1out, 1 + s * 16)
            sp.dma_start(x1[:], d["u"][bass.ds(s * T, T), :].rearrange("(t p) d -> p t d", p=P)).then_inc(s_xres, 16)
            if norm:
                sp.wait_ge(s_xn, 1 + (s + 2) * NT)
                load_x(s + 2)
            sp.wait_ge(s_x1[0], 1 + s + 1)
            sp.wait_ge(s_x1[1], 1 + s + 1)
            sp.dma_start(d["x1"][bass.ds(s * T, T), :].rearrange("(t p) d -> p t d", p=P), x1[:]).then_inc(s_x1out, 16)
            if proj and not norm:
                load_early()
        steps(sp, step)
        sp.wait_ge(s_early, 16 * 6)
        sp.wait_ge(s_x1out, 1 + 16 * NB)

    @block.tensor
    def _(pe):
        def product(out, a_h, a_l, b_h, b_l, start, stop):
            nc.tensor.matmul(out, a_h, b_h, start=start, stop=False)
            nc.tensor.matmul(out, a_h, b_l, start=False, stop=False)
            return nc.tensor.matmul(out, a_l, b_h, start=False, stop=stop)

        def transposes(b, t):
            pe.wait_ge(s_gc, 1 + 3 * b)
            pe.wait_ge(s_xn, 1 + b * NT + t + 1)
            pe.wait_ge(s_tl, 1 + b * NT + t)
            for k in range(KD):
                last = nc.tensor.transpose(pM[:, k * P:(k + 1) * P], xn[:, t, k * P:(k + 1) * P], ident[:])
            last.then_inc(s_tp, 1)

        def tile(b, k, used=True):
            pos = POS[k]
            if pos == 0:
                pe.wait_ge(s_tl, 1 + b * NT + NT)
            if pos < 2 and used:
                pe.wait_ge(s_x1[pos], b)
            pe.wait_ge(s_free, 1 + b * NPROJ + max(pos - 1, 0))
            for kd in range(KD):
                c = slice(k * P, (k + 1) * P)
                last = product(pA[pos % 2][:, 0:T], w["in_h"][:, kd, c], w["in_l"][:, kd, c], xt_h[:, kd, :],
                               xt_l[:, kd, :], kd == 0, kd == KD - 1)
            last.then_inc(s_proj, 1)

        def dt_b_g(b, par):
            for t in range(NT):
                nc.tensor.transpose(pM[:, t * HALF:(t + 1) * HALF], dts[:, 4, t * P:(t + 1) * P], ident[0:HALF, 0:HALF])
            for c in range(NC):
                cs = slice(c * CHUNK, (c + 1) * CHUNK)
                nc.tensor.transpose(pY[0:CHUNK, T + c * CHUNK:T + (c + 1) * CHUNK], gc[0:HALF, par, cs],
                                    ident[0:HALF, 0:HALF])
            for c in range(NC):
                cs = slice(c * CHUNK, (c + 1) * CHUNK)
                last = nc.tensor.matmul(pY[0:CHUNK, cs], bT[HALF:P, cs], gc[HALF:P, par, cs], start=True, stop=True)
            last.then_inc(s_gp, 1)

        def wait_dt_b_g(b):
            pe.wait_ge(s_acum, 1 + b + 1)
            pe.wait_ge(s_silu, 1 + b * NCONV + 2)
            pe.wait_ge(s_ya, 1 + b * NC)
            pe.wait_ge(s_ms, 1 + b)

        def exponents(s, par, c):
            pe.wait_ge(s_segr, 1 + s * NC + c + 1)
            pe.wait_ge(s_segl, 1 + s + 1)
            pe.wait_ge(s_e, 1 + s * 2 * NC + 2 * c)
            for e in range(2):
                nc.tensor.matmul(pE[e][:, :], seg_l[:, par, c, :],
                                 seg_r[:, c % 2].rearrange("p h l -> p (h l)")[:, e * 512:(e + 1) * 512],
                                 start=True, stop=True).then_inc(s_ep, 1)

        def x_pair(s, par, pair, e):
            pe.wait_ge(s_silu, 1 + (s + 1) * NCONV)
            pe.wait_ge(s_xs, 1 + s * 2 * NC + 4 * pair + 2 * e)
            for j in range(4):
                last = nc.tensor.transpose(pX[:, j * P:(j + 1) * P], xT[:, par, 4 * e + j, pair * P:(pair + 1) * P],
                                           ident[:])
            last.then_inc(s_xp, 1)

        def scan_y(s, c):
            pe.wait_ge(s_mc, 1 + s * NC + c + 1)
            pe.wait_ge(s_xs, 1 + s * 2 * NC + 4 * (c // 2) + 4)
            pe.wait_ge(s_state, 1 + s * 2 * NC + 2 * c)
            pe.wait_ge(s_ya, 1 + s * NC + c)
            pe.wait_ge(s_gc, 1 + s * 3 + 3)
            for h in range(HEADS):
                last = nc.tensor.matmul(pY[(h % 2) * HALF:(h % 2) * HALF + HALF, (h // 2) * CHUNK:(h // 2 + 1) * CHUNK],
                                        xs[:, c, h, :], mc[:, h, :], start=True, stop=True)
            last.then_inc(s_yp, 1)

        def next_state(s, par, c, e):
            pe.wait_ge(s_xsd, 1 + s * NC + c + 1)
            pe.wait_ge(s_state, 1 + s * 2 * NC + 2 * c + e)
            nc.tensor.matmul(pS[HALF:P, :], bI[:, par, c, :],
                             xsd[:].rearrange("p h q -> p (h q)")[:, e * 512:(e + 1) * 512],
                             start=True, stop=True).then_inc(s_sp, 1)

        def square_sums(s, proj):
            pe.wait_ge(s_sum, 1 + 3 * NC * (s + 1))
            pe.wait_ge(s_tl, 1 + (s + (2 if proj else 1)) * NT)
            for t in range(NT):
                last = nc.tensor.matmul(pM[:, 256 + t:257 + t], ybuf[:, t, 0, :], ones[:, 0:1], start=True, stop=True)
            last.then_inc(s_ssq, 1)

        def rsqrt_rows(s, proj):
            if proj:
                pe.wait_ge(s_gc, 1 + (s + 2) * 3)
            pe.wait_ge(s_ms, 1 + s + 1)
            pe.wait_ge(s_diag, 1 + s * NT + NT)
            last = nc.tensor.matmul(pM[:, 0:T], ones[:], diag[:].rearrange("p t n -> p (t n)"), start=True, stop=True)
            last.then_inc(s_rb, 1)

        def out_proj(s, t, half):
            pe.wait_ge(s_yl[t], 1 + s + 1)
            pe.wait_ge(s_yh, 1 + s * NT + t + 1)
            for j in range(half * JT // 2, (half + 1) * JT // 2):
                last = product(pA[t][:, :], y_h[t][:, j, :], y_l[t][:, j, :], w["out_h"][:, j, :], w["out_l"][:, j, :],
                               j == 0, j == JT - 1)
            if half:
                last.then_inc(s_op, 1)

        def step(s, par, proj, norm):
            for c in range(NC):
                tiles = IN_CHUNK[c] if proj else []
                if c > 0:
                    scan_y(s, c)
                    if c == 2:
                        exponents(s, par, 3)
                    for k in tiles[0:1]:
                        tile(s + 1, k)
                    next_state(s, par, c, 0)
                    for k in tiles[1:2]:
                        tile(s + 1, k)
                    next_state(s, par, c, 1)
                for k in tiles[2 if c > 0 else 0:]:
                    tile(s + 1, k)
            if proj:
                tile(s + 1, IN_TAIL[0])
                tile(s + 1, IN_TAIL[1])
            square_sums(s, proj)
            if proj:
                wait_dt_b_g(s + 1)
                tile(s + 1, IN_TAIL[2])
                dt_b_g(s + 1, 1 - par)
                x_pair(s + 1, 1 - par, 0, 0)
            rsqrt_rows(s, proj)
            if proj:
                tile(s + 1, IN_TAIL[3])
                exponents(s + 1, 1 - par, 0)
                tile(s + 1, IN_TAIL[4])
                x_pair(s + 1, 1 - par, 0, 1)
                tile(s + 1, IN_TAIL[5])
                pe.wait_ge(s_free, 1 + (s + 2) * NPROJ)
            else:
                pe.wait_ge(s_x1[0], 1 + s)
                pe.wait_ge(s_x1[1], 1 + s)
            out_proj(s, 0, 0)
            if proj:
                x_pair(s + 1, 1 - par, 1, 0)
                scan_y(s + 1, 0)
                exponents(s + 1, 1 - par, 1)
            out_proj(s, 0, 1)
            if proj:
                x_pair(s + 1, 1 - par, 1, 1)
            if norm:
                transposes(s + 2, 0)
            if proj:
                next_state(s + 1, 1 - par, 0, 0)
            out_proj(s, 1, 0)
            if proj:
                next_state(s + 1, 1 - par, 0, 1)
            if norm:
                transposes(s + 2, 1)
            out_proj(s, 1, 1)
            if proj:
                exponents(s + 1, 1 - par, 2)

        for t in range(NT):
            transposes(0, t)
        for k in SEQ[:-1]:
            tile(0, k, used=False)
        wait_dt_b_g(0)
        tile(0, SEQ[-1])
        dt_b_g(0, 0)
        exponents(0, 0, 0)
        x_pair(0, 0, 0, 0)
        x_pair(0, 0, 0, 1)
        x_pair(0, 0, 1, 0)
        scan_y(0, 0)
        exponents(0, 0, 1)
        x_pair(0, 0, 1, 1)
        transposes(1, 0)
        next_state(0, 0, 0, 0)
        next_state(0, 0, 0, 1)
        transposes(1, 1)
        exponents(0, 0, 2)
        steps(pe, step)

    @block.scalar
    def _(act):
        def xt_hi(b, t):
            act.wait_ge(s_tp, 1 + b * NT + t + 1)
            act.activation(xt_h[:, :, t * P:(t + 1) * P], pM[:, :].rearrange("p (k n) -> p k n", k=KD),
                           ACT.Copy).then_inc(s_th, 1)

        def conv_in(b, m):
            lo = HALF if m == DTB else 0
            full = pA[POS[m] % 2]
            src = full[lo:P, 0:T]
            act.wait_ge(s_proj, 1 + b * NPROJ + POS[m] + 1)
            act.wait_ge(s_silu, 1 + b * NCONV + max(m - 2, 0))
            act.activation(acc[lo:P, m % 3, :], src, ACT.Identity, bias=conv_b[lo:P, m:m + 1], scale=conv_w[lo:P, m, 3:4])
            if m == DTB:
                act.activation(dts[:, 0, :], full[0:HALF, 0:T], ACT.Identity, bias=dt_bias[:],
                               scale=unscale[0:HALF, 0:1])
            act.activation(raw[lo:P, m, 3:3 + T], src, ACT.Copy).then_inc(s_free, 1)

        def conv_tanh(b, m):
            lo = HALF if m == DTB else 0
            act.wait_ge(s_conv, 1 + b * NCONV + m + 1)
            act.wait_ge(s_silu, 1 + b * NCONV + max(m - 1, 0))
            act.activation(th[lo:P, m % 2, :], acc[lo:P, m % 3, :], ACT.Tanh).then_inc(s_tanh, 1)

        def softplus_exp(b):
            act.wait_ge(s_free, 1 + b * NPROJ + POS[DTB] + 1)
            act.activation(dts[:, 1, :], dts[:, 0, :], ACT.Abs).then_inc(s_abs, 1)
            act.wait_ge(s_abs, 1 + b + 1)
            act.activation(dts[:, 2, :], dts[:, 1, :], ACT.Exp, scale=-1.0).then_inc(s_exp, 1)

        def softplus_log(b):
            act.wait_ge(s_u, 1 + b + 1)
            act.activation(dts[:, 5, :], dts[:, 3, :], ACT.Ln).then_inc(s_ln, 1)

        def gate_in(b, par, j):
            pos = POS[NCONV + j]
            act.wait_ge(s_proj, 1 + b * NPROJ + pos + 1)
            act.activation(gate[:, par, j, :], pA[pos % 2][:, 0:T], ACT.Copy, scale=unscale[:, 1:2])
            act.wait_ge(s_z, 1 + b * JT + max(j - 3, 0))
            act.activation(tz[:, j % 4, :], pA[pos % 2][:, 0:T], ACT.Tanh, scale=unscale[:, 1:2]).then_inc(s_free, 1)

        def decays(s, c):
            act.wait_ge(s_xsd, 1 + s * NC + max(c - 1, 0))
            for e in range(2):
                act.wait_ge(s_ep, 1 + s * 2 * NC + 2 * c + e + 1)
                act.activation(decay[:, c % 2, 8 * e:8 * e + 8, :].rearrange("p h l -> p (h l)"), pE[e][:, :],
                               ACT.Exp).then_inc(s_e, 1)

        def state(s, c, e):
            act.wait_ge(s_sp, 1 + s * 2 * NC + 2 * c + e + 1)
            act.activation(xs[HALF:P, (c + 1) % NC, 8 * e:8 * e + 8, :].rearrange("p h q -> p (h q)"), pS[HALF:P, :],
                           ACT.Copy).then_inc(s_state, 1)

        def squares(s, par, c):
            act.wait_ge(s_y, 1 + s * NC + c + 1)
            act.wait_ge(s_op, 1 + s * NT)
            act.activation(ybuf[:, c // 2, :, (c % 2) * CHUNK:(c % 2 + 1) * CHUNK],
                           xT[:, par, :, c * CHUNK:(c + 1) * CHUNK], ACT.Square).then_inc(s_sq, 1)

        def step(s, par, proj, norm):
            for c in range(NC):
                tiles = IN_CHUNK[c] if proj else []
                conv_tiles = [k for k in tiles if k < NCONV]
                if c == 2:
                    decays(s, 3)
                for m in conv_tiles[0:1]:
                    conv_in(s + 1, m)
                if c > 0:
                    state(s, c, 0)
                if proj and c > 0:
                    conv_tanh(s + 1, LATE[c - 1])
                for m in conv_tiles[1:2]:
                    conv_in(s + 1, m)
                if c > 0:
                    state(s, c, 1)
                    squares(s, par, c - 1)
                for m in conv_tiles[0:1]:
                    conv_tanh(s + 1, m)
                if proj and c == 0:
                    conv_tanh(s + 1, conv_tiles[1])
                    softplus_exp(s + 1)
                for m in conv_tiles[2:]:
                    conv_in(s + 1, m)
                if proj and c == 0:
                    softplus_log(s + 1)
                for k in tiles[len(conv_tiles):]:
                    gate_in(s + 1, 1 - par, k - NCONV)
            squares(s, par, NC - 1)
            if proj:
                conv_tanh(s + 1, LATE[-1])
                conv_in(s + 1, IN_TAIL[0])
                conv_tanh(s + 1, IN_TAIL[0])
                for k in IN_TAIL[1:-2]:
                    gate_in(s + 1, 1 - par, k - NCONV)
            for t in range(NT):
                act.wait_ge(s_yn, 1 + s * NT + t + 1)
                act.activation(y_h[t], xT[:, par, :, t * P:(t + 1) * P], ACT.Copy).then_inc(s_yh, 1)
                if proj:
                    gate_in(s + 1, 1 - par, JT - 2 + t)
            if proj:
                decays(s + 1, 0)
                decays(s + 1, 1)
            if norm:
                xt_hi(s + 2, 0)
            if proj:
                state(s + 1, 0, 0)
                state(s + 1, 0, 1)
            if norm:
                xt_hi(s + 2, 1)
            if proj:
                decays(s + 1, 2)

        for t in range(NT):
            xt_hi(0, t)
        for i, k in enumerate(SEQ):
            if k < NCONV:
                conv_in(0, k)
            else:
                gate_in(0, 0, k - NCONV)
            if i and SEQ[i - 1] < NCONV:
                conv_tanh(0, SEQ[i - 1])
            if i == 2:
                softplus_exp(0)
            if i == 4:
                softplus_log(0)
        decays(0, 0)
        decays(0, 1)
        xt_hi(1, 0)
        state(0, 0, 0)
        state(0, 0, 1)
        xt_hi(1, 1)
        decays(0, 2)
        steps(act, step)

    @block.gpsimd
    def _(pool):
        def seg_rhs(s, par, c):
            cs = slice(c * CHUNK, (c + 1) * CHUNK)
            pool.wait_ge(s_acum, 1 + s + 1)
            pool.wait_ge(s_ep, 1 + s * 2 * NC + 2 * max(c - 1, 0))
            pool.tensor_tensor(seg_r[0:32, c % 2], delta[:],
                               acum_p[0:32, par, None, cs].to_broadcast([32, HEADS, CHUNK]),
                               ALU.mult).then_inc(s_segr, 1)
            pool.wait_ge(s_segr, 1 + s * NC + c + 1)

        def skip(s, par, c):
            cs = slice(c * CHUNK, (c + 1) * CHUNK)
            pool.wait_ge(s_xp, 1 + s * NC + 2 * (c // 2) + 2)
            pool.tensor_tensor(xT[:, par, :, cs], xT[:, par, :, cs], d_skip[:, :, None].to_broadcast([P, JT, CHUNK]),
                               ALU.mult).then_inc(s_xd, 1)
            pool.wait_ge(s_xd, 1 + s * NC + c + 1)

        def gated(s, par, c):
            cs = slice(c * CHUNK, (c + 1) * CHUNK)
            pool.wait_ge(s_ya, 1 + s * NC + c + 1)
            pool.wait_ge(s_z, 1 + (s + 1) * JT)
            pool.tensor_tensor(xT[:, par, :, cs], xT[:, par, :, cs], gate[:, par, :, cs], ALU.mult).then_inc(s_y, 1)
            pool.wait_ge(s_y, 1 + s * NC + c + 1)

        def normalise(b):
            pool.wait_ge(s_tp, 1 + b * NT)
            pool.wait_ge(s_rs, 1 + b + 1)
            pool.tensor_tensor(waited[:], mv[:, 0, 0:1], mv[:, 1, 0:1], ALU.add)
            for t in range(NT):
                pool.tensor_scalar(xn[:, t, :], xin[:, t, :], mv[:, t, 0:1], rs[:, NT + t:NT + t + 1],
                                   ALU.subtract, ALU.mult).then_inc(s_xn, 1)

        def sum_squares(s, c):
            pool.wait_ge(s_sq, 1 + s * NC + c + 1)
            q = ybuf[:, c // 2, :, (c % 2) * CHUNK:(c % 2 + 1) * CHUNK]
            for i, m in enumerate((4, 2, 1)):
                pool.tensor_tensor(q[:, 0:m], q[:, 0:m], q[:, m:2 * m], ALU.add).then_inc(s_sum, 1)
                pool.wait_ge(s_sum, 1 + 3 * (s * NC + c) + i + 1)

        def step(s, par, proj, norm):
            for c in range(NC):
                if c == 0:
                    skip(s, par, 0)
                if c + 2 < NC:
                    seg_rhs(s, par, c + 2)
                gated(s, par, c)
                if c + 1 < NC:
                    skip(s, par, c + 1)
                if c > 0:
                    sum_squares(s, c - 1)
            sum_squares(s, NC - 1)
            if proj:
                seg_rhs(s + 1, 1 - par, 0)
                seg_rhs(s + 1, 1 - par, 1)
            if norm:
                normalise(s + 2)
            pool.wait_ge(s_yh, 1 + s * NT + 2)
            pool.tensor_tensor(y_l[1], xT[:, par, :, P:2 * P], y_h[1], ALU.subtract).then_inc(s_yl[1], 1)

        seg_rhs(0, 0, 0)
        seg_rhs(0, 0, 1)
        normalise(1)
        steps(pool, step)

    @block.vector
    def _(dve):
        links = [0, 0]

        def link(ins):
            links[1] += 1
            ins.then_inc(s_ch, 1)
            dve.wait_ge(s_ch, 1 + links[0] + links[1])

        def ln_stats(b):
            dve.wait_ge(s_xin, 1 + b * 16)
            for t in range(NT):
                last = dve.bn_stats(stats[:, t, :], xin[:, t, :])
            last.then_inc(s_st, 1)
            dve.wait_ge(s_st, 1 + b + 1)
            dve.wait_ge(s_xn, 1 + b * NT)
            dve.tensor_copy(nw[:, 0, 0:1], stats[:, 0, 0:1])
            for t in range(NT):
                last = dve.bn_aggr(mv[:, t, :], stats[:, t, :])
            last.then_inc(s_mv, 1)
            dve.wait_ge(s_mv, 1 + 2 * b + 1)
            dve.tensor_scalar(var[:, NT:2 * NT], mv[:, :, 1], X_SCALE ** -2, LN_EPS * X_SCALE ** -2, ALU.mult,
                              ALU.add).then_inc(s_mv, 1)
            dve.wait_ge(s_mv, 1 + 2 * b + 2)

        def rsqrt(n):
            a, b = nw[:, 0], nw[:, 1]
            link(dve.tensor_scalar(a.bitcast(I32), var[:].bitcast(I32), 1, 0, ALU.logical_shift_right,
                                   ALU.logical_shift_left))
            link(dve.tensor_scalar(rs[:].bitcast(I32), a.bitcast(I32), -1.0, RSQRT_MAGIC, ALU.mult, ALU.add))
            for i in range(4):
                link(dve.tensor_tensor(a, rs[:], rs[:], ALU.mult))
                link(dve.scalar_tensor_tensor(b, a, -0.5, var[:], ALU.mult, ALU.mult))
                ins = dve.scalar_tensor_tensor(rs[:], b, 1.5, rs[:], ALU.add, ALU.mult)
                if i < 3:
                    link(ins)
            ins.then_inc(s_rs, 1)
            dve.wait_ge(s_rs, 1 + n + 1)

        def xt_lo(b, t):
            dve.wait_ge(s_th, 1 + b * NT + t + 1)
            dve.tensor_tensor(xt_l[:, :, t * P:(t + 1) * P], pM[:, :].rearrange("p (k n) -> p k n", k=KD),
                              xt_h[:, :, t * P:(t + 1) * P], ALU.subtract).then_inc(s_tl, 1)

        def convs(b, tiles):
            written = {}
            for k in range(3):
                for m in tiles:
                    lo = HALF if m == DTB else 0
                    if k == 0:
                        dve.wait_ge(s_free, 1 + b * NPROJ + POS[m] + 1)
                    else:
                        dve.wait_ge(s_ch, 1 + links[0] + written[m])
                    ins = dve.scalar_tensor_tensor(acc[lo:P, m % 3, :], raw[lo:P, m, k:k + T], conv_w[lo:P, m, k:k + 1],
                                                   acc[lo:P, m % 3, :], ALU.mult, ALU.add)
                    if k < 2:
                        links[1] += 1
                        written[m] = links[1]
                        ins.then_inc(s_ch, 1)
                    else:
                        ins.then_inc(s_conv, 1)

        def silu(b, par, m):
            lo = HALF if m == DTB else 0
            dst = gc[:, par, :] if m == 0 else bT[HALF:P, :] if m == DTB else xT[:, par, m - 2, :]
            dve.wait_ge(s_tanh, 1 + b * NCONV + m + 1)
            dve.tensor_copy(raw[lo:P, m, 0:3], raw[lo:P, m, T:T + 3])
            dve.scalar_tensor_tensor(dst, th[lo:P, m % 2, :], 1.0, acc[lo:P, m % 3, :], ALU.add,
                                     ALU.mult).then_inc(s_silu, 1)

        def gates(b, par, j):
            dve.wait_ge(s_free, 1 + b * NPROJ + POS[NCONV + j] + 1)
            dve.scalar_tensor_tensor(gate[:, par, j, :], tz[:, j % 4, :], 1.0, gate[:, par, j, :], ALU.add,
                                     ALU.mult).then_inc(s_z, 1)

        def one_plus(b):
            dve.wait_ge(s_exp, 1 + b + 1)
            dve.tensor_scalar(dts[:, 3, :], dts[:, 2, :], 1.0, None, ALU.add).then_inc(s_u, 1)

        def dt_parts(b, par):
            dve.wait_ge(s_u, 1 + b + 1)
            link(dve.scalar_tensor_tensor(dts[:, 1, :], dts[:, 3, :], -1.0, dts[:, 2, :], ALU.add, ALU.subtract))
            dve.wait_ge(s_ln, 1 + b + 1)
            link(dve.tensor_tensor(dts[:, 5, :], dts[:, 5, :], dts[:, 1, :], ALU.subtract))
            link(dve.scalar_tensor_tensor(dts[:, 4, :], dts[:, 0, :], 0.0, dts[:, 5, :], ALU.max, ALU.add))
            link(dve.tensor_scalar(dts[:, 2, :], dts[:, 4, :], w["a_exp"][0:HALF], -1.0, ALU.mult, ALU.mult))
            link(dve.tensor_tensor_scan(acum[:], keep[:], dts[:, 2, :], 0.0, ALU.mult, ALU.add))
            link(dve.tensor_copy(acum_h[:], acum[:]))
            high = acum_h[:].bitcast(FP32)
            link(dve.tensor_tensor(dts[:, 1, :], acum[:], high, ALU.subtract))
            link(dve.tensor_scalar(dts[:, 3, :], dts[:, 1, :], part[:, 1:2], None, ALU.mult))
            dve.scalar_tensor_tensor(acum_p[:, par, :], high, part[:, 0:1], dts[:, 3, :], ALU.mult,
                                     ALU.add).then_inc(s_acum, 1)
            dve.wait_ge(s_acum, 1 + b + 1)
            dve.tensor_scalar(seg_l[32:HALF, par, :, 0:CHUNK],
                              acum_p[32:HALF, par, :].rearrange("p (c s) -> p c s", c=NC), -1.0, None,
                              ALU.mult).then_inc(s_segl, 1)

        def dt_b_g(b, par):
            dve.wait_ge(s_gp, 1 + b + 1)
            dve.tensor_copy(dtT[:, par], pM[:, 0:NT * HALF].rearrange("p (t r) -> p t r", t=NT)[:, :, 0:HEADS]
                            ).then_inc(s_gc, 1)
            dve.tensor_copy(gc[0:HALF, par, :], pY[0:HALF, 0:T]).then_inc(s_gc, 1)
            dve.tensor_copy(bI[0:CHUNK, par, :, :], pY[0:CHUNK, T:2 * T].rearrange("p (c n) -> p c n", c=NC)
                            ).then_inc(s_gc, 1)

        def x_dt(s, par, pair, e):
            dve.wait_ge(s_xp, 1 + s * NC + 2 * pair + e + 1)
            dve.wait_ge(s_yp, 1 + s * NC)
            dve.wait_ge(s_gc, 1 + s * 3 + 3)
            for b in range(2):
                rows = slice(b * HALF, b * HALF + HALF)
                dve.tensor_tensor(xs[0:HALF, 2 * pair + b, 8 * e:8 * e + 8, :],
                                  pX[rows, :].rearrange("p (h q) -> p h q", h=8),
                                  dtT[rows, par, pair, 8 * e:8 * e + 8, None].to_broadcast([HALF, 8, HEADDIM]),
                                  ALU.mult).then_inc(s_xs, 1)

        def mix(s, par, c):
            dve.wait_ge(s_e, 1 + s * 2 * NC + 2 * c + 2)
            dve.wait_ge(s_yp, 1 + s * NC + c)
            dve.wait_ge(s_gc, 1 + s * 3 + 3)
            dve.tensor_tensor(mc[:], decay[:, c % 2],
                              gc[:, par, None, c * CHUNK:(c + 1) * CHUNK].to_broadcast([P, HEADS, CHUNK]),
                              ALU.mult).then_inc(s_mc, 1)

        def decayed(s, c):
            dve.wait_ge(s_state, 1 + s * 2 * NC + 2 * c)
            dve.wait_ge(s_xs, 1 + s * 2 * NC + 4 * (c // 2) + 4)
            dve.wait_ge(s_sp, 1 + s * 2 * NC + 2 * c)
            dve.tensor_tensor(xsd[:], xs[:, c], decay[:, c % 2, :, CHUNK - 1:CHUNK].to_broadcast([P, HEADS, HEADDIM]),
                              ALU.mult).then_inc(s_xsd, 1)

        def add_skip(s, par, c):
            cs = slice(c * CHUNK, (c + 1) * CHUNK)
            dve.wait_ge(s_yp, 1 + s * NC + c + 1)
            dve.wait_ge(s_xd, 1 + s * NC + c + 1)
            dve.tensor_tensor(xT[:, par, :, cs], pY[:, :].rearrange("p (j l) -> p j l", j=JT), xT[:, par, :, cs],
                              ALU.add).then_inc(s_ya, 1)

        def x1_tile(s, t):
            dve.wait_ge(s_op, 1 + s * NT + t + 1)
            dve.scalar_tensor_tensor(x1[:, t, :], pA[t][:, :], unscale[:, 3:4], x1[:, t, :], ALU.mult,
                                     ALU.add).then_inc(s_x1[t], 1)

        def step(s, par, proj, norm):
            links[0], links[1] = AHEAD + s * NCHAIN, 0
            for c in range(NC):
                early = [k for k in IN_CHUNK[c] if k < LATE[c]] if proj else []
                if c > 1:
                    decayed(s, c)
                if c > 1 and proj:
                    silu(s + 1, 1 - par, LATE[c - 1] - 1)
                    gates(s + 1, 1 - par, c - 2)
                if c > 0 and proj:
                    convs(s + 1, LATE[c - 1:c])
                if c > 0:
                    add_skip(s, par, c)
                if 0 < c < NC - 1:
                    mix(s, par, c + 1)
                if c > 0 and proj:
                    silu(s + 1, 1 - par, LATE[c - 1])
                convs(s + 1, early)
                if proj and c == 0:
                    for m in early:
                        silu(s + 1, 1 - par, m)
                    one_plus(s + 1)
                if proj and c == 1:
                    dt_parts(s + 1, 1 - par)
            if proj:
                silu(s + 1, 1 - par, LATE[-1] - 1)
                gates(s + 1, 1 - par, 2)
                convs(s + 1, LATE[-1:])
            if norm:
                ln_stats(s + 2)
            if proj:
                silu(s + 1, 1 - par, LATE[-1])
                convs(s + 1, IN_TAIL[0:1])
            dve.wait_ge(s_ssq, 1 + s + 1)
            dve.tensor_scalar(var[:, 0:NT], pM[:, 256:256 + NT], 1.0 / D_INNER, MIX_EPS, ALU.mult,
                              ALU.add).then_inc(s_ms, 1)
            dve.wait_ge(s_ms, 1 + s + 1)
            if proj:
                silu(s + 1, 1 - par, IN_TAIL[0])
            rsqrt(s + 2)
            for t in range(NT):
                dve.tensor_scalar(diag[:, t, :], ident[:], rs[:, t:t + 1], Y_SCALE, ALU.mult, ALU.mult
                                  ).then_inc(s_diag, 1)
            if proj:
                gates(s + 1, 1 - par, 3)
                dt_b_g(s + 1, 1 - par)
                gates(s + 1, 1 - par, 4)
                x_dt(s + 1, 1 - par, 0, 0)
            dve.wait_ge(s_rb, 1 + s + 1)
            for t in range(NT):
                ts = slice(t * P, (t + 1) * P)
                dve.tensor_tensor(xT[:, par, :, ts], xT[:, par, :, ts], pM[:, None, ts].to_broadcast([P, JT, P]),
                                  ALU.mult).then_inc(s_yn, 1)
            dve.wait_ge(s_yh, 1 + s * NT + 1)
            dve.tensor_tensor(y_l[0], xT[:, par, :, 0:P], y_h[0], ALU.subtract).then_inc(s_yl[0], 1)
            if proj:
                gates(s + 1, 1 - par, 5)
                x_dt(s + 1, 1 - par, 0, 1)
                gates(s + 1, 1 - par, 6)
                gates(s + 1, 1 - par, 7)
                mix(s + 1, 1 - par, 0)
                decayed(s + 1, 0)
                x_dt(s + 1, 1 - par, 1, 0)
                head(s + 1, 1 - par)
            dve.wait_ge(s_xres, 1 + s * 16 + 16)
            x1_tile(s, 0)
            if proj:
                x_dt(s + 1, 1 - par, 1, 1)
            if norm:
                xt_lo(s + 2, 0)
            if proj:
                decayed(s + 1, 1)
            if norm:
                xt_lo(s + 2, 1)
            x1_tile(s, 1)

        def head(s, par):
            add_skip(s, par, 0)
            mix(s, par, 1)

        ln_stats(0)
        rsqrt(0)
        for t in range(NT):
            dve.tensor_scalar(xn[:, t, :], xin[:, t, :], mv[:, t, 0:1], rs[:, NT + t:NT + t + 1],
                              ALU.subtract, ALU.mult).then_inc(s_xn, 1)
        for t in range(NT):
            xt_lo(0, t)
        ln_stats(1)
        for i, k in enumerate(SEQ + [None]):
            if i < NPROJ and k < NCONV:
                convs(0, [k])
            if i and SEQ[i - 1] < NCONV:
                silu(0, 0, SEQ[i - 1])
            elif i:
                gates(0, 0, SEQ[i - 1] - NCONV)
            if i == 0:
                rsqrt(1)
            if i == 2:
                one_plus(0)
            if i == 5:
                dt_parts(0, 0)
        dt_b_g(0, 0)
        x_dt(0, 0, 0, 0)
        mix(0, 0, 0)
        x_dt(0, 0, 0, 1)
        x_dt(0, 0, 1, 0)
        decayed(0, 0)
        head(0, 0)
        x_dt(0, 0, 1, 1)
        xt_lo(1, 0)
        decayed(0, 1)
        xt_lo(1, 1)
        steps(dve, step)


WORDS_LANES = 128
GL = 8
GR = GT - GL
NIB = 0x1C1C1C1C
SGN = -2139062144


def ffn(nc, ctx, d, early):
    def sb(name, shape, dt=FP32):
        return ctx.enter_context(nc.sbuf_tensor(name, shape, dt))

    def sem(name):
        return ctx.enter_context(nc.semaphore(name))

    def bank(name):
        return ctx.enter_context(nc.psum_tensor(name, [P, 512], FP32))

    wg_h = sb("wg_h", [P, KD, GT * GC], BF16)
    wg_l = sb("wg_l", [P, KD, GT * GC], BF16)
    wd_h = sb("wd_h", [P, GT, D_MODEL], BF16)
    wd_l = sb("wd_l", [P, GT, D_MODEL], BF16)
    word = sb("word", [P, (GT - 2) * GC], I32)
    scale = sb("scale", [P, (GT - 2) * GC], FP16)
    dword = sb("dword", [P, 2 + GR, D_MODEL], I32)
    dscale = sb("dscale", [P, 2 + GR, D_MODEL], FP16)
    shift = sb("shift", [P, 1], I32)
    bits = sb("bits", [P, 3, D_MODEL], I32)
    wf = sb("wf", [P, 4, 4 * GC])
    wfd = [wf[:, 2 * q:2 * q + 2].rearrange("p a b -> p (a b)") for q in range(2)]
    scales_flat, ident, xl = early["scales_flat"], early["ident"], early["x"]
    sjunk = sb("sjunk", [P, P_SC], FP16)
    smax = sb("smax", [P, 2])
    pow2 = sb("pow2", [P, 1], I32)
    rp2 = sb("rp2", [P, 1])
    hs = sb("hs", [P, 1])
    hsx = sb("hsx", [P, 1])
    eps = sb("f_eps", [P, 2])
    xr = sb("f_xr", [P, NTF, D_MODEL])
    stats = sb("f_stats", [P, NTF, 6])
    mv = sb("f_mv", [P, NTF, 2])
    std = sb("f_std", [P, NTF])
    rstd = sb("f_rstd", [P, NTF])
    xn = sb("f_xn", [P, NTF, D_MODEL])
    xt_h = sb("xt_h", [P, KD, TF], FP16)
    xt_l = sb("xt_l", [P, KD, TF], FP16)
    sg = sb("f_sg", [P, 2, TF])
    hf = sb("f_h", [P, 2, TF])
    h_h = sb("h_h", [P, GT, TF], FP16)
    h_l = sb("h_l", [P, GT, TF], FP16)
    junk = sb("f_junk", [P, D_MODEL])
    ssq = sb("f_ssq", [P, 3, NTF])
    o = sb("f_o", [P, NTF, D_MODEL])
    pT = bank("f_pT")
    pG = [bank("f_pG0"), bank("f_pG1")]
    pU = [bank("f_pU0"), bank("f_pU1")]
    pD = [bank("f_pD0"), bank("f_pD1"), pG[0], pU[0]]

    s_wd2 = sem("gate_up_rest_loaded")
    s_dnw = sem("down_words_loaded")
    s_eps = sem("f_eps_ready")
    s_smax = sem("f_scale_max")
    s_bit = sem("bits_ready")
    s_wf = sem("w_float_ready")
    s_wh = sem("w_hi_ready")
    s_wl = sem("w_lo_ready")
    s_x = sem("f_x_loaded")
    s_xr = sem("f_residual_loaded")
    s_st = sem("f_stats_ready")
    s_mv = sem("f_mv_ready")
    s_std = sem("f_std_ready")
    s_rstd = sem("f_rstd_ready")
    s_xn = sem("f_xn_ready")
    s_tp = sem("f_xt_in_psum")
    s_th = sem("f_xt_hi_ready")
    s_tl = sem("f_xt_lo_ready")
    s_g = sem("f_gate_in_psum")
    s_u = sem("f_up_in_psum")
    s_sg = sem("f_silu_ready")
    s_h = sem("f_h_ready")
    s_hh = sem("f_h_hi_ready")
    s_hl = sem("f_h_lo_ready")
    s_d = sem("f_down_in_psum")
    s_q = sem("f_ssq_ready")
    s_r = sem("f_rms_ready")
    s_rr = sem("f_rrms_ready")
    s_o = sem("f_out_ready")
    s_out = sem("f_out_stored")
    for s in (s_x, s_xr, s_st, s_mv, s_std, s_rstd, s_xn, s_tp, s_th, s_tl, s_g, s_u, s_sg, s_h, s_hh, s_hl, s_d,
              s_q, s_r, s_rr, s_o, s_out):
        nc.sync.sem_inc(s, 1)
    block = ctx.enter_context(nc.Block())

    def blocks(eng, step):
        step(0, True, True)
        with eng.Fori(1, NBF - 1) as i:
            step(i, False, True)
        step(NBF - 1, False, False)

    @block.sync
    def _(sp):
        def load_x(i):
            sp.dma_start(xl[:], d["x1"][bass.ds(i * TF, TF), :].rearrange("(t p) d -> p t d", p=P)).then_inc(s_x, 16)

        first = 2 * GC
        for half in range(2):
            sp.dma_start(word[64 * half:64 * half + 64, :], d["gu_packed"][:, first:]).then_inc(s_wd2, 16)
        sp.dma_start(scale[:], d["gu_scale"][:, first:]).then_inc(s_wd2, 16)
        for half in range(2):
            sp.dma_start(dword[64 * half:64 * half + 64, 0:2, :],
                         d["dn_packed"][0:WORDS_LANES].rearrange("(q w) o -> w q o", q=2)).then_inc(s_dnw, 16)
        for n in range(8):
            sp.dma_start(dword[16 * n:16 * n + 16, 2:, :],
                         d["dn_packed"][WORDS_LANES:].rearrange("(g w) o -> w g o", g=GR)).then_inc(s_dnw, 16)
        sp.dma_start(dscale[:], d["dn_scale"]).then_inc(s_dnw, 16)
        sp.dma_start(shift[:], d["shift"]).then_inc(s_dnw, 16)

        def step(i, first, more):
            sp.wait_ge(s_o, 1 + i * NTF)
            sp.dma_start(xr[:], d["x1"][bass.ds(i * TF, TF), :].rearrange("(t p) d -> p t d", p=P)).then_inc(s_xr, 16)
            if more:
                sp.wait_ge(s_xn, 1 + (i + 1) * NTF)
                load_x(i + 1)
            sp.wait_ge(s_o, 1 + (i + 1) * NTF)
            sp.dma_start(d["out"][bass.ds(i * TF, TF), :].rearrange("(t p) d -> p t d", p=P), o[:]).then_inc(s_out, 16)
        blocks(sp, step)
        sp.wait_ge(s_out, 1 + 16 * NBF)

    @block.tensor
    def _(pe):
        def transposes(i, t):
            pe.wait_ge(s_xn, 1 + i * NTF + t + 1)
            pe.wait_ge(s_tl, 1 + i * NTF + t)
            for k in range(KD):
                last = nc.tensor.transpose(pT[:, k * P:(k + 1) * P],
                                           xn[:, t, k * P:(k + 1) * P], ident[:])
            last.then_inc(s_tp, 1)

        def product(out, parts, start, stop):
            for n, (a, b) in enumerate(parts):
                last = nc.tensor.matmul(out, a, b, start=start and n == 0, stop=stop and n == len(parts) - 1)
            return last

        def step(i, first, more):
            pe.wait_ge(s_tl, 1 + i * NTF + NTF)
            for g in range(GT):
                if first:
                    pe.wait_ge(s_wl, g + 1)
                for gu, (ps, done, free) in enumerate(((pG, s_g, s_sg), (pU, s_u, s_h))):
                    pe.wait_ge(free, 1 + i * GT + max(g - 1, 0))
                    if g == 1:
                        pe.wait_ge(s_o, 1 + i * NTF)
                    c = slice(g * GC + gu * P, g * GC + gu * P + P)
                    for k in range(KD):
                        last = product(ps[(g + 1) % 2][:, :], ((wg_h[:, k, c], xt_h[:, k, :]),
                                                                (wg_h[:, k, c], xt_l[:, k, :]),
                                                                (wg_l[:, k, c], xt_h[:, k, :])), k == 0, k == KD - 1)
                    last.then_inc(done, 1)
            for t in range(NTF):
                if more:
                    transposes(i + 1, t)
                ts = slice(t * P, (t + 1) * P)
                pe.wait_ge(s_o, 1 + i * NTF)
                if t >= 2:
                    pe.wait_ge(s_h, 1 + i * GT + GT - 1)
                for g in range(GT):
                    if first and t == 0:
                        pe.wait_ge(s_wl, GT + (g // 4 if g < GL else 2 + g - GL) + 1)
                    if t == 0 and g in (0, GT - 2, GT - 1):
                        pe.wait_ge(s_hl, 1 + i * GT + (GT - 2 if g == 0 else g + 1))
                    last = product(pD[t][:, :], ((h_h[:, g, ts], wd_h[:, g, :]), (h_l[:, g, ts], wd_h[:, g, :]),
                                                 (h_h[:, g, ts], wd_l[:, g, :])), g == 0, g == GT - 1)
                last.then_inc(s_d, 1)

        for t in range(NTF):
            transposes(0, t)
        blocks(pe, step)

    @block.scalar
    def _(act):
        def ln_std(i):
            act.wait_ge(s_mv, 1 + i + 1)
            act.activation(std[:], mv[:, :, 1], ACT.Sqrt, scale=X_SCALE ** -2, bias=eps[:, 0:1]).then_inc(s_std, 1)

        def xt_hi(i, t):
            act.wait_ge(s_tp, 1 + i * NTF + t + 1)
            act.activation(xt_h[:, :, t * P:(t + 1) * P], pT[:, :].rearrange("p (k n) -> p k n", k=KD),
                           ACT.Copy).then_inc(s_th, 1)

        def w_hi(n):
            act.wait_ge(s_wf, n + 1)
            if n < GT:
                act.activation(wg_h[:, :, n * GC:(n + 1) * GC], wf[:, n % 4, :].rearrange("p (k c) -> p k c", k=KD),
                               ACT.Copy).then_inc(s_wh, 1)
            elif n < GT + 2:
                q = n - GT
                act.activation(wd_h[:, 4 * q:4 * q + 4, :].rearrange("p g c -> p (g c)"), wfd[q],
                               ACT.Copy).then_inc(s_wh, 1)
            else:
                g = n - GT - 2 + GL
                act.activation(wd_h[:, g, :], wf[:, n - GT - 2, 0:D_MODEL], ACT.Copy).then_inc(s_wh, 1)

        def step(i, first, more):
            for g in range(GT):
                act.wait_ge(s_g, 1 + i * GT + g + 1)
                act.wait_ge(s_h, 1 + i * GT + max(g - 1, 0))
                act.activation(sg[:, g % 2, :], pG[(g + 1) % 2][:, :], ACT.Silu, scale=1.0 / X_SCALE).then_inc(s_sg, 1)
                if g >= 1:
                    h_hi(i, g - 1)
                if first:
                    for n in UNPACK_AT[g]:
                        w_hi(n)
                if g == LN_AT and more:
                    ln_std(i + 1)
            h_hi(i, GT - 1)
            for t in range(NTF):
                if more:
                    xt_hi(i + 1, t)
                act.wait_ge(s_d, 1 + i * NTF + t + 1)
                act.wait_ge(s_q, 1 + i * NTF + t)
                act.activation(junk[:], pD[t][:, :], ACT.Square, accum_out=ssq[:, 0, t:t + 1]).then_inc(s_q, 1)
            act.wait_ge(s_q, 1 + i * NTF + NTF)
            act.activation(ssq[:, 1, :], ssq[:, 0, :], ACT.Sqrt, scale=1.0 / D_MODEL, bias=eps[:, 1:2]).then_inc(s_r, 1)

        def h_hi(i, g):
            act.wait_ge(s_h, 1 + i * GT + g + 1)
            if g == 0:
                act.wait_ge(s_d, 1 + i * NTF)
            act.activation(h_h[:, g, :], hf[:, g % 2, :], ACT.Copy).then_inc(s_hh, 1)

        act.wait_ge(s_eps, 3)
        ln_std(0)
        xt_hi(0, 0)
        w_hi(0)
        xt_hi(0, 1)
        xt_hi(0, 2)
        w_hi(1)
        xt_hi(0, 3)
        w_hi(2)
        blocks(act, step)

    @block.gpsimd
    def _(pool):
        pool.wait_ge(s_smax, 1)
        pool.partition_all_reduce(smax[:, 1:2], smax[:, 0:1], P, bass.bass_isa.ReduceOp.max).then_inc(s_smax, 1)
        pool.wait_ge(s_smax, 2)
        for units in [[0, 1, 2]] + UNPACK_AT:
            for n in units:
                if n:
                    pool.wait_ge(s_wl, n)
                pool.wait_ge(s_wh, n + 1)
                if n < GT:
                    c = slice(n * GC, (n + 1) * GC)
                    pool.tensor_tensor(wg_l[:, :, c], wf[:, n % 4, :].rearrange("p (k c) -> p k c", k=KD),
                                       wg_h[:, :, c], ALU.subtract).then_inc(s_wl, 1)
                elif n < GT + 2:
                    q = n - GT
                    pool.tensor_tensor(wd_l[:, 4 * q:4 * q + 4, :].rearrange("p g c -> p (g c)"), wfd[q],
                                       wd_h[:, 4 * q:4 * q + 4, :].rearrange("p g c -> p (g c)"),
                                       ALU.subtract).then_inc(s_wl, 1)
                else:
                    gg = n - GT - 2 + GL
                    pool.tensor_tensor(wd_l[:, gg, :], wf[:, n - GT - 2, 0:D_MODEL], wd_h[:, gg, :],
                                       ALU.subtract).then_inc(s_wl, 1)

    @block.vector
    def _(dve):
        bit = [0]

        def link(ins):
            bit[0] += 1
            ins.then_inc(s_bit, 1)
            dve.wait_ge(s_bit, bit[0])

        def lanes(src, dst, tmp):
            dve.tensor_scalar(dst[0:64], src[0:64], 2, NIB, ALU.logical_shift_left, ALU.bitwise_and)
            dve.tensor_scalar(dst[64:P], src[64:P], 2, NIB, ALU.logical_shift_right, ALU.bitwise_and)
            dve.tensor_scalar(tmp[0:64], src[0:64], 4, SGN, ALU.logical_shift_left, ALU.bitwise_and)
            link(dve.tensor_scalar(tmp[64:P], src[64:P], SGN, 0, ALU.bitwise_and, ALU.logical_shift_left))
            link(dve.tensor_tensor(dst, dst, tmp, ALU.bitwise_or))

        def unpack(n):
            if n < GT:
                if n == 2:
                    dve.wait_ge(s_wd2, 48)
                words, scales = (early["word"], early["scale"]) if n < 2 else (word, scale)
                c = slice(n % 2 * GC, (n % 2 + 1) * GC) if n < 2 else slice((n - 2) * GC, (n - 1) * GC)
                lanes(words[:, c], bits[:, 0, 0:GC], bits[:, 1, 0:GC])
                val = bits[:, 0, 0:GC].bitcast(FP8).rearrange("p (o b) -> p o b", b=4)
                if n >= 4:
                    dve.wait_ge(s_wl, n - 3)
                for b in range(KD):
                    last = dve.scalar_tensor_tensor(wf[:, n % 4, b * GC:(b + 1) * GC], val[:, :, b], 64.0, scales[:, c],
                                                    ALU.mult, ALU.mult)
            elif n < GT + 2:
                q = n - GT
                if q == 0:
                    dve.wait_ge(s_dnw, 16 * 12)
                lanes(dword[:, q, :], bits[:, 0, :], bits[:, 1, :])
                val = bits[:, 0, :].bitcast(FP8).rearrange("p (o b) -> p o b", b=4)
                dve.wait_ge(s_wl, n - 1)
                for b in range(4):
                    last = dve.scalar_tensor_tensor(wfd[q][:, b * D_MODEL:(b + 1) * D_MODEL], val[:, :, b], 64.0,
                                                    dscale[:, q, :], ALU.mult, ALU.mult)
            else:
                q = n - GT
                dve.wait_ge(s_wl, GT + 1 + (q - 2) // 2)
                link(dve.tensor_tensor(bits[:, 2, :], dword[:, q, :], shift[:].to_broadcast([P, D_MODEL]),
                                       ALU.logical_shift_right))
                dve.tensor_scalar(bits[:, 1, :], bits[:, 2, :], 8, 4, ALU.bitwise_and, ALU.logical_shift_left)
                link(dve.tensor_scalar(bits[:, 0, :], bits[:, 2, :], 7, 2, ALU.bitwise_and, ALU.logical_shift_left))
                link(dve.tensor_tensor(bits[:, 0, :], bits[:, 0, :], bits[:, 1, :], ALU.bitwise_or))
                val = bits[:, 0, :].bitcast(FP8).rearrange("p (o b) -> p o b", b=4)
                last = dve.scalar_tensor_tensor(wf[:, q - 2, 0:D_MODEL], val[:, :, 0], 64.0, dscale[:, q, :],
                                                ALU.mult, ALU.mult)
            last.then_inc(s_wf, 1)
            dve.wait_ge(s_wf, n + 1)

        def layernorm(i):
            dve.wait_ge(s_x, 1 + i * 16)
            for t in range(NTF):
                last = dve.bn_stats(stats[:, t, :], xl[:, t, :])
            last.then_inc(s_st, 1)
            dve.wait_ge(s_st, 1 + i + 1)
            dve.tensor_copy(rstd[:, 0:1], stats[:, 0, 0:1])
            for t in range(NTF):
                last = dve.bn_aggr(mv[:, t, :], stats[:, t, :])
            last.then_inc(s_mv, 1)

        def normalise(i):
            dve.wait_ge(s_std, 1 + i + 1)
            dve.reciprocal(rstd[:], std[:]).then_inc(s_rstd, 1)
            dve.wait_ge(s_rstd, 1 + i + 1)
            for t in range(NTF):
                dve.wait_ge(s_tp, 1 + i * NTF)
                dve.tensor_scalar(xn[:, t, :].rearrange("p (b n w) -> p b n w", b=4, n=2),
                                  xl[:, t, :].rearrange("p (w b n) -> p b n w", b=4, n=2),
                                  mv[:, t, 0:1], rstd[:, t:t + 1], ALU.subtract, ALU.mult).then_inc(s_xn, 1)

        def xt_lo(i, t):
            dve.wait_ge(s_th, 1 + i * NTF + t + 1)
            dve.tensor_tensor(xt_l[:, :, t * P:(t + 1) * P], pT[:, :].rearrange("p (k n) -> p k n", k=KD),
                              xt_h[:, :, t * P:(t + 1) * P], ALU.subtract).then_inc(s_tl, 1)

        def h_lo(i, g):
            dve.wait_ge(s_hh, 1 + i * GT + g + 1)
            dve.tensor_tensor(h_l[:, g, :], hf[:, g % 2, :], h_h[:, g, :], ALU.subtract).then_inc(s_hl, 1)

        def step(i, first, more):
            for g in range(GT):
                dve.wait_ge(s_u, 1 + i * GT + g + 1)
                dve.wait_ge(s_sg, 1 + i * GT + g + 1)
                if g >= 2:
                    dve.wait_ge(s_hl, 1 + i * GT + g - 1)
                dve.scalar_tensor_tensor(hf[:, g % 2, :], pU[(g + 1) % 2][:, :], hsx[:], sg[:, g % 2, :], ALU.mult,
                                         ALU.mult).then_inc(s_h, 1)
                if g >= 1:
                    h_lo(i, g - 1)
                if first:
                    for n in UNPACK_AT[g]:
                        unpack(n)
                if g == LN_AT - 1 and more:
                    layernorm(i + 1)
                if g == LN_AT + 1 and more:
                    normalise(i + 1)
            h_lo(i, GT - 1)
            if more:
                for t in range(NTF):
                    xt_lo(i + 1, t)
            dve.wait_ge(s_r, 1 + i + 1)
            dve.reciprocal(ssq[:, 2, :], ssq[:, 1, :]).then_inc(s_rr, 1)
            dve.wait_ge(s_rr, 1 + i + 1)
            dve.wait_ge(s_out, 1 + i * 16)
            dve.wait_ge(s_xr, 1 + i * 16 + 16)
            for t in range(NTF):
                dve.scalar_tensor_tensor(o[:, t, :], pD[t][:, :], ssq[:, 2, t:t + 1], xr[:, t, :], ALU.mult,
                                         ALU.add).then_inc(s_o, 1)

        link(dve.scalar_tensor_tensor(sjunk[:], scales_flat[:], -1.0, scales_flat[:], ALU.mult, ALU.max))
        dve.reduce_max(smax[:, 0:1], sjunk[:], mybir.AxisListType.X).then_inc(s_smax, 1)
        dve.memset(eps[:, 0:1], LN_EPS / X_SCALE ** 2).then_inc(s_eps, 1)
        layernorm(0)
        dve.wait_ge(s_smax, 2)
        link(dve.tensor_scalar(smax[:, 0:1], smax[:, 1:2], 2.0 ** -24, None, ALU.max))
        link(dve.tensor_scalar(pow2[:], smax[:, 0:1].bitcast(I32), EXPONENT, 0, ALU.bitwise_and, ALU.logical_shift_left))
        link(dve.reciprocal(rp2[:], pow2[:].bitcast(FP32)))
        link(dve.tensor_scalar(hs[:], rp2[:], rp2[:], 2.0 ** -11, ALU.mult, ALU.mult))
        dve.tensor_scalar(hsx[:], hs[:], 1.0 / X_SCALE, None, ALU.mult).then_inc(s_eps, 1)
        dve.tensor_scalar(eps[:, 1:2], hs[:], hs[:], FFN_EPS, ALU.mult, ALU.mult).then_inc(s_eps, 1)
        normalise(0)
        unpack(0)
        xt_lo(0, 0)
        xt_lo(0, 1)
        unpack(1)
        xt_lo(0, 2)
        xt_lo(0, 3)
        unpack(2)
        dve.wait_ge(s_eps, 3)
        blocks(dve, step)


LN_AT = 7
UNPACK_AT = [[3], [4], [5], [6, 7], [8], [9, 10], [GT], [GT + 1], [GT + 2, GT + 3], [GT + 4], []]


def build(nc, d):
    with ExitStack() as kept, ExitStack() as outer:
        early = {name: kept.enter_context(nc.sbuf_tensor(f"early_{name}", shape, dt)) for name, shape, dt in (
            ("ident", [P, P], FP32), ("scales_flat", [P, P_SC], FP16), ("word", [P, 2 * GC], I32),
            ("scale", [P, 2 * GC], FP16), ("x", [P, NTF, D_MODEL], FP32))}
        with ExitStack() as ctx:
            w = weights(nc, ctx, outer, d)
        with ExitStack() as ctx:
            mixer(nc, ctx, d, w, early)
        outer.close()
        with ExitStack() as ctx:
            ffn(nc, ctx, d, early)


def kernel(L0_attn_u, L0_attn_W_in, L0_attn_conv_w, L0_attn_conv_b, L0_attn_dt_bias, L0_attn_A_log, L0_attn_D,
           L0_attn_norm_w, L0_attn_W_out, L0_ffn_gate_up_packed, L0_ffn_gate_up_scales, L0_ffn_down_packed,
           L0_ffn_down_scales):
    import numpy as np
    import concourse.bacc as bacc
    from concourse.bass_utils import run_bass_kernel_spmd as run

    arr = np.asarray
    w_in = arr(L0_attn_W_in).T
    z, x, bm, cm, dt = np.split(w_in, np.cumsum([D_INNER, D_INNER, D_STATE, D_STATE]), axis=1)
    w_in = np.concatenate([bm, cm] + [dt] * 4 + [bm, x, z], axis=1)

    def conv_rows(a):
        x, bm, cm = np.split(a, np.cumsum([D_INNER, D_STATE]), axis=0)
        return np.concatenate([bm, cm, bm, bm, x], axis=0)

    conv_w = conv_rows(arr(L0_attn_conv_w)).reshape(NCONV, P, 4).transpose(1, 0, 2)
    conv_b = conv_rows(arr(L0_attn_conv_b)).reshape(NCONV, P).T
    heads = lambda a, copies: np.concatenate([arr(a)] * copies).reshape(-1, 1)
    d_skip = np.repeat(arr(L0_attn_D), HEADDIM).reshape(JT, P).T
    norm_w = arr(L0_attn_norm_w).reshape(JT, P).T

    row = np.arange(P)
    order = np.concatenate([8 * (64 * (g // 4) + row % 64) + 2 * (g % 4) + row // 64 if g < GL else
                            P * g + 8 * (row % 16) + row // 16 for g in range(GT)])

    def ffn_cols(a):
        a = a.reshape(a.shape[0], 2, I_FFN)[:, :, order].reshape(a.shape[0], 2, GT, P)
        return a.transpose(0, 2, 1, 3).reshape(a.shape[0], 2 * I_FFN)

    gu_packed = ffn_cols(arr(L0_ffn_gate_up_packed).T)
    gu_scale = ffn_cols(arr(L0_ffn_gate_up_scales))
    gu_scale = np.concatenate([np.repeat(gu_scale, 16, axis=0)] * 2, axis=0)
    dn_packed = arr(L0_ffn_down_packed).T
    dn = arr(L0_ffn_down_scales)
    dn_scale = np.stack([np.concatenate([np.repeat(dn[4 * q:4 * q + 4], 16, axis=0)] * 2) for q in range(2)] +
                        [np.repeat(dn[g:g + 1], P, axis=0) for g in range(GL, GT)], axis=1)

    delta = np.zeros((32, HEADS, CHUNK), np.float32)
    delta[np.arange(32), np.arange(32) % HEADS] = 1.0
    keep = np.ones((HALF, T), np.float32)
    keep[:, ::CHUNK] = 0.0
    part = np.zeros((HALF, 2), np.float32)
    part[np.arange(HALF), np.arange(HALF) // HEADS % 2] = 1.0
    mask = np.full((CHUNK, CHUNK), -1e30, np.float32)
    mask = np.repeat(np.tril(mask, -1)[:, None, :], HEADS, axis=1)
    inputs = {
        "u": arr(L0_attn_u).reshape(L, D_MODEL), "w_in": w_in, "w_out": arr(L0_attn_W_out).T, "conv_w": conv_w,
        "conv_b": conv_b, "dt_bias": heads(L0_attn_dt_bias, 4), "A_log": heads(L0_attn_A_log, 8), "D": d_skip,
        "norm_w": norm_w, "gu_packed": gu_packed, "gu_scale": gu_scale, "dn_packed": dn_packed,
        "dn_scale": dn_scale, "gu_scale_flat": arr(L0_ffn_gate_up_scales).reshape(P, P_SC),
        "ident": np.eye(P, dtype=np.float32),
        "mask": mask, "delta": delta, "keep": keep, "part": part,
        "shift": (4 * (np.arange(P) // 16)).astype(np.int32).reshape(P, 1),
    }
    inputs = {k: np.ascontiguousarray(v) for k, v in inputs.items()}
    nc = bacc.Bacc("TRN2", target_bir_lowering=False, num_devices=1)
    d = {k: nc.dram_tensor(f"in_{k}", v.shape, mybir.dt.from_np(v.dtype), kind="ExternalInput").ap()
         for k, v in inputs.items()}
    d["x1"] = nc.dram_tensor("x1_scratch", [L, D_MODEL], FP32, kind="Internal").ap()
    d["out"] = nc.dram_tensor("out_0", [L, D_MODEL], FP32, kind="ExternalOutput").ap()
    build(nc, d)
    r = run(nc, [{f"in_{k}": v for k, v in inputs.items()}], core_ids=[0])
    return r.results[0]["out_0"].reshape(1, L, D_MODEL)
```
